# Optimizing a Trainium2 kernel written in Bass

```python
import numpy as np
import jax
import jax.numpy as jnp

def _softmax(x, axis=-1):
    return jax.nn.softmax(x, axis=axis)

def _gelu(x):
    return jax.nn.gelu(x, approximate=True)

def _silu(x):
    return jax.nn.silu(x)

def _sigmoid(x):
    return jax.nn.sigmoid(x)

def _layernorm(x, axis=-1, eps=1e-05):
    m = jnp.mean(x, axis=axis, keepdims=True)
    v = jnp.var(x, axis=axis, keepdims=True)
    return (x - m) / jnp.sqrt(v + eps)

def _scatter_add(tgt, idx, src, axis=0):
    return tgt.at[idx].add(src)

def _segment_sum(src, seg, n):
    return jax.ops.segment_sum(src, seg, n)
kernel_name = 'mk_xattn_seq_d2_seqx_r8_12c2cf'

def setup_inputs(seed: int=0):
    np.random.seed(seed)
    _w = jnp.asarray

    def _rec_inputs():
        import jax
        import jax.numpy as jnp
        _rk = jax.random.key(seed)
        x = -0.0005207 + 1.001 * jax.random.normal(jax.random.fold_in(_rk, 1), (8, 256, 256), jnp.float32)
        _lenS = 256 - jax.random.randint(jax.random.fold_in(_rk, 7), (8,), 0, max(1, 256 // 4) + 1, jnp.int32)
        _lenS2 = 64 - jax.random.randint(jax.random.fold_in(_rk, 8), (8,), 0, max(1, 64 // 4) + 1, jnp.int32)
        _ctx_2048P = jax.random.normal(jax.random.fold_in(_rk, 11), (8, 16, 256), jnp.float32)
        _ctx_2048c = jax.random.dirichlet(jax.random.fold_in(_rk, 511), 0.3 * jnp.ones((16,), jnp.float32), (8, 64))
        _ctx_2048t = jnp.einsum('bsk,bkd->bsd', _ctx_2048c, _ctx_2048P)
        _ctx_2048t = _ctx_2048t * jax.lax.rsqrt(jnp.mean(jnp.square(_ctx_2048t)) + 1e-12) * 0.953939
        ctx_2048 = 2.81802e-05 + 1.00001 * (_ctx_2048t + 0.3 * jax.random.normal(jax.random.fold_in(_rk, 611), (8, 64, 256), jnp.float32))
        _validS = jnp.arange(256)[None, :] < _lenS[:, None]
        _validS2 = jnp.arange(64)[None, :] < _lenS2[:, None]
        _causal = jnp.tril(jnp.ones((256, 256), dtype=bool))
        mask_BxS2_ik0 = jnp.where(jnp.broadcast_to(_validS2[:, :], (8, 64)), 0, 1).astype(jnp.int32)
        return (x, ctx_2048, mask_BxS2_ik0)
    x, ctx_2048, mask_BxS2_ik0 = _rec_inputs()

    def _L0_xattn_setup():
        import jax, jax.numpy as jnp
        import numpy as np
        B, Q, S1, S2 = (4, 32, 256, 256)
        D, H, K, F = (256, 16, 128, 1024)
        LN_EPS = 1e-05

        def _layer_norm(x, scale, offset):
            mu = jnp.mean(x, axis=-1, keepdims=True)
            var = jnp.var(x, axis=-1, keepdims=True)
            return (x - mu) * jax.lax.rsqrt(var + LN_EPS) * scale + offset

        def _cross_attention(q_in, kv_in, wq, bq, wk, bk, wv, bv, wo, bo, bias_k, bias_v):
            b, q_len, _ = q_in.shape
            t = kv_in.shape[1]
            qh = (q_in @ wq + bq).reshape(b, q_len, H, K)
            kh = (kv_in @ wk + bk).reshape(b, t, H, K)
            vh = (kv_in @ wv + bv).reshape(b, t, H, K)
            kh = jnp.concatenate([kh, jnp.broadcast_to(bias_k, (b, 1, H, K))], axis=1)
            vh = jnp.concatenate([vh, jnp.broadcast_to(bias_v, (b, 1, H, K))], axis=1)
            scale = jnp.sqrt(jnp.asarray(K, q_in.dtype))
            logits = jnp.einsum('bqhk,bthk->bhqt', qh, kh) / scale
            weights = jax.nn.softmax(logits, axis=-1)
            ctx = jnp.einsum('bhqt,bthk->bqhk', weights, vh).reshape(b, q_len, H * K)
            return ctx @ wo + bo

        def _forward(x, xf_1, xf_2, ln1_scale, ln1_offset, wq1, bq1, wk1, bk1, wv1, bv1, wo1, bo1, bias_k1, bias_v1, ln2_scale, ln2_offset, wq2, bq2, wk2, bk2, wv2, bv2, wo2, bo2, bias_k2, bias_v2, ln_mlp_scale, ln_mlp_offset, w_fc1, b_fc1, w_fc2, b_fc2):
            res = x
            h = _layer_norm(x, ln1_scale, ln1_offset)
            x = res + _cross_attention(h, xf_1, wq1, bq1, wk1, bk1, wv1, bv1, wo1, bo1, bias_k1, bias_v1)
            res = x
            h = _layer_norm(x, ln2_scale, ln2_offset)
            x = res + _cross_attention(h, xf_2, wq2, bq2, wk2, bk2, wv2, bv2, wo2, bo2, bias_k2, bias_v2)
            h = _layer_norm(x, ln_mlp_scale, ln_mlp_offset)
            h = jax.nn.gelu(h @ w_fc1 + b_fc1, approximate=False) @ w_fc2 + b_fc2
            return x + h
        key = jax.random.key(seed)
        ks = iter(jax.random.split(key, 64))

        def rn(shape, s=0.02):
            return jax.random.normal(next(ks), shape, jnp.float32) * s
        inp = {'x': rn((B, Q, D), 1.0), 'xf_1': rn((B, S1, D), 1.0), 'xf_2': rn((B, S2, D), 1.0)}
        for i in (1, 2):
            inp[f'ln{i}_scale'] = jnp.ones((D,), jnp.float32)
            inp[f'ln{i}_offset'] = jnp.zeros((D,), jnp.float32)
            inp[f'wq{i}'] = rn((D, H * K))
            inp[f'bq{i}'] = jnp.zeros((H * K,), jnp.float32)
            inp[f'wk{i}'] = rn((D, H * K))
            inp[f'bk{i}'] = jnp.zeros((H * K,), jnp.float32)
            inp[f'wv{i}'] = rn((D, H * K))
            inp[f'bv{i}'] = jnp.zeros((H * K,), jnp.float32)
            inp[f'wo{i}'] = rn((H * K, D))
            inp[f'bo{i}'] = jnp.zeros((D,), jnp.float32)
            inp[f'bias_k{i}'] = rn((1, 1, H, K))
            inp[f'bias_v{i}'] = rn((1, 1, H, K))
        inp['ln_mlp_scale'] = jnp.ones((D,), jnp.float32)
        inp['ln_mlp_offset'] = jnp.zeros((D,), jnp.float32)
        inp['w_fc1'] = rn((D, F))
        inp['b_fc1'] = jnp.zeros((F,), jnp.float32)
        inp['w_fc2'] = rn((F, D))
        inp['b_fc2'] = jnp.zeros((D,), jnp.float32)
        return inp
    _L0_xattn_all = _L0_xattn_setup()
    _L0_xattn_in = {k: v for k, v in _L0_xattn_all.items() if k in ('ln1_scale', 'ln1_offset', 'wq1', 'bq1', 'wk1', 'bk1', 'wv1', 'bv1', 'wo1', 'bo1', 'bias_k1', 'bias_v1', 'ln2_scale', 'ln2_offset', 'wq2', 'bq2', 'wk2', 'bk2', 'wv2', 'bv2', 'wo2', 'bo2', 'bias_k2', 'bias_v2', 'ln_mlp_scale', 'ln_mlp_offset', 'w_fc1', 'b_fc1', 'w_fc2', 'b_fc2')}
    del _L0_xattn_all

    def _L1_xattn_setup():
        import jax, jax.numpy as jnp
        import numpy as np
        B, P, K, H, NH = (4, 256, 32, 256, 16)
        DH = H // NH
        EPS = 1e-06

        def rmsnorm(x, w):
            var = jnp.mean(jnp.square(x), axis=-1, keepdims=True)
            return x * jax.lax.rsqrt(var + EPS) * w
        key = jax.random.key(seed)
        ks = jax.random.split(key, 12)
        s = 0.02
        return {'x': jax.random.normal(ks[0], (B, P, H), jnp.float32), 'latents': jax.random.normal(ks[1], (B, K, H), jnp.float32), 'attention_mask': jax.random.randint(ks[2], (B, P), 0, 2, jnp.int32), 'q_w': s * jax.random.normal(ks[3], (H, H), jnp.float32), 'q_b': jnp.zeros((H,), jnp.float32), 'kv_w': s * jax.random.normal(ks[4], (H, 2 * H), jnp.float32), 'kv_b': jnp.zeros((2 * H,), jnp.float32), 'out_w': s * jax.random.normal(ks[5], (H, H), jnp.float32), 'out_b': jnp.zeros((H,), jnp.float32), 'postnorm_w': jnp.ones((H,), jnp.float32), 'mlp_w1': s * jax.random.normal(ks[6], (H, 4 * H), jnp.float32), 'mlp_b1': jnp.zeros((4 * H,), jnp.float32), 'mlp_w2': s * jax.random.normal(ks[7], (4 * H, H), jnp.float32), 'mlp_b2': jnp.zeros((H,), jnp.float32)}
    _L1_xattn_all = _L1_xattn_setup()
    _L1_xattn_in = {k: v for k, v in _L1_xattn_all.items() if k in ('q_w', 'q_b', 'kv_w', 'kv_b', 'out_w', 'out_b', 'postnorm_w', 'mlp_w1', 'mlp_b1', 'mlp_w2', 'mlp_b2')}
    del _L1_xattn_all
    return {'x': x, 'ctx_2048': ctx_2048, 'mask_BxS2_ik0': mask_BxS2_ik0, 'L0_xattn_ln1_scale': _L0_xattn_in['ln1_scale'], 'L0_xattn_ln1_offset': _L0_xattn_in['ln1_offset'], 'L0_xattn_wq1': _L0_xattn_in['wq1'], 'L0_xattn_bq1': _L0_xattn_in['bq1'], 'L0_xattn_wk1': _L0_xattn_in['wk1'], 'L0_xattn_bk1': _L0_xattn_in['bk1'], 'L0_xattn_wv1': _L0_xattn_in['wv1'], 'L0_xattn_bv1': _L0_xattn_in['bv1'], 'L0_xattn_wo1': _L0_xattn_in['wo1'], 'L0_xattn_bo1': _L0_xattn_in['bo1'], 'L0_xattn_bias_k1': _L0_xattn_in['bias_k1'], 'L0_xattn_bias_v1': _L0_xattn_in['bias_v1'], 'L0_xattn_ln2_scale': _L0_xattn_in['ln2_scale'], 'L0_xattn_ln2_offset': _L0_xattn_in['ln2_offset'], 'L0_xattn_wq2': _L0_xattn_in['wq2'], 'L0_xattn_bq2': _L0_xattn_in['bq2'], 'L0_xattn_wk2': _L0_xattn_in['wk2'], 'L0_xattn_bk2': _L0_xattn_in['bk2'], 'L0_xattn_wv2': _L0_xattn_in['wv2'], 'L0_xattn_bv2': _L0_xattn_in['bv2'], 'L0_xattn_wo2': _L0_xattn_in['wo2'], 'L0_xattn_bo2': _L0_xattn_in['bo2'], 'L0_xattn_bias_k2': _L0_xattn_in['bias_k2'], 'L0_xattn_bias_v2': _L0_xattn_in['bias_v2'], 'L0_xattn_ln_mlp_scale': _L0_xattn_in['ln_mlp_scale'], 'L0_xattn_ln_mlp_offset': _L0_xattn_in['ln_mlp_offset'], 'L0_xattn_w_fc1': _L0_xattn_in['w_fc1'], 'L0_xattn_b_fc1': _L0_xattn_in['b_fc1'], 'L0_xattn_w_fc2': _L0_xattn_in['w_fc2'], 'L0_xattn_b_fc2': _L0_xattn_in['b_fc2'], 'L1_xattn_q_w': _L1_xattn_in['q_w'], 'L1_xattn_q_b': _L1_xattn_in['q_b'], 'L1_xattn_kv_w': _L1_xattn_in['kv_w'], 'L1_xattn_kv_b': _L1_xattn_in['kv_b'], 'L1_xattn_out_w': _L1_xattn_in['out_w'], 'L1_xattn_out_b': _L1_xattn_in['out_b'], 'L1_xattn_postnorm_w': _L1_xattn_in['postnorm_w'], 'L1_xattn_mlp_w1': _L1_xattn_in['mlp_w1'], 'L1_xattn_mlp_b1': _L1_xattn_in['mlp_b1'], 'L1_xattn_mlp_w2': _L1_xattn_in['mlp_w2'], 'L1_xattn_mlp_b2': _L1_xattn_in['mlp_b2']}

def reference(x, ctx_2048, mask_BxS2_ik0, L0_xattn_ln1_scale, L0_xattn_ln1_offset, L0_xattn_wq1, L0_xattn_bq1, L0_xattn_wk1, L0_xattn_bk1, L0_xattn_wv1, L0_xattn_bv1, L0_xattn_wo1, L0_xattn_bo1, L0_xattn_bias_k1, L0_xattn_bias_v1, L0_xattn_ln2_scale, L0_xattn_ln2_offset, L0_xattn_wq2, L0_xattn_bq2, L0_xattn_wk2, L0_xattn_bk2, L0_xattn_wv2, L0_xattn_bv2, L0_xattn_wo2, L0_xattn_bo2, L0_xattn_bias_k2, L0_xattn_bias_v2, L0_xattn_ln_mlp_scale, L0_xattn_ln_mlp_offset, L0_xattn_w_fc1, L0_xattn_b_fc1, L0_xattn_w_fc2, L0_xattn_b_fc2, L1_xattn_q_w, L1_xattn_q_b, L1_xattn_kv_w, L1_xattn_kv_b, L1_xattn_out_w, L1_xattn_out_b, L1_xattn_postnorm_w, L1_xattn_mlp_w1, L1_xattn_mlp_b1, L1_xattn_mlp_w2, L1_xattn_mlp_b2):
    import jax
    import jax.numpy as jnp

    def _L0_xattn_ref(x, xf_1, xf_2, ln1_scale, ln1_offset, wq1, bq1, wk1, bk1, wv1, bv1, wo1, bo1, bias_k1, bias_v1, ln2_scale, ln2_offset, wq2, bq2, wk2, bk2, wv2, bv2, wo2, bo2, bias_k2, bias_v2, ln_mlp_scale, ln_mlp_offset, w_fc1, b_fc1, w_fc2, b_fc2):
        import jax, jax.numpy as jnp
        import numpy as np
        B, Q, S1, S2 = (4, 32, 256, 256)
        D, H, K, F = (256, 16, 128, 1024)
        LN_EPS = 1e-05

        def _layer_norm(x, scale, offset):
            mu = jnp.mean(x, axis=-1, keepdims=True)
            var = jnp.var(x, axis=-1, keepdims=True)
            return (x - mu) * jax.lax.rsqrt(var + LN_EPS) * scale + offset

        def _cross_attention(q_in, kv_in, wq, bq, wk, bk, wv, bv, wo, bo, bias_k, bias_v):
            b, q_len, _ = q_in.shape
            t = kv_in.shape[1]
            qh = (q_in @ wq + bq).reshape(b, q_len, H, K)
            kh = (kv_in @ wk + bk).reshape(b, t, H, K)
            vh = (kv_in @ wv + bv).reshape(b, t, H, K)
            kh = jnp.concatenate([kh, jnp.broadcast_to(bias_k, (b, 1, H, K))], axis=1)
            vh = jnp.concatenate([vh, jnp.broadcast_to(bias_v, (b, 1, H, K))], axis=1)
            scale = jnp.sqrt(jnp.asarray(K, q_in.dtype))
            logits = jnp.einsum('bqhk,bthk->bhqt', qh, kh) / scale
            weights = jax.nn.softmax(logits, axis=-1)
            ctx = jnp.einsum('bhqt,bthk->bqhk', weights, vh).reshape(b, q_len, H * K)
            return ctx @ wo + bo

        def _forward(x, xf_1, xf_2, ln1_scale, ln1_offset, wq1, bq1, wk1, bk1, wv1, bv1, wo1, bo1, bias_k1, bias_v1, ln2_scale, ln2_offset, wq2, bq2, wk2, bk2, wv2, bv2, wo2, bo2, bias_k2, bias_v2, ln_mlp_scale, ln_mlp_offset, w_fc1, b_fc1, w_fc2, b_fc2):
            res = x
            h = _layer_norm(x, ln1_scale, ln1_offset)
            x = res + _cross_attention(h, xf_1, wq1, bq1, wk1, bk1, wv1, bv1, wo1, bo1, bias_k1, bias_v1)
            res = x
            h = _layer_norm(x, ln2_scale, ln2_offset)
            x = res + _cross_attention(h, xf_2, wq2, bq2, wk2, bk2, wv2, bv2, wo2, bo2, bias_k2, bias_v2)
            h = _layer_norm(x, ln_mlp_scale, ln_mlp_offset)
            h = jax.nn.gelu(h @ w_fc1 + b_fc1, approximate=False) @ w_fc2 + b_fc2
            return x + h
        return _forward(x, xf_1, xf_2, ln1_scale, ln1_offset, wq1, bq1, wk1, bk1, wv1, bv1, wo1, bo1, bias_k1, bias_v1, ln2_scale, ln2_offset, wq2, bq2, wk2, bk2, wv2, bv2, wo2, bo2, bias_k2, bias_v2, ln_mlp_scale, ln_mlp_offset, w_fc1, b_fc1, w_fc2, b_fc2)

    def _L1_xattn_ref(x, latents, attention_mask, q_w, q_b, kv_w, kv_b, out_w, out_b, postnorm_w, mlp_w1, mlp_b1, mlp_w2, mlp_b2):
        import jax, jax.numpy as jnp
        import numpy as np
        B, P, K, H, NH = (4, 256, 32, 256, 16)
        DH = H // NH
        EPS = 1e-06

        def rmsnorm(x, w):
            var = jnp.mean(jnp.square(x), axis=-1, keepdims=True)
            return x * jax.lax.rsqrt(var + EPS) * w
        b, p, _ = x.shape
        k_len = latents.shape[1]
        residual = latents
        h = jnp.concatenate([x, latents], axis=1)
        q = (latents @ q_w + q_b).reshape(b, k_len, NH, DH)
        kv = (h @ kv_w + kv_b).reshape(b, p + k_len, NH, DH, 2)
        kmat, v = (kv[..., 0], kv[..., 1])
        attn = jnp.einsum('bkhd,bnhd->bhkn', q, kmat) / DH
        full_mask = jnp.concatenate([attention_mask.astype(bool), jnp.ones((b, k_len), bool)], axis=-1)
        attn = jnp.where(full_mask[:, None, None, :], attn, -jnp.inf)
        attn = jax.nn.softmax(attn.astype(jnp.float32), axis=-1).astype(q.dtype)
        attn_out = jnp.einsum('bhkn,bnhd->bkhd', attn, v).reshape(b, k_len, H)
        attn_out = attn_out @ out_w + out_b + residual
        out = rmsnorm(attn_out, postnorm_w)
        out = jax.nn.gelu(out @ mlp_w1 + mlp_b1) @ mlp_w2 + mlp_b2
        return out + residual
    x = _L0_xattn_ref(x, ctx_2048, ctx_2048, L0_xattn_ln1_scale, L0_xattn_ln1_offset, L0_xattn_wq1, L0_xattn_bq1, L0_xattn_wk1, L0_xattn_bk1, L0_xattn_wv1, L0_xattn_bv1, L0_xattn_wo1, L0_xattn_bo1, L0_xattn_bias_k1, L0_xattn_bias_v1, L0_xattn_ln2_scale, L0_xattn_ln2_offset, L0_xattn_wq2, L0_xattn_bq2, L0_xattn_wk2, L0_xattn_bk2, L0_xattn_wv2, L0_xattn_bv2, L0_xattn_wo2, L0_xattn_bo2, L0_xattn_bias_k2, L0_xattn_bias_v2, L0_xattn_ln_mlp_scale, L0_xattn_ln_mlp_offset, L0_xattn_w_fc1, L0_xattn_b_fc1, L0_xattn_w_fc2, L0_xattn_b_fc2)
    x = _L1_xattn_ref(ctx_2048, x, mask_BxS2_ik0, L1_xattn_q_w, L1_xattn_q_b, L1_xattn_kv_w, L1_xattn_kv_b, L1_xattn_out_w, L1_xattn_out_b, L1_xattn_postnorm_w, L1_xattn_mlp_w1, L1_xattn_mlp_b1, L1_xattn_mlp_w2, L1_xattn_mlp_b2)
    return x

_drawn_inputs = setup_inputs


def setup_inputs(seed=0):
    import zlib

    import numpy as np

    out = dict(_drawn_inputs(seed))
    spreads = {'L0_xattn_ln1_scale': (1.0, 0.6),
     'L0_xattn_ln1_offset': (0.0, 0.8),
     'L0_xattn_bq1': (0.0, 0.8),
     'L0_xattn_bk1': (0.0, 2.0),
     'L0_xattn_bv1': (0.0, 0.1),
     'L0_xattn_bo1': (0.0, 0.1),
     'L0_xattn_ln2_scale': (1.0, 0.6),
     'L0_xattn_ln2_offset': (0.0, 0.8),
     'L0_xattn_bq2': (0.0, 0.8),
     'L0_xattn_bk2': (0.0, 2.0),
     'L0_xattn_bv2': (0.0, 0.1),
     'L0_xattn_bo2': (0.0, 0.1),
     'L0_xattn_ln_mlp_scale': (1.0, 0.6),
     'L0_xattn_ln_mlp_offset': (0.0, 0.693),
     'L0_xattn_b_fc1': (0.0, 0.1),
     'L0_xattn_b_fc2': (0.0, 0.1),
     'L1_xattn_q_b': (0.0, 2.0),
     'L1_xattn_kv_b': (0.0, 0.8),
     'L1_xattn_out_b': (0.0, 2.0),
     'L1_xattn_postnorm_w': (1.0, 0.6),
     'L1_xattn_mlp_b1': (0.0, 0.1),
     'L1_xattn_mlp_b2': (0.0, 0.1)}
    factors = {'L0_xattn_wq1': 8.0,
     'L0_xattn_wk1': 8.0,
     'L0_xattn_bias_k1': 64.0,
     'L0_xattn_bias_v1': 64.0,
     'L0_xattn_wq2': 8.0,
     'L0_xattn_wk2': 8.0,
     'L0_xattn_bias_k2': 64.0,
     'L0_xattn_bias_v2': 64.0,
     'L1_xattn_q_w': 8.0,
     'L1_xattn_kv_w': 8.0,
     'L1_xattn_out_w': 8.0}
    for name, (base, spread) in spreads.items():
        noise = np.random.default_rng([zlib.crc32(name.encode()), seed]).standard_normal(out[name].shape)
        drawn = base * np.exp(spread * noise) if base else spread * noise
        out[name] = jnp.asarray(drawn.astype(out[name].dtype))
    for name, factor in factors.items():
        out[name] = (out[name] * factor).astype(out[name].dtype)
    return out
```

```python
from contextlib import ExitStack

import concourse.bass as bass
from concourse import mybir

F32 = mybir.dt.float32
BF16 = mybir.dt.bfloat16
I32 = mybir.dt.int32
ALU = mybir.AluOpType
ACT = mybir.ActivationFunctionType
AX = mybir.AxisListType

P = 128
B, Q, T, D = 8, 256, 64, 256
H, K = 16, 128
DC = D // P
QT = Q // P
NU = B * QT
BT = B * T
T1 = T + 1
HT = H * T1
NG = 4
GC = HT // NG
F = 4 * D
FC = F // P
H1, DH = 16, 16
N1 = Q + T
LAYERS = 2
NPAIR = H // 2
LN_EPS = 1e-5
RMS_EPS = 1e-6
MASKED = -1e30
PRODUCTS = [(0, 0), (0, 1), (1, 0), (1, 1), (0, 2), (2, 0)]
ROW_MASK = len(PRODUCTS) * DH
ROWS_1 = ROW_MASK + 1
ROWS_2 = ROW_MASK + 2


def build_program(nc, a, out):
    with ExitStack() as ctx:
        def sb(name, shape, dt=F32, c=ctx):
            return c.enter_context(nc.sbuf_tensor(name, shape, dt))

        sems = {}

        def sem(name):
            if name not in sems:
                sems[name] = ctx.enter_context(nc.semaphore(name))
            return sems[name]

        bank = [ctx.enter_context(nc.psum_tensor(f"bank{i}", [P, 512], F32)) for i in range(8)]

        x_sb = sb("x_sb", [P, NU, D])
        ctxT = sb("ctxT", [P, DC, BT])
        ident = sb("ident", [P, P])
        mhalf = sb("mhalf", [P, 1])
        eps = sb("eps", [P, 2])
        tick = sb("tick", [P, 1])
        stats = sb("stats", [P, 2, 6])
        meanvar = sb("meanvar", [P, 2, 2])
        vareps = sb("vareps", [P, 2, 1])
        rstd = sb("rstd", [P, 2, 1])
        z_sb = sb("z_sb", [P, 2, D])
        lnsc = sb("lnsc", [P, 4, 2, DC])
        b1c = sb("b1c", [P, 2, FC])
        b2bc = sb("b2bc", [P, 2, D])
        stage = sb("stage", [P, 2 * FC * D])
        stage2 = sb("stage2", [P, 2, K])

        block = ctx.enter_context(nc.Block())

        regA = ExitStack()
        bkc = sb("bkc", [P, LAYERS, H], c=regA)
        bvc = sb("bvc", [P, LAYERS, H], c=regA)
        biaskc = sb("biaskc", [P, LAYERS, H], c=regA)
        biasvc = sb("biasvc", [P, LAYERS, H], c=regA)
        rows16 = sb("rows16", [H, LAYERS, 3, K], c=regA)
        prod16 = sb("prod16", [H, K], c=regA)
        cconst = sb("cconst", [H, LAYERS, 2], c=regA)
        kT = sb("kT", [P, 2, BT], c=regA)
        vT = sb("vT", [P, 2, BT], c=regA)
        u_sb = sb("u_sb", [P, DC, H], c=regA)
        miscc = sb("miscc", [P, 4, H], c=regA)
        VWb = sb("VWb", [H + 1, D], c=regA)
        c_parts = sb("c_parts", [H, 3, B * T1], BF16, c=regA)
        crow = sb("crow", [3, 2, HT], BF16, c=regA)
        ones3 = sb("ones3", [3, P], BF16, c=regA)
        WK = sb("WK", [P, DC, B, HT], c=regA)
        VW = sb("VW", [P, B, NPAIR, D], c=regA)
        p_sb = sb("p_sb", [P, HT], c=regA)
        pn = sb("pn", [P, HT], c=regA)
        mx = sb("mx", [P, 2, H], c=regA)
        sm = sb("sm", [P, H], c=regA)
        rs = sb("rs", [P, H], c=regA)
        hT = sb("hT", [P, 2, DC, P], c=regA)
        pT = sb("pT", [P, NPAIR, P], c=regA)
        pTb = sb("pTb", [32, P], c=regA)
        regA.close()

        regB = ExitStack()
        y_sb = sb("y_sb", [P, NU, D], c=regB)
        hM = sb("hM", [P, 2, DC, 512], c=regB)
        gT = sb("gT", [P, 2, FC, 512], c=regB)
        mlp1w = sb("mlp1w", [P, 2 * FC * D], c=regB)
        qw = sb("qw", [P, DC, D], c=regB)
        kw = sb("kw", [P, DC, D], c=regB)
        vw = sb("vw", [P, DC, D], c=regB)
        ow = sb("ow", [P, 4, D], c=regB)
        qbc = sb("qbc", [P, DC], c=regB)
        kbc = sb("kbc", [P, DC], c=regB)
        vbb = sb("vbb", [P, D], c=regB)
        obb = sb("obb", [P, D], c=regB)
        mask_i = sb("mask_i", [B, T], I32, c=regB)
        mask_f = sb("mask_f", [B, T], c=regB)
        mask_g = sb("mask_g", [B, T], c=regB)
        mask_row = sb("mask_row", [B, N1], BF16, c=regB)
        latT = sb("latT", [P, DC, Q], c=regB)
        ctxd = sb("ctxd", [P, DC, 2, T], c=regB)
        proj = sb("proj", [P, 2, DC, N1], c=regB)
        part = sb("part", [P, 2, DC, 3, N1], BF16, c=regB)
        Qst = sb("Qst", [ROWS_2, 2, H1, Q], BF16, c=regB)
        Kst = sb("Kst", [ROWS_2, 2, H1, N1], BF16, c=regB)
        vlat = sb("vlat", [P, 2, 2, H1, 2, DH], c=regB)
        vctx = sb("vctx", [P, 2, H1, 2, DH], c=regB)
        mx1 = sb("mx1", [P, 2, QT, H1], c=regB)
        nmx = sb("nmx", [H1, 2, Q], BF16, c=regB)
        plat = gT[:].rearrange("p s (a i) n -> p s a i n", i=4)[:, 0]
        pctx = sb("pctx", [P, 2, 2, Q], c=regB)
        ssum = sb("ssum", [P, Q], c=regB)
        rsum = sb("rsum", [P, Q], c=regB)
        aT = sb("aT", [P, 4, Q], c=regB)
        regB.close()

        qparts = nc.dram_tensor("qparts", (2, DC * P, 3, Q), BF16, kind="Internal").ap()
        kparts = nc.dram_tensor("kparts", (2, DC * P, 3, N1), BF16, kind="Internal").ap()
        mrows = nc.dram_tensor("mrows", (B, N1), BF16, kind="Internal").ap()

        wstage = stage[:, 0:2 * 1024].rearrange("p (s n) -> p s n", s=2)

        def wk_h(i, c):
            return wstage[:, i, c * K:(c + 1) * K]

        def wqT_h(i, m):
            return wstage[:, i, 256 + m * P:256 + (m + 1) * P]

        def wv_h(i, c):
            return wstage[:, i, 512 + c * K:512 + (c + 1) * K]

        def wo_h(i, lo=0, hi=D):
            return wstage[:, i, 768 + lo:768 + hi]

        uprod = p_sb[:, 0:DC * K].rearrange("p (c k) -> p c k", c=DC)
        c_sb = pn[0:H, 0:B * T1]
        WK5 = WK[:].rearrange("p m b (h t) -> p m b h t", t=T1)
        mlp0w = stage[:]
        mlpw = [(w[:, 0:DC * F].rearrange("p (c f) -> p c f", c=DC) if w is mlp0w
                 else w[:, 0:DC * F].rearrange("p (c f) -> p c f", c=DC),
                 w[:, DC * F:].rearrange("p (c d) -> p c d", c=FC)) for w in (mlp0w, mlp1w[:])]

        x_dram = a["x"].rearrange("b (t p) d -> p (b t) d", p=P)
        out_dram = out.rearrange("b (t p) d -> p (b t) d", p=P)

        def unit(layer, k, qt):
            return NU * layer + QT * k + qt + 1

        def looped(eng, first, last, step):
            step(first)
            with eng.Fori(first + 1, last) as k:
                step(k)
            step(last)

        def wait(eng, s, value):
            if isinstance(value, int) and value <= 0:
                return
            eng.wait_ge(sem(s), value)

        @block.sync
        def _(sp):
            sp.dma_start(ctxT[:], a["ctxT"].rearrange("(c p) n -> p c n", p=P)).then_inc(sem("ctx_in"), 16)

            def small_loads():
                for dst, src in (
                    [(lnsc[:], a["lnsc"])]
                    + [(b1c[:], a["b1c"]), (bkc[:], a["bkc"]), (bvc[:], a["bvc"]),
                       (biaskc[:], a["biaskc"]), (biasvc[:], a["biasvc"]), (rows16[:], a["rows16"])]
                    + [(b2bc[:, i, :], a["b2"][i:i + 1, :].partition_broadcast(P)) for i in range(2)]
                ):
                    sp.dma_start(dst, src).then_inc(sem("small_in"), 16)

            def known(value):
                return value if isinstance(value, int) else sp.snap(sp.to_reg(value))

            def settle():
                sp.wait_ge(sem("ctx_in"), 16)

            def load_heads(layer, j):
                n = NPAIR * layer + j
                folded, summed = known(4 * n), known(2 * n)
                for i in range(2):
                    head = known(j * 2 + i)
                    wait(sp, "vfold_mm", folded)
                    wait(sp, "usum_done", summed)
                    settle()
                    sp.dma_start(wstage[:, i, :], a[f"whead{layer}"][bass.ds(head, 1)].rearrange("o p n -> p (o n)")
                                 ).then_inc(sem(f"w_in{i}"), 16)
                    sp.dma_start(stage2[:, i, :], a[f"bq{layer}"][bass.ds(head, 1), :].partition_broadcast(P)
                                 ).then_inc(sem(f"w_in{i}"), 16)

            def attention_loads(layer):
                def c_rows(k):
                    for s in range(2):
                        through, b = known(NU * layer + QT * (k * 2 + s - 1)), known(k * 2 + s)
                        wait(sp, "logit_mm", through)
                        settle()
                        for j in range(3):
                            sp.dma_start(
                                crow[j:j + 1, s, :].rearrange("o (h t) -> o h t", t=T1),
                                c_parts[:, j, :].rearrange("h (b t) -> h b t", t=T1)[:, bass.ds(b, 1), :].rearrange("h o t -> h (o t)")
                            ).then_inc(sem(f"crow_in{s}"), 16)
                sp.wait_ge(sem("cparts_done"), layer + 1)
                c_rows(0)
                with sp.Fori(1, B // 2) as k:
                    c_rows(k)

            for layer in range(LAYERS):
                wait(sp, "av_mm", NU * layer)
                sp.dma_start(VWb[H:H + 1, :], a["bo"][layer:layer + 1, :]).then_inc(sem("bo_in"), 16)
                if layer == 0:
                    load_heads(0, 0)
                    small_loads()
                    sp.dma_start(x_sb[:], x_dram).then_inc(sem("x_in"), 16)
                else:
                    load_heads(layer, 0)
                with sp.Fori(1, NPAIR) as j:
                    load_heads(layer, j)
                attention_loads(layer)

            sp.wait_ge(sem("vfold_mm"), 4 * NPAIR * LAYERS)
            sp.wait_ge(sem("usum_done"), 2 * NPAIR * LAYERS)
            for n in range(2):
                if n == 1:
                    sp.wait_ge(sem("av_mm"), NU * LAYERS)
                    sp.wait_ge(sem("logit_mm"), NU * LAYERS)
                    sp.wait_ge(sem("resid_done"), NU * LAYERS)
                w1, w2 = mlpw[n]
                sp.dma_start(w1, a[f"w1_{n}"].rearrange("(c p) f -> p c f", p=P)).then_inc(sem(f"mlpw_in{n}"), 16)
                sp.dma_start(w2, a[f"w2_{n}"].rearrange("(c p) d -> p c d", p=P)).then_inc(sem(f"mlpw_in{n}"), 16)
            sp.wait_ge(sem("ow_zero"), 1)
            loads = [(mask_i[:], a["mask"]),
                     (qw[:], a["qw"].rearrange("(c p) n -> p c n", p=P)),
                     (kw[:], a["kw"].rearrange("(c p) n -> p c n", p=P)),
                     (vw[:], a["vw"].rearrange("(c p) n -> p c n", p=P)),
                     (qbc[:], a["qbc"]), (kbc[:], a["kbc"]),
                     (vbb[:], a["vb"][0:1, :].partition_broadcast(P)),
                     (obb[:], a["ob"][0:1, :].partition_broadcast(P))]
            for i in range(4):
                loads.append((ow[32 * i:32 * i + DH, :, :],
                              a["ow"].rearrange("(g i d) n -> i d g n", i=4, d=DH)[i]))
            for dst, src in loads:
                sp.dma_start(dst, src).then_inc(sem("l1w_in"), 16)
            L1_LOADS = 16 * len(loads)
            sp.wait_ge(sem("mask_done"), 1)
            sp.dma_start(mrows, mask_row[:]).then_inc(sem("mrows_out"), 16)
            sp.wait_ge(sem("mrows_out"), 16)

            def stack_in(b, s):
                made, written = known(b + 1), known((b + 1) * 64)
                early = isinstance(b, int) and b < 2
                lats, ctxs = (0, 0) if early else (known((b - 1) * H1), known((b - 1) * 4))
                b = known(b)
                sp.wait_ge(sem("qpart_done"), made)
                sp.wait_ge(sem("kpart_done"), made)
                for m in range(DC):
                    sp.dma_start(qparts[s, m * P:(m + 1) * P], part[:, 0, m, :, 0:Q]).then_inc(sem("parts_out"), 16)
                    sp.dma_start(kparts[s, m * P:(m + 1) * P], part[:, 1, m, :, :]).then_inc(sem("parts_out"), 16)
                sp.wait_ge(sem("parts_out"), written)
                wait(sp, "lat_mm", lats)
                wait(sp, "ctxp_mm", ctxs)
                settle()
                for j, (jq, jk) in enumerate(PRODUCTS):
                    rows = slice(j * DH, (j + 1) * DH)
                    sp.dma_start(Qst[rows, s, :, :], qparts[s].rearrange("(h d) j q -> d h j q", d=DH)[:, :, jq, :]
                                 ).then_inc(sem(f"stack_in{s}"), 16)
                    sp.dma_start(Kst[rows, s, :, :], kparts[s].rearrange("(h d) j q -> d h j q", d=DH)[:, :, jk, :]
                                 ).then_inc(sem(f"stack_in{s}"), 16)
                sp.dma_start(Kst[ROW_MASK:ROW_MASK + 1, s, :, :],
                             mrows[bass.ds(b, 1), :].unsqueeze(1).broadcast_to([1, H1, N1])).then_inc(sem(f"stack_in{s}"), 16)

            def max_in(b, s):
                sp.wait_ge(sem("nmx_done"), b + 1)
                sp.dma_start(Qst[ROWS_1:ROWS_2, s, :, :], nmx[:, s, :]).then_inc(sem(f"nmx_in{s}"), 16)

            sp.wait_ge(sem("ones_done"), 4)

            def l1_loads(k):
                for s in range(2):
                    stack_in(k * 2 + s, s)
                    max_in(k * 2 + s, s)
            l1_loads(0)
            with sp.Fori(1, B // 2) as k:
                l1_loads(k)

            for n in range(4):
                sp.wait_ge(sem("fc2_done"), 16 + 4 * (n + 1))
                sp.dma_start(out_dram[:, 4 * n:4 * n + 4, :], x_sb[:, 4 * n:4 * n + 4, :]).then_inc(sem("out_done"), 16)
            sp.wait_ge(sem("out_done"), 64)

        @block.gpsimd
        def _(pool):
            nc.gpsimd.memset(ident[:], 0.0).then_inc(sem("ident_zero"), 1)
            nc.gpsimd.memset(mhalf[:], -0.5)
            nc.gpsimd.memset(ones3[:], 1.0)
            nc.gpsimd.memset(eps[:, 0:1], LN_EPS)
            nc.gpsimd.memset(eps[:, 1:2], RMS_EPS)
            nc.gpsimd.memset(pTb[:], 1.0).then_inc(sem("pool_const"), 1)
            pool.wait_ge(sem("ident_zero"), 1)
            nc.gpsimd.affine_select(out=ident[:], in_=ident[:], compare_op=ALU.not_equal, fill=1.0, base=0,
                                    pattern=[[-1, P]], channel_multiplier=1).then_inc(sem("ident_done"), 1)

            def root(n, s, e):
                pool.wait_ge(sem("var_done"), n)
                nc.gpsimd.tensor_tensor(vareps[:, s, :], meanvar[:, s, 1:2], eps[:, e:e + 1], ALU.add
                                        ).then_inc(sem("vareps_done"), 1)
                pool.wait_ge(sem("vareps_done"), n)
                nc.gpsimd.tensor_tensor(rstd[:, s, :], vareps[:, s, :], mhalf[:], ALU.pow).then_inc(sem("rstd_done"), 1)

            pool.wait_ge(sem("pool_const"), 1)
            with pool.Fori(0, (LAYERS + 1) * NU // 2) as k:
                for s in range(2):
                    root(k * 2 + s + 1, s, 0)
            pool.wait_ge(sem("av_mm"), NU * LAYERS)
            pool.wait_ge(sem("logit_mm"), NU * LAYERS)
            pool.wait_ge(sem("resid_done"), NU * LAYERS)
            nc.gpsimd.memset(ow[:], 0.0).then_inc(sem("ow_zero"), 1)
            pool.wait_ge(sem("ow_zero"), 1)
            nc.gpsimd.memset(mask_row[:], 0.0).then_inc(sem("ow_zero"), 1)
            pool.wait_ge(sem("ow_zero"), 2)
            ones = (vlat[:], vctx[:], Qst[ROW_MASK:ROWS_2], Kst[ROW_MASK:ROWS_2])
            for n, t in enumerate(ones):
                nc.gpsimd.memset(t, 1.0).then_inc(sem("ones_done"), 1)
                pool.wait_ge(sem("ones_done"), n + 1)

            def ctx_copy(b):
                wait(pool, "v_mm", b)
                for r in range(2):
                    last = nc.gpsimd.tensor_copy(ctxd[:, :, r, :], ctxT[:, :, bass.ds(b * T, T)])
                last.then_inc(sem("ctxd_done"), 1)
            ctx_copy(0)
            with pool.Fori(1, B) as b:
                ctx_copy(b)
            with pool.Fori((LAYERS + 1) * NU // 2, (LAYERS + 2) * NU // 2) as k:
                for s in range(2):
                    root(k * 2 + s + 1, s, 1)

        @block.tensor
        def _(pe):
            def mm(o, w, r, start=True, stop=True):
                return pe.matmul(o, w, r, start=start, stop=stop)

            pe.wait_ge(sem("ctx_in"), 16)
            pe.wait_ge(sem("ident_done"), 1)

            def kv_pair(layer, j):
                n = NPAIR * layer + j
                for i in range(2):
                    g = 2 * n + i
                    pe.wait_ge(sem(f"w_in{i}"), 32 * n + 32)
                    wait(pe, "kT_done", g)
                    for c in range(DC):
                        ins = mm(bank[0][:], wk_h(i, c), ctxT[:, c, :], c == 0, c == DC - 1)
                    ins.then_inc(sem("k_mm"), 1)
                    wait(pe, "vT_done", g)
                    for c in range(DC):
                        ins = mm(bank[1][:], wv_h(i, c), ctxT[:, c, :], c == 0, c == DC - 1)
                    ins.then_inc(sem("v0_mm"), 1)
                    wait(pe, "misc_done", g)
                    for m in range(DC):
                        mm(bank[4][:, m:m + 1], wqT_h(i, m), biaskc[:, layer, bass.ds(j * 2 + i, 1)])
                    for m in range(DC):
                        ins = mm(bank[4][:, 2 + m:3 + m], wo_h(i, m * P, (m + 1) * P), biasvc[:, layer, bass.ds(j * 2 + i, 1)])
                    ins.then_inc(sem("misc_mm"), 1)
                    wait(pe, "kT_done", g + 1)
                    wait(pe, "wk_done", g)
                    for m in range(DC):
                        ins = mm(bank[2 + m][:], wqT_h(i, m), kT[:, i, :])
                    ins.then_inc(sem("kfold_mm"), 1)
                pe.wait_ge(sem("vT_done"), 2 * n + 2)
                for q in range(4):
                    wait(pe, "vw_done", 4 * n + (1 if q == 3 else 0))
                    for e in range(2):
                        b = 2 * q + e
                        for i in range(2):
                            ins = mm(bank[(5, 6, 7, 5)[q]][64 * i:64 * i + 64, e * D:(e + 1) * D],
                                     vT[:, i, b * T:(b + 1) * T], wo_h(i))
                    ins.then_inc(sem("vfold_mm"), 1)

            def c_row(layer):
                n = 2 * NPAIR * (layer + 1)
                pe.wait_ge(sem("usum_done"), n)
                pe.wait_ge(sem("kT_done"), n)
                for c in range(DC):
                    ins = mm(bank[0][0:H, :], u_sb[:, c, :], ctxT[:, c, :], c == 0, c == DC - 1)
                ins.then_inc(sem("c_mm"), 1)
                pe.wait_ge(sem("misc_done"), n)
                for m in range(DC):
                    ins = pe.transpose(bank[4][0:H, m * P:(m + 1) * P], miscc[:, 2 + m, :], ident[:])
                ins.then_inc(sem("vwb_mm"), 1)

            def turn_h(layer, k, qt):
                n = unit(layer, k, qt)
                pe.wait_ge(sem("z_done"), n)
                wait(pe, "hT_done", n - 1)
                for m in range(DC):
                    ins = pe.transpose(bank[6][:, m * P:(m + 1) * P], z_sb[:, qt, m * P:(m + 1) * P], ident[:])
                ins.then_inc(sem("h_mm"), 1)

            def logits(layer, k, qt):
                pass

            def att_unit(layer, k2, s, qt, first=False, last=False):
                b = k2 * 2 + s
                n = unit(layer, b, qt)
                pe.wait_ge(sem("hT_done"), n)
                wait(pe, "sub_done", n - 1)
                if qt == 0:
                    pe.wait_ge(sem(f"crow_in{s}"), 48 * (B // 2 * layer + k2 + 1))
                for g in range(NG):
                    cols = slice(g * GC, (g + 1) * GC)
                    for m in range(DC):
                        mm(bank[g][:, 0:GC], hT[:, qt, m, :], WK[:, m, bass.ds(b, 1), cols].rearrange("p o n -> p (o n)"), m == 0, False)
                    ins = mm(bank[g][:, 0:GC], ones3[:], crow[:, s, cols], False, True)
                ins.then_inc(sem("logit_mm"), 1)
                pqt = 1 - qt
                pb = b if qt == 1 else b - 1
                if not first:
                    turn_p(layer, pb, pqt)
                if not last:
                    turn_h(layer, b + (qt == 1), 1 - qt)
                if not first:
                    pv(layer, pb, pqt)

            def turn_p(layer, b, qt):
                n = unit(layer, b, qt)
                pe.wait_ge(sem("pn_done"), n)
                wait(pe, "resid_done", n - 1)
                pe.transpose(bank[7][0:H, D:D + P], pn[:, NPAIR * P:], ident[:])
                for j in range(NPAIR):
                    ins = pe.transpose(bank[4 + j // 4][:, (j % 4) * P:(j % 4 + 1) * P], pn[:, j * P:(j + 1) * P], ident[:])
                    if j % 4 == 3:
                        ins.then_inc(sem("p_mm"), 1)

            def pv(layer, b, qt):
                n = unit(layer, b, qt)
                for j in range(NPAIR):
                    if j % 4 == 0:
                        pe.wait_ge(sem("pT_done"), 2 * (n - 1) + j // 4 + 1)
                    mm(bank[7][:, 0:D], pT[:, j, :], VW[:, bass.ds(b, 1), j, :].rearrange("p o d -> p (o d)"), j == 0, False)
                mm(bank[7][:, 0:D], pTb[0:H + 1, :], VWb[:], False, True).then_inc(sem("av_mm"), 1)

            pe.wait_ge(sem("small_in"), 16 * 9)
            for layer in range(LAYERS):
                if layer:
                    pe.wait_ge(sem("sub_done"), NU * layer)
                    pe.wait_ge(sem("pT_done"), 2 * NU * layer)
                    pe.wait_ge(sem("hT_done"), NU * layer)
                    pe.wait_ge(sem("resid_done"), NU * layer)
                    pe.wait_ge(sem("c_done"), layer)
                    pe.wait_ge(sem("vwb_done"), layer)
                kv_pair(layer, 0)
                with pe.Fori(1, NPAIR) as j:
                    kv_pair(layer, j)
                c_row(layer)
                pe.wait_ge(sem("c_done"), layer + 1)
                pe.wait_ge(sem("vT_done"), H * (layer + 1))
                pe.wait_ge(sem("wk_done"), H * (layer + 1))
                pe.wait_ge(sem("vw_done"), 4 * NPAIR * (layer + 1))
                pe.wait_ge(sem("vwb_done"), layer + 1)
                pe.wait_ge(sem("wkb_done"), layer + 1)
                pe.wait_ge(sem("bo_in"), 16 * (layer + 1))
                turn_h(layer, 0, 0)
                for s in range(2):
                    for qt in range(QT):
                        att_unit(layer, 0, s, qt, first=(s == 0 and qt == 0))
                with pe.Fori(1, B // 2 - 1) as k2:
                    for s in range(2):
                        for qt in range(QT):
                            att_unit(layer, k2, s, qt)
                for s in range(2):
                    for qt in range(QT):
                        att_unit(layer, B // 2 - 1, s, qt, last=(s == 1 and qt == 1))
                turn_p(layer, B - 1, 1)
                pv(layer, B - 1, 1)

            def mlp(n):
                w1, w2 = mlpw[n]
                u0 = NU * (LAYERS + n)

                def turn(t):
                    wait(pe, "hM_done", 2 * (4 * n + t))
                    for i in range(4):
                        pe.wait_ge(sem("z_done"), u0 + 4 * t + i + 1)
                        for m in range(DC):
                            ins = pe.transpose(bank[6 + m][:, i * P:(i + 1) * P], z_sb[:, i % 2, m * P:(m + 1) * P], ident[:])
                        ins.then_inc(sem("h_mm"), 1)

                def fc1(t):
                    pe.wait_ge(sem("hM_done"), 2 * (4 * n + t + 1))
                    for f in range(FC):
                        g = FC * (4 * n + t) + f
                        wait(pe, "gelu_done", g - 3)
                        for m in range(DC):
                            ins = mm(bank[f % 4][:], w1[:, m, f * P:(f + 1) * P], hM[:, t % 2, m, :], m == 0, m == DC - 1)
                        ins.then_inc(sem("fc1_mm"), 1)

                def fc2(t):
                    for i in range(4):
                        r = 4 * (4 * n + t) + i
                        wait(pe, "fc2_done", r - 1)
                        for f in range(FC):
                            if i == 0:
                                pe.wait_ge(sem("gelu_done"), FC * (4 * n + t) + f + 1)
                            ins = mm(bank[4 + i % 2][:, 0:D], gT[:, t % 2, f, i * P:(i + 1) * P], w2[:, f, :], f == 0, f == FC - 1)
                        ins.then_inc(sem("fc2_mm"), 1)

                pe.wait_ge(sem(f"mlpw_in{n}"), 32)
                turn(0)
                for t in range(4):
                    fc1(t)
                    if t < 3:
                        turn(t + 1)
                    if t:
                        fc2(t - 1)
                fc2(3)

            pe.wait_ge(sem("sub_done"), NU * LAYERS)
            pe.wait_ge(sem("pT_done"), 2 * NU * LAYERS)
            pe.wait_ge(sem("hT_done"), NU * LAYERS)
            pe.wait_ge(sem("resid_done"), NU * LAYERS)
            mlp(0)

            def project(b):
                for u in range(2):
                    for m in range(DC):
                        ins = pe.transpose(bank[0][:, m * Q + u * P:m * Q + (u + 1) * P],
                                           x_sb_stage(u, m), ident[:])
                ins.then_inc(sem("lat_t_mm"), 1)

            def x_sb_stage(u, m):
                return xlat[:, u, m * P:(m + 1) * P]

            xlat = z_sb

            def stage_qkv(b):
                n = b
                pe.wait_ge(sem("xlat_done"), n + 1)
                wait(pe, "proj_free", 8 * n)
                project(b)
                pe.wait_ge(sem("latT_done"), n + 1)
                wait(pe, "proj_free", 8 * n)
                for m in range(DC):
                    for c in range(DC):
                        ins = mm(bank[1][:, m * Q:(m + 1) * Q], qw[:, c, m * P:(m + 1) * P], latT[:, c, :], c == 0, c == DC - 1)
                ins.then_inc(sem("q_mm"), 1)
                for m in range(DC):
                    pe.wait_ge(sem("proj_free"), 8 * n + (1 if m == 0 else 2))
                    for c in range(DC):
                        mm(bank[m][:, 0:Q], kw[:, c, m * P:(m + 1) * P], latT[:, c, :], c == 0, c == DC - 1)
                    for c in range(DC):
                        ins = mm(bank[m][:, Q:N1], kw[:, c, m * P:(m + 1) * P], ctxT[:, c, bass.ds(b * T, T)], c == 0, c == DC - 1)
                    ins.then_inc(sem("kk_mm"), 1)
                pe.wait_ge(sem("proj_free"), 8 * n + 3)
                for u in range(2):
                    for c in range(DC):
                        ins = mm(bank[0][:, u * D:(u + 1) * D], latT[:, c, u * P:(u + 1) * P], vw[:, c, :], c == 0, c == DC - 1)
                ins.then_inc(sem("vl_mm"), 1)
                pe.wait_ge(sem("proj_free"), 8 * n + 4)
                pe.wait_ge(sem("ctxd_done"), n + 1)
                for c in range(DC):
                    ins = mm(bank[1][:, 0:D], ctxd[:, c, :, :].rearrange("p r t -> p (r t)"), vw[:, c, :], c == 0, c == DC - 1)
                ins.then_inc(sem("v_mm"), 1)

            def max_product(b, s, r):
                qt, hp = r // 8, r % 8
                n = b * 16 + r
                wait(pe, "mx_done", n)
                if r == 0:
                    pe.wait_ge(sem(f"stack_in{s}"), 16 * 13 * half(b, s))
                for i in range(2):
                    h = 2 * hp + i
                    ins = mm(bank[2 + i][:, 0:N1], Qst[0:ROWS_1, s, h, qt * P:(qt + 1) * P], Kst[0:ROWS_1, s, h, :])
                ins.then_inc(sem("max_mm"), 1)

            def half(b, s):
                return b // 2 + 1 if isinstance(b, int) else halves[s]

            def turn_max(b, s):
                pe.wait_ge(sem("mx_done"), b * 16 + 16)
                pe.wait_ge(sem("proj_free"), 8 * b + 5 + 8 * early(b))
                for qt in range(QT):
                    ins = pe.transpose(bank[0][0:H1, qt * P:(qt + 1) * P], mx1[:, s, qt, :], ident[:])
                ins.then_inc(sem("mxt_mm"), 1)

            def early(b):
                return 0

            def second_product(b, s, g):
                if g == 0:
                    pe.wait_ge(sem(f"nmx_in{s}"), 16 * half(b, s))
                wait(pe, "pctx_done", b * 4 + g)
                for i in range(4):
                    h = 4 * g + i
                    ins = mm(bank[6][64 * (i % 2):64 * (i % 2) + 64, (i // 2) * Q:(i // 2 + 1) * Q],
                             Kst[0:ROWS_2, s, h, Q:N1], Qst[0:ROWS_2, s, h, :])
                ins.then_inc(sem("ctxp_mm"), 1)
                for i in range(4):
                    h = 4 * g + i
                    n = b * H1 + h
                    wait(pe, "plat_done", n - 1)
                    for c in range(2):
                        ins = mm(bank[4 + i % 2][:, c * Q:(c + 1) * Q], Kst[0:ROWS_2, s, h, c * P:(c + 1) * P], Qst[0:ROWS_2, s, h, :])
                    ins.then_inc(sem("lat_mm"), 1)

            def values_product(b, s, g):
                pe.wait_ge(sem("v_done"), b + 1)
                pe.wait_ge(sem("plat_done"), b * H1 + 4 * g + 4)
                pe.wait_ge(sem("pctx_done"), b * 4 + g + 1)
                wait(pe, "av_free", b * 4 + g)
                o = [bank[7][32 * i:32 * i + 32, 0:Q] for i in range(4)]
                for c in range(2):
                    for i in range(4):
                        h = 4 * g + i
                        mm(o[i], vlat[:, s, c, h, :, :].rearrange("p r d -> p (r d)"), plat[:, g % 2, i, c * Q:(c + 1) * Q], c == 0, False)
                for i in range(4):
                    h = 4 * g + i
                    rows = slice(64 * (i % 2), 64 * (i % 2) + 64)
                    ins = mm(o[i], vctx[rows, s, h, :, :].rearrange("p r d -> p (r d)"), pctx[rows, g % 2, i // 2, :], False, True)
                ins.then_inc(sem("o_mm"), 1)

            def out_product(b):
                pe.wait_ge(sem("aT_done"), b * 4 + 4)
                pe.wait_ge(sem("proj_free"), 8 * b + 6)
                for u in range(2):
                    for g in range(4):
                        ins = mm(bank[1][:, u * D:(u + 1) * D], aT[:, g, u * P:(u + 1) * P], ow[:, g, :], g == 0, g == 3)
                ins.then_inc(sem("y_mm"), 1)

            halves = [None, None]

            def l1_batch(b, s):
                stage_qkv(b)
                for r in range(16):
                    max_product(b, s, r)
                turn_max(b, s)
                for g in range(4):
                    second_product(b, s, g)
                    if g:
                        values_product(b, s, g - 1)
                values_product(b, s, 3)
                out_product(b)

            pe.wait_ge(sem("gelu_done"), FC * 4)
            pe.wait_ge(sem("hM_done"), 8)
            pe.wait_ge(sem("fc2_done"), 16)
            pe.wait_ge(sem("l1w_in"), 16 * 12)
            for s in range(2):
                l1_batch(s, s)
            with pe.Fori(1, B // 2) as k:
                for s in range(2):
                    halves[s] = k + 1
                    l1_batch(k * 2 + s, s)
            pe.wait_ge(sem("proj_free"), 8 * B)
            pe.wait_ge(sem("mx_done"), 16 * B)
            pe.wait_ge(sem("plat_done"), H1 * B)
            pe.wait_ge(sem("pctx_done"), 4 * B)
            pe.wait_ge(sem("av_free"), 4 * B)
            mlp(1)

        @block.scalar
        def _(act):
            def kv_pair(layer, j):
                n = NPAIR * layer + j
                for i in range(2):
                    g = 2 * n + i
                    act.wait_ge(sem("k_mm"), g + 1)
                    if not (isinstance(g, int) and g < 2):
                        act.wait_ge(sem("kfold_mm"), g - 1)
                    nc.scalar.activation(kT[:, i, :], bank[0][:], ACT.Identity, bias=bkc[:, layer, bass.ds(j * 2 + i, 1)]
                                         ).then_inc(sem("kT_done"), 1)
                    act.wait_ge(sem("v0_mm"), g + 1)
                    wait(act, "vfold_mm", 4 * n)
                    nc.scalar.activation(vT[:, i, :], bank[1][:], ACT.Identity, bias=bvc[:, layer, bass.ds(j * 2 + i, 1)]
                                         ).then_inc(sem("vT_done"), 1)
                for q in range(4):
                    act.wait_ge(sem("vfold_mm"), 4 * n + q + 1)
                    nc.scalar.activation(VW[:, 2 * q:2 * q + 2, bass.ds(j, 1), :].rearrange("p b o d -> p b (o d)"),
                                         bank[(5, 6, 7, 5)[q]][:].rearrange("p (b d) -> p b d", b=2), ACT.Copy
                                         ).then_inc(sem("vw_done"), 1)

            def turned_h(layer, k, qt):
                n = unit(layer, k, qt)
                act.wait_ge(sem("h_mm"), n)
                if not (isinstance(n, int) and n <= 2):
                    act.wait_ge(sem("logit_mm"), n - 2)
                for m in range(DC):
                    ins = nc.scalar.activation(hT[:, qt, m, :], bank[6][:, m * P:(m + 1) * P], ACT.Identity,
                                               bias=lnsc[:, layer, 1, m:m + 1], scale=lnsc[:, layer, 0, m:m + 1])
                ins.then_inc(sem("hT_done"), 1)

            def turned_p(layer, b, qt):
                n = unit(layer, b, qt)
                act.wait_ge(sem("p_mm"), 2 * n - 1)
                wait(act, "av_mm", n - 1)
                nc.scalar.activation(pTb[0:H, :], bank[7][0:H, D:D + P], ACT.Copy)
                nc.scalar.activation(pT[:, 0:4, :], bank[4][:].rearrange("p (j q) -> p j q", j=4), ACT.Copy
                                     ).then_inc(sem("pT_done"), 1)
                act.wait_ge(sem("p_mm"), 2 * n)
                nc.scalar.activation(pT[:, 4:8, :], bank[5][:].rearrange("p (j q) -> p j q", j=4), ACT.Copy
                                     ).then_inc(sem("pT_done"), 1)

            def att_unit(layer, b, qt, first=False, last=False):
                n = unit(layer, b, qt)
                if not first:
                    turned_p(layer, b if qt else b - 1, 1 - qt)
                if not last:
                    turned_h(layer, b + (qt == 1), 1 - qt)
                act.wait_ge(sem("sub_done"), n)
                nc.scalar.activation(p_sb[:], p_sb[:], ACT.Exp, scale=float(K) ** -0.5
                                     ).then_inc(sem("exp_done"), 1)

            act.wait_ge(sem("small_in"), 16 * 9)
            act.wait_ge(sem("pool_const"), 1)
            for layer in range(LAYERS):
                wait(act, "av_mm", NU * layer)
                kv_pair(layer, 0)
                with act.Fori(1, NPAIR) as j:
                    kv_pair(layer, j)
                act.wait_ge(sem("vwb_mm"), layer + 1)
                nc.scalar.activation(VWb[0:H, :], bank[4][0:H, 0:D], ACT.Copy).then_inc(sem("vwb_done"), 1)
                turned_h(layer, 0, 0)
                for qt in range(QT):
                    att_unit(layer, 0, qt, first=(qt == 0))
                with act.Fori(1, B - 1) as b:
                    for qt in range(QT):
                        att_unit(layer, b, qt)
                for qt in range(QT):
                    att_unit(layer, B - 1, qt, last=(qt == 1))
                turned_p(layer, B - 1, 1)

            def mlp(n, func):
                def turned(t):
                    u0 = NU * (LAYERS + n)
                    act.wait_ge(sem("h_mm"), u0 + 4 * t + 4)
                    if t >= 2:
                        act.wait_ge(sem("fc1_mm"), FC * (4 * n + t - 1))
                    for m in range(DC):
                        nc.scalar.activation(hM[:, t % 2, m, :], bank[6 + m][:], ACT.Identity,
                                             bias=lnsc[:, LAYERS + n, 1, m:m + 1], scale=lnsc[:, LAYERS + n, 0, m:m + 1]
                                             ).then_inc(sem("hM_done"), 1)

                turned(0)
                for t in range(4):
                    for f in range(FC):
                        act.wait_ge(sem("fc1_mm"), FC * (4 * n + t) + f + 1)
                        if f == 0 and t >= 2:
                            act.wait_ge(sem("fc2_mm"), 4 * (4 * n + t - 1))
                        nc.scalar.activation(gT[:, t % 2, f, :], bank[f % 4][:], func, bias=b1c[:, n, f:f + 1]
                                             ).then_inc(sem("gelu_done"), 1)
                    if t < 3:
                        turned(t + 1)

            act.wait_ge(sem("av_mm"), NU * LAYERS)
            act.wait_ge(sem("logit_mm"), NU * LAYERS)
            act.wait_ge(sem("resid_done"), NU * LAYERS)
            mlp(0, ACT.Gelu)

            def l1_batch(b, s):
                for g in range(4):
                    act.wait_ge(sem("ctxp_mm"), b * 4 + g + 1)
                    if not (isinstance(b, int) and b == 0 and g < 2):
                        act.wait_ge(sem("o_mm"), b * 4 + g - 1)
                    nc.scalar.activation(pctx[:, g % 2, :, :], bank[6][:].rearrange("p (i q) -> p i q", i=2), ACT.Exp,
                                         scale=1.0 / DH).then_inc(sem("pctx_done"), 1)
                    for i in range(4):
                        act.wait_ge(sem("lat_mm"), b * H1 + 4 * g + i + 1)
                        nc.scalar.activation(plat[:, g % 2, i, :], bank[4 + i % 2][:], ACT.Exp, scale=1.0 / DH
                                             ).then_inc(sem("plat_done"), 1)
            l1_batch(0, 0)
            with act.Fori(1, B) as b:
                l1_batch(b, 0)
            mlp(1, ACT.Gelu_apprx_tanh)

        @block.vector
        def _(dve):
            V = nc.vector

            def row_stats(n, s, row):
                if not (isinstance(n, int) and n <= 2):
                    dve.wait_ge(sem("z_done"), n - 2)
                V.bn_stats(stats[:, s, :], row).then_inc(sem("stats_done"), 1)
                dve.wait_ge(sem("stats_done"), n)
                V.memset(tick[:], 0.0)
                V.bn_aggr(meanvar[:, s, :], stats[:, s, :]).then_inc(sem("var_done"), 1)

            def row_norm(n, s, row):
                dve.wait_ge(sem("rstd_done"), n)
                if not (isinstance(n, int) and n <= 2):
                    dve.wait_ge(sem("h_mm"), n - 2)
                V.tensor_scalar(z_sb[:, s, :], row, meanvar[:, s, 0:1], rstd[:, s, :], ALU.subtract, ALU.mult
                                ).then_inc(sem("z_done"), 1)

            def x_row(b, qt):
                return x_sb[:, bass.ds(b * QT + qt, 1), :].rearrange("p o d -> p (o d)")

            def kv_pair(layer, j):
                n = NPAIR * layer + j
                for i in range(2):
                    g = 2 * n + i
                    dve.wait_ge(sem(f"w_in{i}"), 32 * n + 32)
                    wait(dve, "usum_done", g)
                    V.tensor_tensor(uprod, wstage[:, i, 0:2 * K].rearrange("p (c k) -> p c k", c=DC),
                                    stage2[:, i, :].unsqueeze(1).broadcast_to([P, DC, K]), ALU.mult
                                    ).then_inc(sem("uprod_done"), 1)
                    dve.wait_ge(sem("uprod_done"), g + 1)
                    V.tensor_reduce(u_sb[:, :, bass.ds(j * 2 + i, 1)].rearrange("p c o -> p (c o)"), uprod, AX.X, ALU.add
                                    ).then_inc(sem("usum_done"), 1)
                    dve.wait_ge(sem("misc_mm"), g + 1)
                    V.tensor_copy(miscc[:, :, bass.ds(j * 2 + i, 1)].rearrange("p c o -> p (c o)"), bank[4][:, 0:4]
                                  ).then_inc(sem("misc_done"), 1)
                    dve.wait_ge(sem("kfold_mm"), g + 1)
                    for m in range(DC):
                        ins = V.tensor_copy(WK5[:, m, :, bass.ds(j * 2 + i, 1), 0:T].rearrange("p b o t -> p b (o t)"),
                                            bank[2 + m][:].rearrange("p (b t) -> p b t", b=B))
                    ins.then_inc(sem("wk_done"), 1)

            def key_constants(layer):
                dve.wait_ge(sem("misc_done"), H * (layer + 1))
                for m in range(DC):
                    ins = V.tensor_copy(WK5[:, m, :, :, T], miscc[:, m, :].unsqueeze(1).broadcast_to([P, B, H]))
                ins.then_inc(sem("wkb_done"), 1)
                for e in range(2):
                    wait(dve, "prod16_done", 2 * layer + e)
                    V.tensor_tensor(prod16[:], rows16[:, layer, 0, :], rows16[:, layer, 1 + e, :], ALU.mult
                                    ).then_inc(sem("prod_done"), 1)
                    dve.wait_ge(sem("prod_done"), 2 * layer + e + 1)
                    V.tensor_reduce(cconst[:, layer, e:e + 1], prod16[:], AX.X, ALU.add).then_inc(sem("prod16_done"), 1)
                dve.wait_ge(sem("prod16_done"), 2 * layer + 2)
                dve.wait_ge(sem("c_mm"), layer + 1)
                c3 = c_sb.rearrange("h (b t) -> h b t", t=T1)
                V.tensor_scalar(c3[:, :, 0:T], bank[0][0:H, :].rearrange("h (b t) -> h b t", t=T),
                                cconst[:, layer, 0:1], None, ALU.add).then_inc(sem("c_done"), 1)
                V.tensor_copy(c3[:, :, T], cconst[:, layer, 1:2].broadcast_to([H, B])).then_inc(sem("cp"), 1)
                dve.wait_ge(sem("c_done"), layer + 1)
                for j in range(3):
                    n = 6 * layer + 2 * j
                    dve.wait_ge(sem("cp"), n + 1)
                    ins = V.tensor_copy(c_parts[:, j, :], c_sb)
                    if j < 2:
                        ins.then_inc(sem("cp"), 1)
                        dve.wait_ge(sem("cp"), n + 2)
                        V.tensor_tensor(c_sb, c_sb, c_parts[:, j, :], ALU.subtract).then_inc(sem("cp"), 1)
                    else:
                        ins.then_inc(sem("cparts_done"), 1)
                V.tensor_copy(prod16[:, 0:1], cconst[:, layer, 0:1]).then_inc(sem("cp"), 1)

            def residual(layer, b, qt):
                n = unit(layer, b, qt)
                dve.wait_ge(sem("av_mm"), n)
                V.tensor_tensor(x_row(b, qt), bank[7][:, 0:D], x_row(b, qt), ALU.add).then_inc(sem("resid_done"), 1)

            def att_unit(layer, b, qt, first=False, last=False):
                n = unit(layer, b, qt)
                if not last:
                    row_stats(n + 2, qt, x_row(b + 1, qt))
                dve.wait_ge(sem("logit_mm"), n)
                s5 = [bank[g][:, 0:GC].rearrange("p (h t) -> p h t", t=T1) for g in range(NG)]
                for g in range(NG):
                    ins = V.tensor_reduce(mx[:, qt, g * 4:(g + 1) * 4], s5[g], AX.X, ALU.max)
                ins.then_inc(sem("max_done"), 1)
                dve.wait_ge(sem("max_done"), n)
                wait(dve, "pn_done", n - 1)
                for g in range(NG):
                    ins = V.tensor_tensor(p_sb[:, g * GC:(g + 1) * GC].rearrange("p (h t) -> p h t", t=T1), s5[g],
                                          mx[:, qt, g * 4:(g + 1) * 4].unsqueeze(2).broadcast_to([P, 4, T1]), ALU.subtract)
                ins.then_inc(sem("sub_done"), 1)
                if not last:
                    row_norm(n + 2, qt, x_row(b + 1, qt))
                dve.wait_ge(sem("exp_done"), n)
                p3 = p_sb[:].rearrange("p (h t) -> p h t", t=T1)
                V.tensor_reduce(sm[:], p3, AX.X, ALU.add).then_inc(sem("sum_done"), 1)
                dve.wait_ge(sem("sum_done"), n)
                V.reciprocal(rs[:], sm[:]).then_inc(sem("rs_done"), 1)
                dve.wait_ge(sem("rs_done"), n)
                wait(dve, "p_mm", 2 * n - 2)
                V.tensor_tensor(pn[:, NPAIR * P:], p3[:, :, T], rs[:], ALU.mult)
                V.tensor_tensor(pn[:, 0:NPAIR * P].rearrange("p (h t) -> p h t", t=T), p3[:, :, 0:T],
                                rs[:].unsqueeze(2).broadcast_to([P, H, T]), ALU.mult).then_inc(sem("pn_done"), 1)
                if not first:
                    residual(layer, b if qt else b - 1, 1 - qt)

            dve.wait_ge(sem("small_in"), 16 * 9)
            dve.wait_ge(sem("x_in"), 16)
            for layer in range(LAYERS):
                wait(dve, "logit_mm", NU * layer)
                wait(dve, "p_mm", 2 * NU * layer)
                kv_pair(layer, 0)
                with dve.Fori(1, NPAIR) as j:
                    kv_pair(layer, j)
                if layer:
                    dve.wait_ge(sem("crow_in0"), 48 * (B // 2) * layer)
                    dve.wait_ge(sem("crow_in1"), 48 * (B // 2) * layer)
                key_constants(layer)
                wait(dve, "resid_done", NU * layer)
                for qt in range(QT):
                    row_stats(unit(layer, 0, qt), qt, x_row(0, qt))
                    row_norm(unit(layer, 0, qt), qt, x_row(0, qt))
                for qt in range(QT):
                    att_unit(layer, 0, qt, first=(qt == 0))
                with dve.Fori(1, B - 1) as b:
                    for qt in range(QT):
                        att_unit(layer, b, qt)
                for qt in range(QT):
                    att_unit(layer, B - 1, qt, last=True)
                residual(layer, B - 1, 1)

            def norms(n, src):
                def one(i):
                    u = NU * (LAYERS + n) + i + 1
                    if n == 0:
                        row_stats(u, i % 2, src[:, i, :])
                    else:
                        dve.wait_ge(sem("z_done"), u - 2)
                        V.tensor_tensor_reduce(ybuf[:], src[:, i, :], src[:, i, :], 1.0 / D, 0.0, ALU.mult, ALU.add,
                                               meanvar[:, i % 2, 1:2]).then_inc(sem("var_done"), 1)

                def two(i):
                    u = NU * (LAYERS + n) + i + 1
                    if n == 0:
                        row_norm(u, i % 2, src[:, i, :])
                    else:
                        dve.wait_ge(sem("rstd_done"), u)
                        dve.wait_ge(sem("h_mm"), u - 2)
                        V.tensor_scalar(z_sb[:, i % 2, :], src[:, i, :], rstd[:, i % 2, :], None, ALU.mult
                                        ).then_inc(sem("z_done"), 1)
                return one, two

            ybuf = ssum

            def mlp(n, src, dst):
                one, two = norms(n, src)
                for i in range(4):
                    one(i)
                    two(i)

                def added(t):
                    for i in range(4):
                        u = 4 * t + i
                        r = 4 * (4 * n + t) + i
                        V.tensor_tensor(dst[:, u, :], dst[:, u, :], b2bc[:, n, :], ALU.add).then_inc(sem("bias_done"), 1)
                        dve.wait_ge(sem("bias_done"), r + 1)
                        dve.wait_ge(sem("fc2_mm"), r + 1)
                        ins = V.tensor_tensor(dst[:, u, :], bank[4 + i % 2][:, 0:D], dst[:, u, :], ALU.add)
                        ins.then_inc(sem("fc2_done"), 1)
                for t in range(4):
                    if t < 3:
                        for i in range(4):
                            one(4 * t + 4 + i)
                            two(4 * t + 4 + i)
                    if t:
                        added(t - 1)
                added(3)

            dve.wait_ge(sem("resid_done"), NU * LAYERS)
            mlp(0, x_sb, x_sb)

            dve.wait_ge(sem("fc2_done"), 16)
            dve.wait_ge(sem("l1w_in"), 16 * 12)
            dve.wait_ge(sem("ow_zero"), 2)
            V.tensor_copy(mask_f[:], mask_i[:]).then_inc(sem("mask_step"), 1)
            dve.wait_ge(sem("mask_step"), 1)
            V.tensor_scalar(mask_g[:], mask_f[:], 0.0, MASKED, ALU.is_equal, ALU.mult).then_inc(sem("mask_step"), 1)
            dve.wait_ge(sem("mask_step"), 2)
            V.tensor_copy(mask_row[:, Q:N1], mask_g[:]).then_inc(sem("mask_done"), 1)
            dve.wait_ge(sem("ones_done"), 4)

            def step(b, i):
                return b * 10 + i

            def l1_batch(b, s):
                wait(dve, "lat_t_mm", b)
                for u in range(2):
                    ins = V.tensor_copy(z_sb[:, u, :], x_row(b, u))
                ins.then_inc(sem("xlat_done"), 1)
                dve.wait_ge(sem("lat_t_mm"), b + 1)
                wait(dve, "vl_mm", b)
                V.tensor_copy(latT[:], bank[0][:].rearrange("p (c q) -> p c q", c=DC)).then_inc(sem("latT_done"), 1)
                dve.wait_ge(sem("latT_done"), b + 1)
                dve.wait_ge(sem("q_mm"), b + 1)
                wait(dve, "parts_out", b * 64)
                for m in range(DC):
                    ins = V.tensor_scalar(proj[:, 0, m, 0:Q], bank[1][:, m * Q:(m + 1) * Q], qbc[:, m:m + 1], None, ALU.add)
                ins.then_inc(sem("proj_free"), 2)
                for m in range(DC):
                    dve.wait_ge(sem("kk_mm"), b * 2 + m + 1)
                    V.tensor_scalar(proj[:, 1, m, :], bank[m][:, 0:N1], kbc[:, m:m + 1], None, ALU.add
                                    ).then_inc(sem("proj_free"), 1)
                dve.wait_ge(sem("proj_free"), 8 * b + 4)
                for e, width, name in ((0, Q, "qpart_done"), (1, N1, "kpart_done")):
                    src = proj[:, e, :, 0:width]
                    for j in range(3):
                        ins = V.tensor_copy(part[:, e, :, j, 0:width], src)
                        if j < 2:
                            ins.then_inc(sem("split_step"), 1)
                            dve.wait_ge(sem("split_step"), 8 * b + 4 * e + 2 * j + 1)
                            V.tensor_tensor(src, src, part[:, e, :, j, 0:width], ALU.subtract).then_inc(sem("split_step"), 1)
                            dve.wait_ge(sem("split_step"), 8 * b + 4 * e + 2 * j + 2)
                        else:
                            ins.then_inc(sem(name), 1)
                if not (isinstance(b, int) and b < 2):
                    dve.wait_ge(sem("o_mm"), (b - 1) * 4)
                dve.wait_ge(sem("vl_mm"), b + 1)
                vb3 = vbb[:].rearrange("p (h d) -> p h d", d=DH)
                for u in range(2):
                    ins = V.tensor_tensor(vlat[:, s, u, :, 0, :], bank[0][:, u * D:(u + 1) * D].rearrange("p (h d) -> p h d", d=DH),
                                          vb3, ALU.add)
                ins.then_inc(sem("proj_free"), 1)
                dve.wait_ge(sem("v_mm"), b + 1)
                ins = V.tensor_tensor(vctx[:, s, :, 0, :], bank[1][:, 0:D].rearrange("p (h d) -> p h d", d=DH), vb3, ALU.add)
                ins.then_inc(sem("v_done"), 1)
                V.tensor_copy(ybuf[:, 0:1], vbb[:, 0:1]).then_inc(sem("proj_free"), 1)
                for r in range(16):
                    qt, hp = r // 8, r % 8
                    dve.wait_ge(sem("max_mm"), b * 16 + r + 1)
                    for i in range(2):
                        ins = V.tensor_reduce(mx1[:, s, qt, 2 * hp + i:2 * hp + i + 1], bank[2 + i][:, 0:N1], AX.X, ALU.max)
                    ins.then_inc(sem("mx_done"), 1)
                dve.wait_ge(sem("mxt_mm"), b + 1)
                V.tensor_scalar(nmx[:, s, :], bank[0][0:H1, 0:Q], -1.0, None, ALU.mult).then_inc(sem("nmx_done"), 1)
                for g in range(4):
                    n = b * 4 + g
                    dve.wait_ge(sem("o_mm"), n + 1)
                    wait(dve, "aT_done", n)
                    V.memset(tick[:], 0.0)
                    V.stream_shuffle(ssum[:], bank[7][:, 0:Q], [DH + i % DH for i in range(32)]).then_inc(sem("ssum_done"), 1)
                    dve.wait_ge(sem("ssum_done"), n + 1)
                    V.reciprocal(rsum[:], ssum[:]).then_inc(sem("rsum_done"), 1)
                    dve.wait_ge(sem("rsum_done"), n + 1)
                    if g == 0:
                        wait(dve, "y_mm", b)
                    V.tensor_tensor(aT[:, g, :], bank[7][:, 0:Q], rsum[:], ALU.mult).then_inc(sem("aT_done"), 1)
                    dve.wait_ge(sem("aT_done"), n + 1)
                    V.tensor_copy(rsum[:, 0:1], ssum[:, 0:1]).then_inc(sem("av_free"), 1)
                dve.wait_ge(sem("y_mm"), b + 1)
                for u in range(2):
                    ins = V.tensor_tensor(y_sb[:, bass.ds(b * QT + u, 1), :].rearrange("p o d -> p (o d)"),
                                          bank[1][:, u * D:(u + 1) * D], x_row(b, u), ALU.add)
                ins.then_inc(sem("proj_free"), 2)
                dve.wait_ge(sem("proj_free"), 8 * b + 8)
                for u in range(2):
                    ins = V.tensor_tensor(y_sb[:, bass.ds(b * QT + u, 1), :].rearrange("p o d -> p (o d)"),
                                          y_sb[:, bass.ds(b * QT + u, 1), :].rearrange("p o d -> p (o d)"), obb[:], ALU.add)
                ins.then_inc(sem("y_done"), 1)

            for s in range(2):
                l1_batch(s, s)
            with dve.Fori(1, B // 2) as k:
                for s in range(2):
                    l1_batch(k * 2 + s, s)
            dve.wait_ge(sem("y_done"), B)
            mlp(1, y_sb, x_sb)


def kernel(**inputs):
    import numpy as np
    import concourse.bacc as bacc
    from concourse.bass_utils import run_bass_kernel_spmd

    v = {k: np.asarray(x) for k, x in inputs.items()}

    def cols(n, width=P):
        return v[n].reshape(-1, width).T

    arrays = {"x": v["x"], "ctxT": v["ctx_2048"].reshape(BT, D).T, "mask": v["mask_BxS2_ik0"]}
    l0 = "L0_xattn_"
    for n in range(LAYERS):
        wq, wk, wv, wo = (v[f"{l0}w{c}{n + 1}"] for c in "qkvo")
        by_head = lambda w: w.reshape(DC, P, H, K).transpose(2, 1, 0, 3).reshape(H, P, DC * K)
        arrays[f"whead{n}"] = np.concatenate(
            [by_head(wk), wq.reshape(D, H, K).transpose(1, 2, 0), by_head(wv), wo.reshape(H, K, D)], axis=2)
        arrays[f"bq{n}"] = v[f"{l0}bq{n + 1}"].reshape(H, K)
    arrays["bkc"] = np.stack([cols(f"{l0}bk{n + 1}") for n in range(LAYERS)], 1)
    arrays["bvc"] = np.stack([cols(f"{l0}bv{n + 1}") for n in range(LAYERS)], 1)
    arrays["biaskc"] = np.stack([cols(f"{l0}bias_k{n + 1}") for n in range(LAYERS)], 1)
    arrays["biasvc"] = np.stack([cols(f"{l0}bias_v{n + 1}") for n in range(LAYERS)], 1)
    arrays["rows16"] = np.stack([np.stack([v[f"{l0}{c}{n + 1}"].reshape(H, K) for c in ("bq", "bk", "bias_k")], 1)
                                 for n in range(LAYERS)], 1)
    arrays["bo"] = np.stack([v[f"{l0}bo{n + 1}"] for n in range(LAYERS)])
    norms = [(v[f"{l0}ln{n}_scale"], v[f"{l0}ln{n}_offset"]) for n in ("1", "2", "_mlp")]
    norms.append((v["L1_xattn_postnorm_w"], np.zeros(D, np.float32)))
    arrays["lnsc"] = np.stack([np.stack([s.reshape(DC, P).T for s in pair], 1) for pair in norms], 1)
    l1 = "L1_xattn_"
    arrays["b1c"] = np.stack([cols(l0 + "b_fc1"), cols(l1 + "mlp_b1")], 1)
    arrays["b2"] = np.stack([v[l0 + "b_fc2"], v[l1 + "mlp_b2"]])
    arrays["w1_0"], arrays["w2_0"] = v[l0 + "w_fc1"], v[l0 + "w_fc2"]
    arrays["w1_1"], arrays["w2_1"] = v[l1 + "mlp_w1"], v[l1 + "mlp_w2"]
    arrays["qw"], arrays["ow"] = v[l1 + "q_w"], v[l1 + "out_w"]
    arrays["kw"], arrays["vw"] = v[l1 + "kv_w"][:, 0::2], v[l1 + "kv_w"][:, 1::2]
    arrays["qbc"] = cols(l1 + "q_b")
    arrays["kbc"] = v[l1 + "kv_b"][0::2].reshape(DC, P).T
    arrays["vb"] = v[l1 + "kv_b"][1::2].reshape(1, D)
    arrays["ob"] = v[l1 + "out_b"].reshape(1, D)
    arrays = {k: np.ascontiguousarray(x) for k, x in arrays.items()}

    nc = bacc.Bacc("TRN2", target_bir_lowering=False, num_devices=1)
    aps = {k: nc.dram_tensor(f"in_{k}", x.shape, mybir.dt.from_np(x.dtype), kind="ExternalInput").ap()
           for k, x in arrays.items()}
    out = nc.dram_tensor("out_0", (B, Q, D), F32, kind="ExternalOutput").ap()
    build_program(nc, aps, out)
    r = run_bass_kernel_spmd(nc, [{f"in_{k}": x for k, x in arrays.items()}], core_ids=[0])
    return r.results[0]["out_0"]
```

```python
from contextlib import ExitStack

import concourse.bass as bass
from concourse import mybir

F32 = mybir.dt.float32
BF16 = mybir.dt.bfloat16
I32 = mybir.dt.int32
ALU = mybir.AluOpType
ACT = mybir.ActivationFunctionType
AX = mybir.AxisListType

P = 128
B, Q, T, D = 8, 256, 64, 256
H, K = 16, 128
DC = D // P
QT = Q // P
NU = B * QT
BT = B * T
T1 = T + 1
HT = H * T1
NG = 4
GC = HT // NG
F = 4 * D
FC = F // P
H1, DH = 16, 16
N1 = Q + T
LAYERS = 2
NPAIR = H // 2
LN_EPS = 1e-5
RMS_EPS = 1e-6
MASKED = -1e30
PRODUCTS = [(0, 0), (0, 1), (1, 0), (1, 1), (0, 2), (2, 0)]
ROW_MASK = len(PRODUCTS) * DH
ROWS_1 = ROW_MASK + 1
ROWS_2 = ROW_MASK + 2


def build_program(nc, a, out):
    with ExitStack() as ctx:
        def sb(name, shape, dt=F32, c=ctx):
            return c.enter_context(nc.sbuf_tensor(name, shape, dt))

        sems = {}

        def sem(name):
            if name not in sems:
                sems[name] = ctx.enter_context(nc.semaphore(name))
            return sems[name]

        ps = ctx.enter_context(nc.psum_tensor("ps", [P, 8, 512], F32))
        bank = [ps[:, i, :] for i in range(8)]

        x_sb = sb("x_sb", [P, NU, D])
        ctxT = sb("ctxT", [P, DC, BT])
        ident = sb("ident", [P, P])
        mhalf = sb("mhalf", [P, 1])
        eps = sb("eps", [P, 2])
        tick = sb("tick", [P, 1])
        stats = sb("stats", [P, 2, 6])
        meanvar = sb("meanvar", [P, 2, 2])
        vareps = sb("vareps", [P, 2, 1])
        rstd = sb("rstd", [P, 2, 1])
        z_sb = sb("z_sb", [P, 2, D])
        lnsc = sb("lnsc", [P, 4, 2, DC])
        b1c = sb("b1c", [P, 2, FC])
        b2bc = sb("b2bc", [P, 2, D])
        stage = sb("stage", [P, 2 * FC * D])
        stage2 = sb("stage2", [P, 2, K])

        block = ctx.enter_context(nc.Block())

        regA = ExitStack()
        bkc = sb("bkc", [P, LAYERS, H], c=regA)
        bvc = sb("bvc", [P, LAYERS, H], c=regA)
        biaskc = sb("biaskc", [P, LAYERS, H], c=regA)
        biasvc = sb("biasvc", [P, LAYERS, H], c=regA)
        rows16 = sb("rows16", [H, LAYERS, 3, K], c=regA)
        prod16 = sb("prod16", [H, K], c=regA)
        cconst = sb("cconst", [H, LAYERS, 2], c=regA)
        kT = sb("kT", [P, 2, BT], c=regA)
        vT = sb("vT", [P, 2, BT], c=regA)
        u_sb = sb("u_sb", [P, DC, H], c=regA)
        miscc = sb("miscc", [P, 4, H], c=regA)
        VWb = sb("VWb", [H + 1, D], c=regA)
        c_parts = sb("c_parts", [H, 3, B * T1], BF16, c=regA)
        crow = sb("crow", [3, 2, HT], BF16, c=regA)
        ones3 = sb("ones3", [3, P], BF16, c=regA)
        WK = sb("WK", [P, DC, B, HT], c=regA)
        VW = sb("VW", [P, B, NPAIR, D], c=regA)
        p_sb = sb("p_sb", [P, HT], c=regA)
        pn = sb("pn", [P, HT], c=regA)
        mx = sb("mx", [P, 2, H], c=regA)
        sm = sb("sm", [P, H], c=regA)
        rs = sb("rs", [P, H], c=regA)
        hT = sb("hT", [P, 2, DC, P], c=regA)
        pT = sb("pT", [P, NPAIR, P], c=regA)
        pTb = sb("pTb", [32, P], c=regA)
        regA.close()

        regB = ExitStack()
        y_sb = sb("y_sb", [P, NU, D], c=regB)
        hM = sb("hM", [P, 2, DC, 512], c=regB)
        gT = sb("gT", [P, 2, FC, 512], c=regB)
        mlp1w = sb("mlp1w", [P, 2 * FC * D], c=regB)
        qw = sb("qw", [P, DC, D], c=regB)
        kw = sb("kw", [P, DC, D], c=regB)
        vw = sb("vw", [P, DC, D], c=regB)
        ow = sb("ow", [P, 4, D], c=regB)
        qbc = sb("qbc", [P, DC], c=regB)
        kbc = sb("kbc", [P, DC], c=regB)
        vbb = sb("vbb", [P, D], c=regB)
        obb = sb("obb", [P, D], c=regB)
        mask_i = sb("mask_i", [B, T], I32, c=regB)
        mask_f = sb("mask_f", [B, T], c=regB)
        mask_g = sb("mask_g", [B, T], c=regB)
        mask_row = sb("mask_row", [B, N1], BF16, c=regB)
        latT = sb("latT", [P, DC, Q], c=regB)
        ctxd = sb("ctxd", [P, DC, 2, T], c=regB)
        proj = sb("proj", [P, 2, DC, N1], c=regB)
        part = sb("part", [P, 2, DC, 3, N1], BF16, c=regB)
        Qst = sb("Qst", [ROWS_2, 2, H1, Q], BF16, c=regB)
        Kst = sb("Kst", [ROWS_2, 2, H1, N1], BF16, c=regB)
        vlat = sb("vlat", [P, 2, 2, H1, 2, DH], c=regB)
        vctx = sb("vctx", [P, 2, H1, 2, DH], c=regB)
        mx1 = sb("mx1", [P, 2, QT, H1], c=regB)
        nmx = sb("nmx", [H1, 2, Q], BF16, c=regB)
        plat = gT[:].rearrange("p s (a i) n -> p s a i n", i=4)[:, 0]
        pctx = sb("pctx", [P, 2, 2, Q], c=regB)
        ssum = sb("ssum", [P, Q], c=regB)
        rsum = sb("rsum", [P, Q], c=regB)
        aT = sb("aT", [P, 4, Q], c=regB)
        regB.close()

        qparts = nc.dram_tensor("qparts", (2, DC * P, 3, Q), BF16, kind="Internal").ap()
        kparts = nc.dram_tensor("kparts", (2, DC * P, 3, N1), BF16, kind="Internal").ap()
        mrows = nc.dram_tensor("mrows", (B, N1), BF16, kind="Internal").ap()

        wstage = stage[:, 0:2 * 1024].rearrange("p (s n) -> p s n", s=2)

        def wk_h(i, c):
            return wstage[:, i, c * K:(c + 1) * K]

        def wqT_h(i, m):
            return wstage[:, i, 256 + m * P:256 + (m + 1) * P]

        def wv_h(i, c):
            return wstage[:, i, 512 + c * K:512 + (c + 1) * K]

        def wo_h(i, lo=0, hi=D):
            return wstage[:, i, 768 + lo:768 + hi]

        uprod = p_sb[:, 0:DC * K].rearrange("p (c k) -> p c k", c=DC)
        c_sb = pn[0:H, 0:B * T1]
        WK5 = WK[:].rearrange("p m b (h t) -> p m b h t", t=T1)
        mlp0w = stage[:]
        mlpw = [(w[:, 0:DC * F].rearrange("p (c f) -> p c f", c=DC) if w is mlp0w
                 else w[:, 0:DC * F].rearrange("p (c f) -> p c f", c=DC),
                 w[:, DC * F:].rearrange("p (c d) -> p c d", c=FC)) for w in (mlp0w, mlp1w[:])]

        x_dram = a["x"].rearrange("b (t p) d -> p (b t) d", p=P)
        out_dram = out.rearrange("b (t p) d -> p (b t) d", p=P)

        def unit(layer, k, qt):
            return NU * layer + QT * k + qt + 1

        def looped(eng, first, last, step):
            step(first)
            with eng.Fori(first + 1, last) as k:
                step(k)
            step(last)

        def wait(eng, s, value):
            if isinstance(value, int) and value <= 0:
                return
            eng.wait_ge(sem(s), value)

        @block.sync
        def _(sp):
            sp.dma_start(ctxT[:], a["ctxT"].rearrange("(c p) n -> p c n", p=P)).then_inc(sem("ctx_in"), 16)

            def small_loads():
                for dst, src in (
                    [(lnsc[:], a["lnsc"])]
                    + [(b1c[:], a["b1c"]), (bkc[:], a["bkc"]), (bvc[:], a["bvc"]),
                       (biaskc[:], a["biaskc"]), (biasvc[:], a["biasvc"]), (rows16[:], a["rows16"])]
                    + [(b2bc[:, i, :], a["b2"][i:i + 1, :].partition_broadcast(P)) for i in range(2)]
                ):
                    sp.dma_start(dst, src).then_inc(sem("small_in"), 16)

            def known(value):
                return value if isinstance(value, int) else sp.snap(sp.to_reg(value))

            def settle():
                sp.wait_ge(sem("ctx_in"), 16)

            def load_heads(layer, j):
                n = NPAIR * layer + j
                folded, summed = known(4 * n), known(2 * n)
                for i in range(2):
                    head = known(j * 2 + i)
                    wait(sp, "vfold_mm", folded)
                    wait(sp, "usum_done", summed)
                    settle()
                    sp.dma_start(wstage[:, i, :], a[f"whead{layer}"][bass.ds(head, 1)].rearrange("o p n -> p (o n)")
                                 ).then_inc(sem(f"w_in{i}"), 16)
                    sp.dma_start(stage2[:, i, :], a[f"bq{layer}"][bass.ds(head, 1), :].partition_broadcast(P)
                                 ).then_inc(sem(f"w_in{i}"), 16)

            def attention_loads(layer):
                def c_rows(k):
                    for s in range(2):
                        through, b = known(NU * layer + QT * (k * 2 + s - 1)), known(k * 2 + s)
                        wait(sp, "logit_mm", through)
                        settle()
                        for j in range(3):
                            sp.dma_start(
                                crow[j:j + 1, s, :].rearrange("o (h t) -> o h t", t=T1),
                                c_parts[:, j, :].rearrange("h (b t) -> h b t", t=T1)[:, bass.ds(b, 1), :].rearrange("h o t -> h (o t)")
                            ).then_inc(sem(f"crow_in{s}"), 16)
                sp.wait_ge(sem("cparts_done"), layer + 1)
                c_rows(0)
                with sp.Fori(1, B // 2) as k:
                    c_rows(k)

            for layer in range(LAYERS):
                wait(sp, "av_mm", NU * layer)
                sp.dma_start(VWb[H:H + 1, :], a["bo"][layer:layer + 1, :]).then_inc(sem("bo_in"), 16)
                if layer == 0:
                    load_heads(0, 0)
                    small_loads()
                    sp.dma_start(x_sb[:], x_dram).then_inc(sem("x_in"), 16)
                else:
                    load_heads(layer, 0)
                with sp.Fori(1, NPAIR) as j:
                    load_heads(layer, j)
                attention_loads(layer)

            sp.wait_ge(sem("vfold_mm"), 4 * NPAIR * LAYERS)
            sp.wait_ge(sem("usum_done"), 2 * NPAIR * LAYERS)
            for n in range(2):
                if n == 1:
                    sp.wait_ge(sem("av_mm"), NU * LAYERS)
                    sp.wait_ge(sem("logit_mm"), NU * LAYERS)
                    sp.wait_ge(sem("resid_done"), NU * LAYERS)
                w1, w2 = mlpw[n]
                sp.dma_start(w1, a[f"w1_{n}"].rearrange("(c p) f -> p c f", p=P)).then_inc(sem(f"mlpw_in{n}"), 16)
                sp.dma_start(w2, a[f"w2_{n}"].rearrange("(c p) d -> p c d", p=P)).then_inc(sem(f"mlpw_in{n}"), 16)
            sp.wait_ge(sem("ow_zero"), 1)
            loads = [(mask_i[:], a["mask"]),
                     (qw[:], a["qw"].rearrange("(c p) n -> p c n", p=P)),
                     (kw[:], a["kw"].rearrange("(c p) n -> p c n", p=P)),
                     (vw[:], a["vw"].rearrange("(c p) n -> p c n", p=P)),
                     (qbc[:], a["qbc"]), (kbc[:], a["kbc"]),
                     (vbb[:], a["vb"][0:1, :].partition_broadcast(P)),
                     (obb[:], a["ob"][0:1, :].partition_broadcast(P))]
            for i in range(4):
                loads.append((ow[32 * i:32 * i + DH, :, :],
                              a["ow"].rearrange("(g i d) n -> i d g n", i=4, d=DH)[i]))
            for dst, src in loads:
                sp.dma_start(dst, src).then_inc(sem("l1w_in"), 16)
            L1_LOADS = 16 * len(loads)
            sp.wait_ge(sem("mask_done"), 1)
            sp.dma_start(mrows, mask_row[:]).then_inc(sem("mrows_out"), 16)
            sp.wait_ge(sem("mrows_out"), 16)

            def parts_out(k, s):
                b = k * 2 + s
                made, written, stacked = known(b + 1), known((b + 1) * 64), known(k * 16 * 13)
                sp.wait_ge(sem("qpart_done"), made)
                sp.wait_ge(sem("kpart_done"), made)
                wait(sp, f"stack_in{s}", stacked)
                for m in range(DC):
                    sp.dma_start(qparts[s, m * P:(m + 1) * P], part[:, 0, m, :, 0:Q]).then_inc(sem("parts_out"), 16)
                    sp.dma_start(kparts[s, m * P:(m + 1) * P], part[:, 1, m, :, :]).then_inc(sem("parts_out"), 16)
                sp.wait_ge(sem("parts_out"), written)

            def stack_in(k, s):
                b = k * 2 + s
                early = isinstance(b, int) and b < 2
                lats, ctxs = (0, 0) if early else (known((b - 1) * 8), known((b - 1) * 4))
                b = known(b)
                wait(sp, "lat_mm", lats)
                wait(sp, "ctxp_mm", ctxs)
                settle()
                for j, (jq, jk) in enumerate(PRODUCTS):
                    rows = slice(j * DH, (j + 1) * DH)
                    sp.dma_start(Qst[rows, s, :, :], qparts[s].rearrange("(h d) j q -> d h j q", d=DH)[:, :, jq, :]
                                 ).then_inc(sem(f"stack_in{s}"), 16)
                    sp.dma_start(Kst[rows, s, :, :], kparts[s].rearrange("(h d) j q -> d h j q", d=DH)[:, :, jk, :]
                                 ).then_inc(sem(f"stack_in{s}"), 16)
                sp.dma_start(Kst[ROW_MASK:ROW_MASK + 1, s, :, :],
                             mrows[bass.ds(b, 1), :].unsqueeze(1).broadcast_to([1, H1, N1])).then_inc(sem(f"stack_in{s}"), 16)

            def max_in(k, s):
                made = known(k * 2 + s + 1)
                sp.wait_ge(sem("nmx_done"), made)
                sp.dma_start(Qst[ROWS_1:ROWS_2, s, :, :], nmx[:, s, :]).then_inc(sem(f"nmx_in{s}"), 16)

            def l1_loads(k, last=False):
                for s in range(2):
                    if not last:
                        parts_out(k + 1, s)
                        stack_in(k + 1, s)
                    if not (last and s == 1):
                        max_in(k + s, 1 - s)

            sp.wait_ge(sem("ones_done"), 4)
            for s in range(2):
                parts_out(0, s)
                stack_in(0, s)
            max_in(0, 0)
            l1_loads(0)
            with sp.Fori(1, B // 2 - 1) as k:
                l1_loads(k)
            l1_loads(B // 2 - 1, last=True)

            for n in range(4):
                sp.wait_ge(sem("fc2_done"), 16 + 4 * (n + 1))
                sp.dma_start(out_dram[:, 4 * n:4 * n + 4, :], x_sb[:, 4 * n:4 * n + 4, :]).then_inc(sem("out_done"), 16)
            sp.wait_ge(sem("out_done"), 64)

        @block.gpsimd
        def _(pool):
            nc.gpsimd.memset(ident[:], 0.0).then_inc(sem("ident_zero"), 1)
            nc.gpsimd.memset(mhalf[:], -0.5)
            nc.gpsimd.memset(ones3[:], 1.0)
            nc.gpsimd.memset(eps[:, 0:1], LN_EPS)
            nc.gpsimd.memset(eps[:, 1:2], RMS_EPS)
            nc.gpsimd.memset(pTb[:], 1.0).then_inc(sem("pool_const"), 1)
            pool.wait_ge(sem("ident_zero"), 1)
            nc.gpsimd.affine_select(out=ident[:], in_=ident[:], compare_op=ALU.not_equal, fill=1.0, base=0,
                                    pattern=[[-1, P]], channel_multiplier=1).then_inc(sem("ident_done"), 1)

            def root(n, s, e):
                pool.wait_ge(sem("var_done"), n)
                nc.gpsimd.tensor_tensor(vareps[:, s, :], meanvar[:, s, 1:2], eps[:, e:e + 1], ALU.add
                                        ).then_inc(sem("vareps_done"), 1)
                pool.wait_ge(sem("vareps_done"), n)
                nc.gpsimd.tensor_tensor(rstd[:, s, :], vareps[:, s, :], mhalf[:], ALU.pow).then_inc(sem("rstd_done"), 1)

            pool.wait_ge(sem("pool_const"), 1)
            with pool.Fori(0, (LAYERS + 1) * NU // 2) as k:
                for s in range(2):
                    root(k * 2 + s + 1, s, 0)
            pool.wait_ge(sem("av_mm"), NU * LAYERS)
            pool.wait_ge(sem("logit_mm"), NU * LAYERS)
            pool.wait_ge(sem("resid_done"), NU * LAYERS)
            nc.gpsimd.memset(ow[:], 0.0).then_inc(sem("ow_zero"), 1)
            pool.wait_ge(sem("ow_zero"), 1)
            nc.gpsimd.memset(mask_row[:], 0.0).then_inc(sem("ow_zero"), 1)
            pool.wait_ge(sem("ow_zero"), 2)
            ones = (vlat[:], vctx[:], Qst[ROW_MASK:ROWS_2], Kst[ROW_MASK:ROWS_2])
            for n, t in enumerate(ones):
                nc.gpsimd.memset(t, 1.0).then_inc(sem("ones_done"), 1)
                pool.wait_ge(sem("ones_done"), n + 1)

            def ctx_copy(b):
                wait(pool, "v_mm", b)
                for r in range(2):
                    last = nc.gpsimd.tensor_copy(ctxd[:, :, r, :], ctxT[:, :, bass.ds(b * T, T)])
                last.then_inc(sem("ctxd_done"), 1)
            ctx_copy(0)
            with pool.Fori(1, B) as b:
                ctx_copy(b)
            with pool.Fori((LAYERS + 1) * NU // 2, (LAYERS + 2) * NU // 2) as k:
                for s in range(2):
                    root(k * 2 + s + 1, s, 1)

        @block.tensor
        def _(pe):
            def mm(o, w, r, start=True, stop=True):
                return pe.matmul(o, w, r, start=start, stop=stop)

            pe.wait_ge(sem("ctx_in"), 16)
            pe.wait_ge(sem("ident_done"), 1)

            def kv_pair(layer, j):
                n = NPAIR * layer + j
                for i in range(2):
                    g = 2 * n + i
                    pe.wait_ge(sem(f"w_in{i}"), 32 * n + 32)
                    wait(pe, "kT_done", g)
                    for c in range(DC):
                        ins = mm(bank[0], wk_h(i, c), ctxT[:, c, :], c == 0, c == DC - 1)
                    ins.then_inc(sem("k_mm"), 1)
                    wait(pe, "vT_done", g)
                    for c in range(DC):
                        ins = mm(bank[1], wv_h(i, c), ctxT[:, c, :], c == 0, c == DC - 1)
                    ins.then_inc(sem("v0_mm"), 1)
                    wait(pe, "misc_done", g)
                    for m in range(DC):
                        mm(bank[4][:, m:m + 1], wqT_h(i, m), biaskc[:, layer, bass.ds(j * 2 + i, 1)])
                    for m in range(DC):
                        ins = mm(bank[4][:, 2 + m:3 + m], wo_h(i, m * P, (m + 1) * P), biasvc[:, layer, bass.ds(j * 2 + i, 1)])
                    ins.then_inc(sem("misc_mm"), 1)
                    wait(pe, "kT_done", g + 1)
                    wait(pe, "wk_done", g)
                    for m in range(DC):
                        ins = mm(bank[2 + m], wqT_h(i, m), kT[:, i, :])
                    ins.then_inc(sem("kfold_mm"), 1)
                pe.wait_ge(sem("vT_done"), 2 * n + 2)
                for q in range(4):
                    wait(pe, "vw_done", 4 * n + (1 if q == 3 else 0))
                    for e in range(2):
                        b = 2 * q + e
                        for i in range(2):
                            ins = mm(bank[(5, 6, 7, 5)[q]][64 * i:64 * i + 64, e * D:(e + 1) * D],
                                     vT[:, i, b * T:(b + 1) * T], wo_h(i))
                    ins.then_inc(sem("vfold_mm"), 1)

            def c_row(layer):
                n = 2 * NPAIR * (layer + 1)
                pe.wait_ge(sem("usum_done"), n)
                pe.wait_ge(sem("kT_done"), n)
                for c in range(DC):
                    ins = mm(bank[0][0:H, :], u_sb[:, c, :], ctxT[:, c, :], c == 0, c == DC - 1)
                ins.then_inc(sem("c_mm"), 1)
                pe.wait_ge(sem("misc_done"), n)
                for m in range(DC):
                    ins = pe.transpose(bank[4][0:H, m * P:(m + 1) * P], miscc[:, 2 + m, :], ident[:])
                ins.then_inc(sem("vwb_mm"), 1)

            def turn_h(layer, k, qt):
                n = unit(layer, k, qt)
                pe.wait_ge(sem("z_done"), n)
                wait(pe, "hT_done", n - 1)
                for m in range(DC):
                    ins = pe.transpose(bank[6][:, m * P:(m + 1) * P], z_sb[:, qt, m * P:(m + 1) * P], ident[:])
                ins.then_inc(sem("h_mm"), 1)

            def logits(layer, k, qt):
                pass

            def att_unit(layer, k2, s, qt, first=False, last=False):
                b = k2 * 2 + s
                n = unit(layer, b, qt)
                pe.wait_ge(sem("hT_done"), n)
                wait(pe, "sub_done", n - 1)
                if qt == 0:
                    pe.wait_ge(sem(f"crow_in{s}"), 48 * (B // 2 * layer + k2 + 1))
                for g in range(NG):
                    cols = slice(g * GC, (g + 1) * GC)
                    for m in range(DC):
                        mm(bank[g][:, 0:GC], hT[:, qt, m, :], WK[:, m, bass.ds(b, 1), cols].rearrange("p o n -> p (o n)"), m == 0, False)
                    ins = mm(bank[g][:, 0:GC], ones3[:], crow[:, s, cols], False, True)
                ins.then_inc(sem("logit_mm"), 1)
                pqt = 1 - qt
                pb = b if qt == 1 else b - 1
                if not first:
                    turn_p(layer, pb, pqt)
                if not last:
                    turn_h(layer, b + (qt == 1), 1 - qt)
                if not first:
                    pv(layer, pb, pqt)

            def turn_p(layer, b, qt):
                n = unit(layer, b, qt)
                pe.wait_ge(sem("pn_done"), n)
                wait(pe, "resid_done", n - 1)
                pe.transpose(bank[7][0:H, D:D + P], pn[:, NPAIR * P:], ident[:])
                for j in range(NPAIR):
                    ins = pe.transpose(bank[4 + j // 4][:, (j % 4) * P:(j % 4 + 1) * P], pn[:, j * P:(j + 1) * P], ident[:])
                    if j % 4 == 3:
                        ins.then_inc(sem("p_mm"), 1)

            def pv(layer, b, qt):
                n = unit(layer, b, qt)
                for j in range(NPAIR):
                    if j % 4 == 0:
                        pe.wait_ge(sem("pT_done"), 2 * (n - 1) + j // 4 + 1)
                    mm(bank[7][:, 0:D], pT[:, j, :], VW[:, bass.ds(b, 1), j, :].rearrange("p o d -> p (o d)"), j == 0, False)
                mm(bank[7][:, 0:D], pTb[0:H + 1, :], VWb[:], False, True).then_inc(sem("av_mm"), 1)

            pe.wait_ge(sem("small_in"), 16 * 9)
            for layer in range(LAYERS):
                if layer:
                    pe.wait_ge(sem("sub_done"), NU * layer)
                    pe.wait_ge(sem("pT_done"), 2 * NU * layer)
                    pe.wait_ge(sem("hT_done"), NU * layer)
                    pe.wait_ge(sem("resid_done"), NU * layer)
                    pe.wait_ge(sem("c_done"), layer)
                    pe.wait_ge(sem("vwb_done"), layer)
                kv_pair(layer, 0)
                with pe.Fori(1, NPAIR) as j:
                    kv_pair(layer, j)
                c_row(layer)
                pe.wait_ge(sem("c_done"), layer + 1)
                pe.wait_ge(sem("vT_done"), H * (layer + 1))
                pe.wait_ge(sem("wk_done"), H * (layer + 1))
                pe.wait_ge(sem("vw_done"), 4 * NPAIR * (layer + 1))
                pe.wait_ge(sem("vwb_done"), layer + 1)
                pe.wait_ge(sem("wkb_done"), layer + 1)
                pe.wait_ge(sem("bo_in"), 16 * (layer + 1))
                turn_h(layer, 0, 0)
                for s in range(2):
                    for qt in range(QT):
                        att_unit(layer, 0, s, qt, first=(s == 0 and qt == 0))
                with pe.Fori(1, B // 2 - 1) as k2:
                    for s in range(2):
                        for qt in range(QT):
                            att_unit(layer, k2, s, qt)
                for s in range(2):
                    for qt in range(QT):
                        att_unit(layer, B // 2 - 1, s, qt, last=(s == 1 and qt == 1))
                turn_p(layer, B - 1, 1)
                pv(layer, B - 1, 1)

            def mlp(n):
                w1, w2 = mlpw[n]
                u0 = NU * (LAYERS + n)

                def turn(t):
                    wait(pe, "hM_done", 2 * (4 * n + t))
                    for i in range(4):
                        pe.wait_ge(sem("z_done"), u0 + 4 * t + i + 1)
                        for m in range(DC):
                            ins = pe.transpose(bank[6 + m][:, i * P:(i + 1) * P], z_sb[:, i % 2, m * P:(m + 1) * P], ident[:])
                        ins.then_inc(sem("h_mm"), 1)

                def fc1(t):
                    pe.wait_ge(sem("hM_done"), 2 * (4 * n + t + 1))
                    for f in range(FC):
                        g = FC * (4 * n + t) + f
                        wait(pe, "gelu_done", g - 3)
                        for m in range(DC):
                            ins = mm(bank[f % 4], w1[:, m, f * P:(f + 1) * P], hM[:, t % 2, m, :], m == 0, m == DC - 1)
                        ins.then_inc(sem("fc1_mm"), 1)

                def fc2(t):
                    for i in range(4):
                        r = 4 * (4 * n + t) + i
                        wait(pe, "fc2_done", r - 1)
                        for f in range(FC):
                            if i == 0:
                                pe.wait_ge(sem("gelu_done"), FC * (4 * n + t) + f + 1)
                            ins = mm(bank[4 + i % 2][:, 0:D], gT[:, t % 2, f, i * P:(i + 1) * P], w2[:, f, :], f == 0, f == FC - 1)
                        ins.then_inc(sem("fc2_mm"), 1)

                pe.wait_ge(sem(f"mlpw_in{n}"), 32)
                turn(0)
                for t in range(4):
                    fc1(t)
                    if t < 3:
                        turn(t + 1)
                    if t:
                        fc2(t - 1)
                fc2(3)

            pe.wait_ge(sem("sub_done"), NU * LAYERS)
            pe.wait_ge(sem("pT_done"), 2 * NU * LAYERS)
            pe.wait_ge(sem("hT_done"), NU * LAYERS)
            pe.wait_ge(sem("resid_done"), NU * LAYERS)
            mlp(0)

            def latents(k, s):
                b = k * 2 + s
                pe.wait_ge(sem("xlat_done"), b + 1)
                if not (isinstance(b, int) and b < 2):
                    pe.wait_ge(sem("nmx_done"), b - 1)
                elif b:
                    pe.wait_ge(sem("vl_done"), b)
                for u in range(2):
                    for m in range(DC):
                        ins = pe.transpose(bank[0][:, m * Q + u * P:m * Q + (u + 1) * P], z_sb[:, u, m * P:(m + 1) * P], ident[:])
                ins.then_inc(sem("lat_t_mm"), 1)

            def q_product(k, s):
                b = k * 2 + s
                pe.wait_ge(sem("latT_done"), b + 1)
                if not (isinstance(b, int) and b < 3):
                    pe.wait_ge(sem("y_read"), b - 2)
                elif b:
                    pe.wait_ge(sem("vc_done"), b)
                for m in range(DC):
                    for c in range(DC):
                        ins = mm(bank[1][:, m * Q:(m + 1) * Q], qw[:, c, m * P:(m + 1) * P], latT[:, c, :], c == 0, c == DC - 1)
                ins.then_inc(sem("q_mm"), 1)

            def k_product(k, s):
                b = k * 2 + s
                for m in range(DC):
                    if m:
                        pe.wait_ge(sem("q_read"), b + 1)
                    for c in range(DC):
                        mm(bank[m][:, 0:Q], kw[:, c, m * P:(m + 1) * P], latT[:, c, :], c == 0, c == DC - 1)
                    for c in range(DC):
                        ins = mm(bank[m][:, Q:N1], kw[:, c, m * P:(m + 1) * P], ctxT[:, c, bass.ds(b * T, T)], c == 0, c == DC - 1)
                    ins.then_inc(sem("kk_mm"), 1)

            def v_product(k, s):
                b = k * 2 + s
                pe.wait_ge(sem("k_read"), 2 * b + 1)
                for u in range(2):
                    for c in range(DC):
                        ins = mm(bank[0][:, u * D:(u + 1) * D], latT[:, c, u * P:(u + 1) * P], vw[:, c, :], c == 0, c == DC - 1)
                ins.then_inc(sem("vl_mm"), 1)
                pe.wait_ge(sem("k_read"), 2 * b + 2)
                pe.wait_ge(sem("ctxd_done"), b + 1)
                for c in range(DC):
                    ins = mm(bank[1][:, 0:D], ctxd[:, c, :, :].rearrange("p r t -> p (r t)"), vw[:, c, :], c == 0, c == DC - 1)
                ins.then_inc(sem("v_mm"), 1)

            def max_product(k, s, r):
                b = k * 2 + s
                qt, hp = r // 8, r % 8
                if r == 0:
                    pe.wait_ge(sem(f"stack_in{s}"), k * (16 * 13) + 16 * 13)
                if r < 2:
                    wait(pe, "plat_done", b * 8)
                else:
                    pe.wait_ge(sem("mx_done"), b * 16 + r - 1)
                for i in range(2):
                    h = 2 * hp + i
                    ins = mm(bank[2 + 2 * (r % 2) + i][:, 0:N1], Qst[0:ROWS_1, s, h, qt * P:(qt + 1) * P], Kst[0:ROWS_1, s, h, :])
                ins.then_inc(sem("max_mm"), 1)

            def turn_max(k, s):
                b = k * 2 + s
                pe.wait_ge(sem("mx_done"), b * 16 + 16)
                pe.wait_ge(sem("vl_done"), b + 2 if not (isinstance(b, int) and b == B - 1) else B)
                for qt in range(QT):
                    ins = pe.transpose(bank[0][0:H1, qt * P:(qt + 1) * P], mx1[:, s, qt, :], ident[:])
                ins.then_inc(sem("mxt_mm"), 1)

            def second_product(k, s, g):
                b = k * 2 + s
                if g == 0:
                    pe.wait_ge(sem(f"nmx_in{s}"), k * 16 + 16)
                wait(pe, "pctx_done", b * 4 + g)
                for i in range(4):
                    h = 4 * g + i
                    ins = mm(bank[6][64 * (i % 2):64 * (i % 2) + 64, (i // 2) * Q:(i // 2 + 1) * Q],
                             Kst[0:ROWS_2, s, h, Q:N1], Qst[0:ROWS_2, s, h, :])
                ins.then_inc(sem("ctxp_mm"), 1)
                for e in range(2):
                    n = b * 8 + 2 * g + e
                    wait(pe, "plat_done", n - 1)
                    for i in range(2):
                        h = 4 * g + 2 * e + i
                        for c in range(2):
                            ins = mm(bank[2 + 2 * e + i][:, c * Q:(c + 1) * Q], Kst[0:ROWS_2, s, h, c * P:(c + 1) * P], Qst[0:ROWS_2, s, h, :])
                    ins.then_inc(sem("lat_mm"), 1)

            def values_product(k, s, g):
                b = k * 2 + s
                pe.wait_ge(sem("vc_done"), b + 1)
                pe.wait_ge(sem("plat_done"), b * 8 + 2 * g + 2)
                pe.wait_ge(sem("pctx_done"), b * 4 + g + 1)
                wait(pe, "aT_done", b * 4 + g)
                o = [bank[7][32 * i:32 * i + 32, 0:Q] for i in range(4)]
                for c in range(2):
                    for i in range(4):
                        h = 4 * g + i
                        mm(o[i], vlat[:, s, c, h, :, :].rearrange("p r d -> p (r d)"), plat[:, g % 2, i, c * Q:(c + 1) * Q], c == 0, False)
                for i in range(4):
                    h = 4 * g + i
                    rows = slice(64 * (i % 2), 64 * (i % 2) + 64)
                    ins = mm(o[i], vctx[rows, s, h, :, :].rearrange("p r d -> p (r d)"), pctx[rows, g % 2, i // 2, :], False, True)
                ins.then_inc(sem("o_mm"), 1)

            def out_product(k, s):
                b = k * 2 + s
                pe.wait_ge(sem("aT_done"), b * 4 + 4)
                pe.wait_ge(sem("vc_done"), b + 3 if not (isinstance(b, int) and b > B - 3) else B)
                for u in range(2):
                    for g in range(4):
                        ins = mm(bank[1][:, u * D:(u + 1) * D], aT[:, g, u * P:(u + 1) * P], ow[:, g, :], g == 0, g == 3)
                ins.then_inc(sem("y_mm"), 1)

            def l1_step(k, s, ahead=2):
                one = (k + s, 1 - s)
                two = (k + 1, s)
                second_product(k, s, 0)
                if ahead > 1:
                    latents(*two)
                second_product(k, s, 1)
                values_product(k, s, 0)
                if ahead > 1:
                    q_product(*two)
                second_product(k, s, 2)
                values_product(k, s, 1)
                if ahead > 1:
                    k_product(*two)
                second_product(k, s, 3)
                values_product(k, s, 2)
                if ahead:
                    for r in range(2):
                        max_product(*one, r)
                values_product(k, s, 3)
                if ahead > 1:
                    v_product(*two)
                if ahead:
                    for r in range(2, 16):
                        max_product(*one, r)
                    turn_max(*one)
                out_product(k, s)

            pe.wait_ge(sem("gelu_done"), FC * 4)
            pe.wait_ge(sem("hM_done"), 8)
            pe.wait_ge(sem("fc2_done"), 16)
            pe.wait_ge(sem("l1w_in"), 16 * 12)
            for s in range(2):
                latents(0, s)
                q_product(0, s)
                k_product(0, s)
                v_product(0, s)
            for r in range(16):
                max_product(0, 0, r)
            turn_max(0, 0)
            for s in range(2):
                l1_step(0, s)
            with pe.Fori(1, B // 2 - 1) as k:
                for s in range(2):
                    l1_step(k, s)
            for s in range(2):
                l1_step(B // 2 - 1, s, ahead=1 - s)
            pe.wait_ge(sem("y_read"), B)
            pe.wait_ge(sem("plat_done"), 8 * B)
            pe.wait_ge(sem("pctx_done"), 4 * B)
            pe.wait_ge(sem("aT_done"), 4 * B)
            mlp(1)

        @block.scalar
        def _(act):
            def kv_pair(layer, j):
                n = NPAIR * layer + j
                for i in range(2):
                    g = 2 * n + i
                    act.wait_ge(sem("k_mm"), g + 1)
                    if not (isinstance(g, int) and g < 2):
                        act.wait_ge(sem("kfold_mm"), g - 1)
                    nc.scalar.activation(kT[:, i, :], bank[0], ACT.Identity, bias=bkc[:, layer, bass.ds(j * 2 + i, 1)]
                                         ).then_inc(sem("kT_done"), 1)
                    act.wait_ge(sem("v0_mm"), g + 1)
                    wait(act, "vfold_mm", 4 * n)
                    nc.scalar.activation(vT[:, i, :], bank[1], ACT.Identity, bias=bvc[:, layer, bass.ds(j * 2 + i, 1)]
                                         ).then_inc(sem("vT_done"), 1)
                for q in range(4):
                    act.wait_ge(sem("vfold_mm"), 4 * n + q + 1)
                    nc.scalar.activation(VW[:, 2 * q:2 * q + 2, bass.ds(j, 1), :].rearrange("p b o d -> p b (o d)"),
                                         bank[(5, 6, 7, 5)[q]].rearrange("p (b d) -> p b d", b=2), ACT.Copy
                                         ).then_inc(sem("vw_done"), 1)

            def turned_h(layer, k, qt):
                n = unit(layer, k, qt)
                act.wait_ge(sem("h_mm"), n)
                if not (isinstance(n, int) and n <= 2):
                    act.wait_ge(sem("logit_mm"), n - 2)
                for m in range(DC):
                    ins = nc.scalar.activation(hT[:, qt, m, :], bank[6][:, m * P:(m + 1) * P], ACT.Identity,
                                               bias=lnsc[:, layer, 1, m:m + 1], scale=lnsc[:, layer, 0, m:m + 1])
                ins.then_inc(sem("hT_done"), 1)

            def turned_p(layer, b, qt):
                n = unit(layer, b, qt)
                act.wait_ge(sem("p_mm"), 2 * n - 1)
                wait(act, "av_mm", n - 1)
                nc.scalar.activation(pTb[0:H, :], bank[7][0:H, D:D + P], ACT.Copy)
                nc.scalar.activation(pT[:, 0:4, :], bank[4].rearrange("p (j q) -> p j q", j=4), ACT.Copy
                                     ).then_inc(sem("pT_done"), 1)
                act.wait_ge(sem("p_mm"), 2 * n)
                nc.scalar.activation(pT[:, 4:8, :], bank[5].rearrange("p (j q) -> p j q", j=4), ACT.Copy
                                     ).then_inc(sem("pT_done"), 1)

            def att_unit(layer, b, qt, first=False, last=False):
                n = unit(layer, b, qt)
                if not first:
                    turned_p(layer, b if qt else b - 1, 1 - qt)
                if not last:
                    turned_h(layer, b + (qt == 1), 1 - qt)
                act.wait_ge(sem("sub_done"), n)
                nc.scalar.activation(p_sb[:], p_sb[:], ACT.Exp, scale=float(K) ** -0.5
                                     ).then_inc(sem("exp_done"), 1)

            act.wait_ge(sem("small_in"), 16 * 9)
            act.wait_ge(sem("pool_const"), 1)
            for layer in range(LAYERS):
                wait(act, "av_mm", NU * layer)
                kv_pair(layer, 0)
                with act.Fori(1, NPAIR) as j:
                    kv_pair(layer, j)
                act.wait_ge(sem("vwb_mm"), layer + 1)
                nc.scalar.activation(VWb[0:H, :], bank[4][0:H, 0:D], ACT.Copy).then_inc(sem("vwb_done"), 1)
                turned_h(layer, 0, 0)
                for qt in range(QT):
                    att_unit(layer, 0, qt, first=(qt == 0))
                with act.Fori(1, B - 1) as b:
                    for qt in range(QT):
                        att_unit(layer, b, qt)
                for qt in range(QT):
                    att_unit(layer, B - 1, qt, last=(qt == 1))
                turned_p(layer, B - 1, 1)

            def mlp(n, func):
                def turned(t):
                    u0 = NU * (LAYERS + n)
                    act.wait_ge(sem("h_mm"), u0 + 4 * t + 4)
                    if t >= 2:
                        act.wait_ge(sem("fc1_mm"), FC * (4 * n + t - 1))
                    for m in range(DC):
                        nc.scalar.activation(hM[:, t % 2, m, :], bank[6 + m], ACT.Identity,
                                             bias=lnsc[:, LAYERS + n, 1, m:m + 1], scale=lnsc[:, LAYERS + n, 0, m:m + 1]
                                             ).then_inc(sem("hM_done"), 1)

                turned(0)
                for t in range(4):
                    for f in range(FC):
                        act.wait_ge(sem("fc1_mm"), FC * (4 * n + t) + f + 1)
                        if f == 0 and t >= 2:
                            act.wait_ge(sem("fc2_mm"), 4 * (4 * n + t - 1))
                        nc.scalar.activation(gT[:, t % 2, f, :], bank[f % 4], func, bias=b1c[:, n, f:f + 1]
                                             ).then_inc(sem("gelu_done"), 1)
                    if t < 3:
                        turned(t + 1)

            act.wait_ge(sem("av_mm"), NU * LAYERS)
            act.wait_ge(sem("logit_mm"), NU * LAYERS)
            act.wait_ge(sem("resid_done"), NU * LAYERS)
            mlp(0, ACT.Gelu)

            def latents(b):
                wait(act, "lat_t_mm", b)
                nc.scalar.activation(z_sb[:], x_sb[:, bass.ds(b * QT, QT), :], ACT.Copy).then_inc(sem("xlat_done"), 1)

            def exponentials(b, ahead=True):
                for g in range(4):
                    act.wait_ge(sem("ctxp_mm"), b * 4 + g + 1)
                    if not (isinstance(b, int) and b == 0 and g < 2):
                        act.wait_ge(sem("o_mm"), b * 4 + g - 1)
                    nc.scalar.activation(pctx[:, g % 2, :, :], bank[6].rearrange("p (i q) -> p i q", i=2), ACT.Exp,
                                         scale=1.0 / DH).then_inc(sem("pctx_done"), 1)
                    for e in range(2):
                        act.wait_ge(sem("lat_mm"), b * 8 + 2 * g + e + 1)
                        nc.scalar.activation(plat[:, g % 2, 2 * e:2 * e + 2, :], ps[:, 2 + 2 * e:4 + 2 * e, :], ACT.Exp,
                                             scale=1.0 / DH).then_inc(sem("plat_done"), 1)
                if ahead:
                    latents(b + 3)

            act.wait_ge(sem("fc2_done"), 16)
            for b in range(3):
                latents(b)
            exponentials(0)
            with act.Fori(1, B - 3) as b:
                exponentials(b)
            for b in range(B - 3, B):
                exponentials(b, ahead=False)
            mlp(1, ACT.Gelu_apprx_tanh)

        @block.vector
        def _(dve):
            V = nc.vector

            def row_stats(n, s, row):
                if not (isinstance(n, int) and n <= 2):
                    dve.wait_ge(sem("z_done"), n - 2)
                V.bn_stats(stats[:, s, :], row).then_inc(sem("stats_done"), 1)
                dve.wait_ge(sem("stats_done"), n)
                V.memset(tick[:], 0.0)
                V.bn_aggr(meanvar[:, s, :], stats[:, s, :]).then_inc(sem("var_done"), 1)

            def row_norm(n, s, row):
                dve.wait_ge(sem("rstd_done"), n)
                if not (isinstance(n, int) and n <= 2):
                    dve.wait_ge(sem("h_mm"), n - 2)
                V.tensor_scalar(z_sb[:, s, :], row, meanvar[:, s, 0:1], rstd[:, s, :], ALU.subtract, ALU.mult
                                ).then_inc(sem("z_done"), 1)

            def x_row(b, qt):
                return x_sb[:, bass.ds(b * QT + qt, 1), :].rearrange("p o d -> p (o d)")

            def kv_pair(layer, j):
                n = NPAIR * layer + j
                for i in range(2):
                    g = 2 * n + i
                    dve.wait_ge(sem(f"w_in{i}"), 32 * n + 32)
                    wait(dve, "usum_done", g)
                    V.tensor_tensor(uprod, wstage[:, i, 0:2 * K].rearrange("p (c k) -> p c k", c=DC),
                                    stage2[:, i, :].unsqueeze(1).broadcast_to([P, DC, K]), ALU.mult
                                    ).then_inc(sem("uprod_done"), 1)
                    dve.wait_ge(sem("uprod_done"), g + 1)
                    V.tensor_reduce(u_sb[:, :, bass.ds(j * 2 + i, 1)].rearrange("p c o -> p (c o)"), uprod, AX.X, ALU.add
                                    ).then_inc(sem("usum_done"), 1)
                    dve.wait_ge(sem("misc_mm"), g + 1)
                    V.tensor_copy(miscc[:, :, bass.ds(j * 2 + i, 1)].rearrange("p c o -> p (c o)"), bank[4][:, 0:4]
                                  ).then_inc(sem("misc_done"), 1)
                    dve.wait_ge(sem("kfold_mm"), g + 1)
                    for m in range(DC):
                        ins = V.tensor_copy(WK5[:, m, :, bass.ds(j * 2 + i, 1), 0:T].rearrange("p b o t -> p b (o t)"),
                                            bank[2 + m].rearrange("p (b t) -> p b t", b=B))
                    ins.then_inc(sem("wk_done"), 1)

            def key_constants(layer):
                dve.wait_ge(sem("misc_done"), H * (layer + 1))
                for m in range(DC):
                    ins = V.tensor_copy(WK5[:, m, :, :, T], miscc[:, m, :].unsqueeze(1).broadcast_to([P, B, H]))
                ins.then_inc(sem("wkb_done"), 1)
                for e in range(2):
                    wait(dve, "prod16_done", 2 * layer + e)
                    V.tensor_tensor(prod16[:], rows16[:, layer, 0, :], rows16[:, layer, 1 + e, :], ALU.mult
                                    ).then_inc(sem("prod_done"), 1)
                    dve.wait_ge(sem("prod_done"), 2 * layer + e + 1)
                    V.tensor_reduce(cconst[:, layer, e:e + 1], prod16[:], AX.X, ALU.add).then_inc(sem("prod16_done"), 1)
                dve.wait_ge(sem("prod16_done"), 2 * layer + 2)
                dve.wait_ge(sem("c_mm"), layer + 1)
                c3 = c_sb.rearrange("h (b t) -> h b t", t=T1)
                V.tensor_scalar(c3[:, :, 0:T], bank[0][0:H, :].rearrange("h (b t) -> h b t", t=T),
                                cconst[:, layer, 0:1], None, ALU.add).then_inc(sem("c_done"), 1)
                V.tensor_copy(c3[:, :, T], cconst[:, layer, 1:2].broadcast_to([H, B])).then_inc(sem("cp"), 1)
                dve.wait_ge(sem("c_done"), layer + 1)
                for j in range(3):
                    n = 6 * layer + 2 * j
                    dve.wait_ge(sem("cp"), n + 1)
                    ins = V.tensor_copy(c_parts[:, j, :], c_sb)
                    if j < 2:
                        ins.then_inc(sem("cp"), 1)
                        dve.wait_ge(sem("cp"), n + 2)
                        V.tensor_tensor(c_sb, c_sb, c_parts[:, j, :], ALU.subtract).then_inc(sem("cp"), 1)
                    else:
                        ins.then_inc(sem("cparts_done"), 1)
                V.tensor_copy(prod16[:, 0:1], cconst[:, layer, 0:1]).then_inc(sem("cp"), 1)

            def residual(layer, b, qt):
                n = unit(layer, b, qt)
                dve.wait_ge(sem("av_mm"), n)
                V.tensor_tensor(x_row(b, qt), bank[7][:, 0:D], x_row(b, qt), ALU.add).then_inc(sem("resid_done"), 1)

            def att_unit(layer, b, qt, first=False, last=False):
                n = unit(layer, b, qt)
                if not last:
                    row_stats(n + 2, qt, x_row(b + 1, qt))
                dve.wait_ge(sem("logit_mm"), n)
                s4 = ps[:, 0:NG, 0:GC].rearrange("p g (h t) -> p g h t", t=T1)
                V.tensor_reduce(mx[:, qt, :].rearrange("p (g h) -> p g h", g=NG), s4, AX.X, ALU.max).then_inc(sem("max_done"), 1)
                dve.wait_ge(sem("max_done"), n)
                wait(dve, "pn_done", n - 1)
                V.tensor_tensor(p_sb[:].rearrange("p (g h t) -> p g h t", g=NG, t=T1), s4,
                                mx[:, qt, :].rearrange("p (g h) -> p g h", g=NG).unsqueeze(3).broadcast_to([P, NG, H // NG, T1]),
                                ALU.subtract).then_inc(sem("sub_done"), 1)
                if not last:
                    row_norm(n + 2, qt, x_row(b + 1, qt))
                dve.wait_ge(sem("exp_done"), n)
                p3 = p_sb[:].rearrange("p (h t) -> p h t", t=T1)
                V.tensor_reduce(sm[:], p3, AX.X, ALU.add).then_inc(sem("sum_done"), 1)
                dve.wait_ge(sem("sum_done"), n)
                V.reciprocal(rs[:], sm[:]).then_inc(sem("rs_done"), 1)
                dve.wait_ge(sem("rs_done"), n)
                wait(dve, "p_mm", 2 * n - 2)
                V.tensor_tensor(pn[:, NPAIR * P:], p3[:, :, T], rs[:], ALU.mult)
                V.tensor_tensor(pn[:, 0:NPAIR * P].rearrange("p (h t) -> p h t", t=T), p3[:, :, 0:T],
                                rs[:].unsqueeze(2).broadcast_to([P, H, T]), ALU.mult).then_inc(sem("pn_done"), 1)
                if not first:
                    residual(layer, b if qt else b - 1, 1 - qt)

            dve.wait_ge(sem("small_in"), 16 * 9)
            dve.wait_ge(sem("x_in"), 16)
            for layer in range(LAYERS):
                wait(dve, "logit_mm", NU * layer)
                wait(dve, "p_mm", 2 * NU * layer)
                kv_pair(layer, 0)
                with dve.Fori(1, NPAIR) as j:
                    kv_pair(layer, j)
                if layer:
                    dve.wait_ge(sem("crow_in0"), 48 * (B // 2) * layer)
                    dve.wait_ge(sem("crow_in1"), 48 * (B // 2) * layer)
                key_constants(layer)
                wait(dve, "resid_done", NU * layer)
                for qt in range(QT):
                    row_stats(unit(layer, 0, qt), qt, x_row(0, qt))
                    row_norm(unit(layer, 0, qt), qt, x_row(0, qt))
                for qt in range(QT):
                    att_unit(layer, 0, qt, first=(qt == 0))
                with dve.Fori(1, B - 1) as b:
                    for qt in range(QT):
                        att_unit(layer, b, qt)
                for qt in range(QT):
                    att_unit(layer, B - 1, qt, last=True)
                residual(layer, B - 1, 1)

            def norms(n, src):
                def one(i):
                    u = NU * (LAYERS + n) + i + 1
                    if n == 0:
                        row_stats(u, i % 2, src[:, i, :])
                    else:
                        dve.wait_ge(sem("z_done"), u - 2)
                        V.tensor_tensor_reduce(ybuf[:], src[:, i, :], src[:, i, :], 1.0 / D, 0.0, ALU.mult, ALU.add,
                                               meanvar[:, i % 2, 1:2]).then_inc(sem("var_done"), 1)

                def two(i):
                    u = NU * (LAYERS + n) + i + 1
                    if n == 0:
                        row_norm(u, i % 2, src[:, i, :])
                    else:
                        dve.wait_ge(sem("rstd_done"), u)
                        dve.wait_ge(sem("h_mm"), u - 2)
                        V.tensor_scalar(z_sb[:, i % 2, :], src[:, i, :], rstd[:, i % 2, :], None, ALU.mult
                                        ).then_inc(sem("z_done"), 1)
                return one, two

            ybuf = ssum

            def mlp(n, src, dst):
                one, two = norms(n, src)
                for i in range(4):
                    one(i)
                    two(i)

                def added(t):
                    for i in range(4):
                        u = 4 * t + i
                        r = 4 * (4 * n + t) + i
                        V.tensor_tensor(dst[:, u, :], dst[:, u, :], b2bc[:, n, :], ALU.add).then_inc(sem("bias_done"), 1)
                        dve.wait_ge(sem("bias_done"), r + 1)
                        dve.wait_ge(sem("fc2_mm"), r + 1)
                        ins = V.tensor_tensor(dst[:, u, :], bank[4 + i % 2][:, 0:D], dst[:, u, :], ALU.add)
                        ins.then_inc(sem("fc2_done"), 1)
                for t in range(4):
                    if t < 3:
                        for i in range(4):
                            one(4 * t + 4 + i)
                            two(4 * t + 4 + i)
                    if t:
                        added(t - 1)
                added(3)

            dve.wait_ge(sem("resid_done"), NU * LAYERS)
            mlp(0, x_sb, x_sb)

            dve.wait_ge(sem("fc2_done"), 16)
            dve.wait_ge(sem("l1w_in"), 16 * 12)
            dve.wait_ge(sem("ow_zero"), 2)
            V.tensor_copy(mask_f[:], mask_i[:]).then_inc(sem("mask_step"), 1)
            dve.wait_ge(sem("mask_step"), 1)
            V.tensor_scalar(mask_g[:], mask_f[:], 0.0, MASKED, ALU.is_equal, ALU.mult).then_inc(sem("mask_step"), 1)
            dve.wait_ge(sem("mask_step"), 2)
            V.tensor_copy(mask_row[:, Q:N1], mask_g[:]).then_inc(sem("mask_done"), 1)
            dve.wait_ge(sem("ones_done"), 4)

            def q_k_copies(k, s, part_of):
                b = k * 2 + s
                if part_of == 0:
                    dve.wait_ge(sem("lat_t_mm"), b + 1)
                    wait(dve, "vl_mm", b)
                    V.tensor_copy(latT[:], bank[0].rearrange("p (c q) -> p c q", c=DC)).then_inc(sem("latT_done"), 1)
                elif part_of == 1:
                    dve.wait_ge(sem("q_mm"), b + 1)
                    wait(dve, "qpart_done", b)
                    for m in range(DC):
                        ins = V.tensor_scalar(proj[:, 0, m, 0:Q], bank[1][:, m * Q:(m + 1) * Q], qbc[:, m:m + 1], None, ALU.add)
                    ins.then_inc(sem("q_read"), 1)
                elif part_of == 2:
                    wait(dve, "kpart_done", b)
                    for m in range(DC):
                        dve.wait_ge(sem("kk_mm"), b * 2 + m + 1)
                        V.tensor_scalar(proj[:, 1, m, :], bank[m][:, 0:N1], kbc[:, m:m + 1], None, ALU.add
                                        ).then_inc(sem("k_read"), 1)
                else:
                    e, width, name, read = ((0, Q, "qpart_done", b + 1), (1, N1, "kpart_done", 2 * b + 2))[part_of - 3]
                    if e == 0:
                        wait(dve, "parts_out", b * 64)
                    dve.wait_ge(sem("k_read" if e else "q_read"), read)
                    src = proj[:, e, :, 0:width]
                    for j in range(3):
                        ins = V.tensor_copy(part[:, e, :, j, 0:width], src)
                        if j < 2:
                            ins.then_inc(sem("split_step"), 1)
                            dve.wait_ge(sem("split_step"), 8 * b + 4 * e + 2 * j + 1)
                            V.tensor_tensor(src, src, part[:, e, :, j, 0:width], ALU.subtract).then_inc(sem("split_step"), 1)
                            dve.wait_ge(sem("split_step"), 8 * b + 4 * e + 2 * j + 2)
                        else:
                            ins.then_inc(sem(name), 1)

            def v_copies(k, s):
                b = k * 2 + s
                if not (isinstance(b, int) and b < 2):
                    dve.wait_ge(sem("o_mm"), (b - 1) * 4)
                dve.wait_ge(sem("vl_mm"), b + 1)
                vb3 = vbb[:].rearrange("p (h d) -> p h d", d=DH)
                for u in range(2):
                    ins = V.tensor_tensor(vlat[:, s, u, :, 0, :], bank[0][:, u * D:(u + 1) * D].rearrange("p (h d) -> p h d", d=DH),
                                          vb3, ALU.add)
                ins.then_inc(sem("vl_done"), 1)
                dve.wait_ge(sem("v_mm"), b + 1)
                V.tensor_tensor(vctx[:, s, :, 0, :], bank[1][:, 0:D].rearrange("p (h d) -> p h d", d=DH), vb3, ALU.add
                                ).then_inc(sem("vc_done"), 1)

            def maxima(k, s, rounds):
                b = k * 2 + s
                for r in rounds:
                    qt, hp = r // 8, r % 8
                    dve.wait_ge(sem("max_mm"), b * 16 + r + 1)
                    V.tensor_reduce(mx1[:, s, qt, 2 * hp:2 * hp + 2], ps[:, 2 + 2 * (r % 2):4 + 2 * (r % 2), 0:N1], AX.X, ALU.max
                                    ).then_inc(sem("mx_done"), 1)

            def negated_maxima(k, s):
                b = k * 2 + s
                dve.wait_ge(sem("mxt_mm"), b + 1)
                V.tensor_scalar(nmx[:, s, :], bank[0][0:H1, 0:Q], -1.0, None, ALU.mult).then_inc(sem("nmx_done"), 1)

            def normalised(k, s, g):
                b = k * 2 + s
                n = b * 4 + g
                dve.wait_ge(sem("o_mm"), n + 1)
                wait(dve, "aT_done", n)
                V.memset(tick[:], 0.0)
                V.stream_shuffle(ssum[:], bank[7][:, 0:Q], [DH + i % DH for i in range(32)]).then_inc(sem("ssum_done"), 1)
                dve.wait_ge(sem("ssum_done"), n + 1)
                V.reciprocal(rsum[:], ssum[:]).then_inc(sem("rsum_done"), 1)
                dve.wait_ge(sem("rsum_done"), n + 1)
                if g == 0:
                    wait(dve, "y_mm", b)
                V.tensor_tensor(aT[:, g, :], bank[7][:, 0:Q], rsum[:], ALU.mult).then_inc(sem("aT_done"), 1)

            def output(k, s):
                b = k * 2 + s
                dve.wait_ge(sem("y_mm"), b + 1)
                row = [y_sb[:, bass.ds(b * QT + u, 1), :].rearrange("p o d -> p (o d)") for u in range(2)]
                for u in range(2):
                    ins = V.tensor_tensor(row[u], bank[1][:, u * D:(u + 1) * D], x_row(b, u), ALU.add)
                ins.then_inc(sem("y_read"), 1)
                dve.wait_ge(sem("y_read"), b + 1)
                for u in range(2):
                    ins = V.tensor_tensor(row[u], row[u], obb[:], ALU.add)
                ins.then_inc(sem("y_done"), 1)

            def l1_step(k, s, ahead=2):
                one = (k + s, 1 - s)
                two = (k + 1, s)

                def q_k(*parts):
                    if ahead > 1:
                        for p in parts:
                            q_k_copies(*two, p)
                q_k(0)
                normalised(k, s, 0)
                q_k(1, 3)
                normalised(k, s, 1)
                q_k(2, 4)
                normalised(k, s, 2)
                if ahead:
                    maxima(*one, range(2))
                normalised(k, s, 3)
                if ahead > 1:
                    v_copies(*two)
                if ahead:
                    maxima(*one, range(2, 16))
                    negated_maxima(*one)
                output(k, s)

            for s in range(2):
                for p in (0, 1, 2, 3, 4):
                    q_k_copies(0, s, p)
                v_copies(0, s)
            maxima(0, 0, range(16))
            negated_maxima(0, 0)
            for s in range(2):
                l1_step(0, s)
            with dve.Fori(1, B // 2 - 1) as k:
                for s in range(2):
                    l1_step(k, s)
            for s in range(2):
                l1_step(B // 2 - 1, s, ahead=1 - s)
            dve.wait_ge(sem("y_done"), B)
            mlp(1, y_sb, x_sb)


def kernel(**inputs):
    import numpy as np
    import concourse.bacc as bacc
    from concourse.bass_utils import run_bass_kernel_spmd

    v = {k: np.asarray(x) for k, x in inputs.items()}

    def cols(n, width=P):
        return v[n].reshape(-1, width).T

    arrays = {"x": v["x"], "ctxT": v["ctx_2048"].reshape(BT, D).T, "mask": v["mask_BxS2_ik0"]}
    l0 = "L0_xattn_"
    for n in range(LAYERS):
        wq, wk, wv, wo = (v[f"{l0}w{c}{n + 1}"] for c in "qkvo")
        by_head = lambda w: w.reshape(DC, P, H, K).transpose(2, 1, 0, 3).reshape(H, P, DC * K)
        arrays[f"whead{n}"] = np.concatenate(
            [by_head(wk), wq.reshape(D, H, K).transpose(1, 2, 0), by_head(wv), wo.reshape(H, K, D)], axis=2)
        arrays[f"bq{n}"] = v[f"{l0}bq{n + 1}"].reshape(H, K)
    arrays["bkc"] = np.stack([cols(f"{l0}bk{n + 1}") for n in range(LAYERS)], 1)
    arrays["bvc"] = np.stack([cols(f"{l0}bv{n + 1}") for n in range(LAYERS)], 1)
    arrays["biaskc"] = np.stack([cols(f"{l0}bias_k{n + 1}") for n in range(LAYERS)], 1)
    arrays["biasvc"] = np.stack([cols(f"{l0}bias_v{n + 1}") for n in range(LAYERS)], 1)
    arrays["rows16"] = np.stack([np.stack([v[f"{l0}{c}{n + 1}"].reshape(H, K) for c in ("bq", "bk", "bias_k")], 1)
                                 for n in range(LAYERS)], 1)
    arrays["bo"] = np.stack([v[f"{l0}bo{n + 1}"] for n in range(LAYERS)])
    norms = [(v[f"{l0}ln{n}_scale"], v[f"{l0}ln{n}_offset"]) for n in ("1", "2", "_mlp")]
    norms.append((v["L1_xattn_postnorm_w"], np.zeros(D, np.float32)))
    arrays["lnsc"] = np.stack([np.stack([s.reshape(DC, P).T for s in pair], 1) for pair in norms], 1)
    l1 = "L1_xattn_"
    arrays["b1c"] = np.stack([cols(l0 + "b_fc1"), cols(l1 + "mlp_b1")], 1)
    arrays["b2"] = np.stack([v[l0 + "b_fc2"], v[l1 + "mlp_b2"]])
    arrays["w1_0"], arrays["w2_0"] = v[l0 + "w_fc1"], v[l0 + "w_fc2"]
    arrays["w1_1"], arrays["w2_1"] = v[l1 + "mlp_w1"], v[l1 + "mlp_w2"]
    arrays["qw"], arrays["ow"] = v[l1 + "q_w"], v[l1 + "out_w"]
    arrays["kw"], arrays["vw"] = v[l1 + "kv_w"][:, 0::2], v[l1 + "kv_w"][:, 1::2]
    arrays["qbc"] = cols(l1 + "q_b")
    arrays["kbc"] = v[l1 + "kv_b"][0::2].reshape(DC, P).T
    arrays["vb"] = v[l1 + "kv_b"][1::2].reshape(1, D)
    arrays["ob"] = v[l1 + "out_b"].reshape(1, D)
    arrays = {k: np.ascontiguousarray(x) for k, x in arrays.items()}

    nc = bacc.Bacc("TRN2", target_bir_lowering=False, num_devices=1)
    aps = {k: nc.dram_tensor(f"in_{k}", x.shape, mybir.dt.from_np(x.dtype), kind="ExternalInput").ap()
           for k, x in arrays.items()}
    out = nc.dram_tensor("out_0", (B, Q, D), F32, kind="ExternalOutput").ap()
    build_program(nc, aps, out)
    r = run_bass_kernel_spmd(nc, [{f"in_{k}": x for k, x in arrays.items()}], core_ids=[0])
    return r.results[0]["out_0"]
```

```python
from contextlib import ExitStack

import concourse.bass as bass
from concourse import mybir

F32 = mybir.dt.float32
F32R = mybir.dt.float32r
BF16 = mybir.dt.bfloat16
I32 = mybir.dt.int32
ALU = mybir.AluOpType
ACT = mybir.ActivationFunctionType
AX = mybir.AxisListType

P = 128
B, Q, T, D = 8, 256, 64, 256
H, K = 16, 128
DC = D // P
QT = Q // P
NU = B * QT
BT = B * T
T1 = T + 1
HT = H * T1
NG = 4
GC = HT // NG
F = 4 * D
FC = F // P
H1, DH = 16, 16
N1 = Q + T
LAYERS = 2
NPAIR = H // 2
LN_EPS = 1e-5
RMS_EPS = 1e-6
TURN_AFTER = 5
MASKED = -1e30
PRODUCTS = [(0, 0), (0, 1), (1, 0), (1, 1), (0, 2), (2, 0)]
ROW_MASK = len(PRODUCTS) * DH
ROWS_1 = ROW_MASK + 1
ROWS_2 = ROW_MASK + 2


def build_program(nc, a, out):
    with ExitStack() as ctx:
        def sb(name, shape, dt=F32, c=ctx):
            return c.enter_context(nc.sbuf_tensor(name, shape, dt))

        def twins(name, shape, c):
            with ExitStack() as first:
                full = sb(name, shape, c=first)
            return full, sb(name + "_r", shape, F32R, c=c)

        sems = {}

        def sem(name):
            if name not in sems:
                sems[name] = ctx.enter_context(nc.semaphore(name))
            return sems[name]

        ps = ctx.enter_context(nc.psum_tensor("ps", [P, 8, 512], F32))
        bank = [ps[:, i, :] for i in range(8)]

        x_sb = sb("x_sb", [P, NU, D])
        ctxT = sb("ctxT", [P, DC, BT])
        ident = sb("ident", [P, P])
        mhalf = sb("mhalf", [P, 1])
        eps = sb("eps", [P, 2])
        tick = sb("tick", [P, 1])
        stats = sb("stats", [P, 2, 6])
        meanvar = sb("meanvar", [P, 2, 2])
        vareps = sb("vareps", [P, 2, 1])
        rstd = sb("rstd", [P, 2, 1])
        z_sb = sb("z_sb", [P, 4, D])
        lnsc = sb("lnsc", [P, 4, 2, DC])
        b1c = sb("b1c", [P, 2, FC])
        b2bc = sb("b2bc", [P, 2, D])
        stage, stage_r = twins("stage", [P, 2 * FC * D], ctx)

        block = ctx.enter_context(nc.Block())

        regA = ExitStack()
        bkc = sb("bkc", [P, LAYERS, H], c=regA)
        bvc = sb("bvc", [P, LAYERS, H], c=regA)
        biaskc = sb("biaskc", [P, LAYERS, H], c=regA)
        biasvc = sb("biasvc", [P, LAYERS, H], c=regA)
        rows16 = sb("rows16", [H, LAYERS, 3, K], c=regA)
        prod16 = sb("prod16", [H, K], c=regA)
        cconst = sb("cconst", [H, LAYERS, 2], c=regA)
        kT = sb("kT", [P, 2, BT], c=regA)
        vT = sb("vT", [P, 2, BT], c=regA)
        u_sb = sb("u_sb", [P, DC, H], c=regA)
        miscc = sb("miscc", [P, 4, H], c=regA)
        VWb = sb("VWb", [H + 1, D], c=regA)
        c_parts = sb("c_parts", [H, 3, B * T1], BF16, c=regA)
        crow = sb("crow", [3, 2, HT], BF16, c=regA)
        ones3 = sb("ones3", [3, P], BF16, c=regA)
        WK = sb("WK", [P, DC, B, HT], c=regA)
        VW = sb("VW", [P, B, NPAIR, D], c=regA)
        p_sb = sb("p_sb", [P, HT], c=regA)
        pn = sb("pn", [P, HT], c=regA)
        mx = sb("mx", [P, 2, H], c=regA)
        sm = sb("sm", [P, H], c=regA)
        rs = sb("rs", [P, H], c=regA)
        hT = sb("hT", [P, 2, DC, P], c=regA)
        pT = sb("pT", [P, NPAIR, P], c=regA)
        pTb = sb("pTb", [32, P], c=regA)
        regA.close()

        regB = ExitStack()
        y_sb = sb("y_sb", [P, NU, D], c=regB)
        hM, hML = twins("hM", [P, 2, DC, 512], regB)
        gT, gL = twins("gT", [P, 2, FC, 512], regB)
        mlp1w, mlp1w_r = twins("mlp1w", [P, 2 * FC * D], regB)
        qw = sb("qw", [P, DC, D], c=regB)
        kw = sb("kw", [P, DC, D], c=regB)
        vw = sb("vw", [P, DC, D], c=regB)
        ow = sb("ow", [P, DC, D], c=regB)
        qbc = sb("qbc", [P, DC], c=regB)
        kbc = sb("kbc", [P, DC], c=regB)
        vbb = sb("vbb", [P, D], c=regB)
        obb = sb("obb", [P, D], c=regB)
        mask_i = sb("mask_i", [B, T], I32, c=regB)
        mask_f = sb("mask_f", [B, T], c=regB)
        mask_g = sb("mask_g", [B, T], c=regB)
        mask_row = sb("mask_row", [B, N1], BF16, c=regB)
        latT = sb("latT", [P, DC, Q], c=regB)
        ctxd = sb("ctxd", [P, DC, 2, T], c=regB)
        vlat = sb("vlat", [P, 2, 2, H1, 2, DH], c=regB)
        vctx = sb("vctx", [P, 2, H1, 2, DH], c=regB)
        mx1 = sb("mx1", [P, 2, QT, H1], c=regB)
        nmx = sb("nmx", [H1, 2, Q], BF16, c=regB)
        plat = gT[:].rearrange("p s (a i) n -> p s a i n", i=4)[:, 0]
        pctx = sb("pctx", [P, 2, 2, Q], c=regB)
        pv_raw = sb("pv_raw", [P, 4, Q], c=regB)
        rsum = sb("rsum", [P, QT, H1], c=regB)
        attn = sb("attn", [P, QT, D], c=regB)
        aT = sb("aT", [P, DC, Q], c=regB)
        squares = sb("squares", [P, 2, D], c=regB)
        regC = ExitStack()
        Qst = sb("Qst", [ROWS_2, 2, H1, Q], BF16, c=regC)
        Kst = sb("Kst", [ROWS_2, 2, H1, N1], BF16, c=regC)
        proj = sb("proj", [P, 2, DC, N1], c=regC)
        part = sb("part", [P, 2, DC, 3, N1], BF16, c=regC)
        regC.close()
        regD = ExitStack()
        gH = sb("gH", [P, 2, FC, 512], F32R, c=regD)
        hMH = sb("hMH", [P, 2, DC, 512], F32R, c=regD)
        regD.close()
        regB.close()

        qparts = nc.dram_tensor("qparts", (2, DC * P, 3, Q), BF16, kind="Internal").ap()
        kparts = nc.dram_tensor("kparts", (2, DC * P, 3, N1), BF16, kind="Internal").ap()
        mrows = nc.dram_tensor("mrows", (B, N1), BF16, kind="Internal").ap()

        wstage = stage[:].rearrange("p (s n) -> p s n", s=4)

        head_bq = z_sb[:, 2:4, :].rearrange("p u (i k) -> p (u i) k", k=K)

        def wk_h(i, c):
            return wstage[:, i, c * K:(c + 1) * K]

        def wqT_h(i, m):
            return wstage[:, i, 256 + m * P:256 + (m + 1) * P]

        def wv_h(i, c):
            return wstage[:, i, 512 + c * K:512 + (c + 1) * K]

        def wo_h(i, lo=0, hi=D):
            return wstage[:, i, 768 + lo:768 + hi]

        uprod = p_sb[:, 0:DC * K].rearrange("p (c k) -> p c k", c=DC)
        c_sb = pn[0:H, 0:B * T1]
        WK5 = WK[:].rearrange("p m b (h t) -> p m b h t", t=T1)
        weights = (stage[:], mlp1w[:])
        halves = ((mlp1w_r[:], stage_r[:]), (stage_r[:], mlp1w_r[:]))

        def fc1_part(w):
            return w[:, 0:DC * F].rearrange("p (c f) -> p c f", c=DC)

        def fc2_part(w):
            return w[:, DC * F:].rearrange("p (c d) -> p c d", c=FC)

        W_HALF = (slice(0, DC * F), slice(DC * F, 2 * DC * F))

        x_dram = a["x"].rearrange("b (t p) d -> p (b t) d", p=P)
        out_dram = out.rearrange("b (t p) d -> p (b t) d", p=P)

        def unit(layer, k, qt):
            return NU * layer + QT * k + qt + 1

        def wait(eng, s, value):
            if isinstance(value, int) and value <= 0:
                return
            eng.wait_ge(sem(s), value)

        @block.sync
        def _(sp):
            sp.dma_start(ctxT[:], a["ctxT"].rearrange("(c p) n -> p c n", p=P)).then_inc(sem("ctx_in"), 16)

            def small_loads():
                for dst, src in (
                    [(lnsc[:], a["lnsc"])]
                    + [(b1c[:], a["b1c"]), (bkc[:], a["bkc"]), (bvc[:], a["bvc"]),
                       (biaskc[:], a["biaskc"]), (biasvc[:], a["biasvc"]), (rows16[:], a["rows16"])]
                    + [(b2bc[:, i, :], a["b2"][i:i + 1, :].partition_broadcast(P)) for i in range(2)]
                ):
                    sp.dma_start(dst, src).then_inc(sem("small_in"), 16)

            def known(value):
                return value if isinstance(value, int) else sp.snap(sp.to_reg(value))

            def settle():
                sp.wait_ge(sem("ctx_in"), 16)

            def load_heads(layer, j2, e):
                n = NPAIR * layer + j2 * 2 + e
                folded, summed = known(4 * (n - 1)), known(2 * (n - 1))
                for i in range(2):
                    head = known((j2 * 2 + e) * 2 + i)
                    slot = 2 * e + i
                    wait(sp, "vfold_mm", folded)
                    wait(sp, "usum_done", summed)
                    settle()
                    sp.dma_start(wstage[:, slot, :], a[f"whead{layer}"][bass.ds(head, 1)].rearrange("o p n -> p (o n)")
                                 ).then_inc(sem(f"w_in{slot}"), 16)
                    sp.dma_start(head_bq[:, slot, :], a[f"bq{layer}"][bass.ds(head, 1), :].partition_broadcast(P)
                                 ).then_inc(sem(f"w_in{slot}"), 16)

            def attention_loads(layer):
                def c_rows(k):
                    for s in range(2):
                        through, b = known(NU * layer + QT * (k * 2 + s - 1)), known(k * 2 + s)
                        wait(sp, "logit_mm", through)
                        settle()
                        for j in range(3):
                            sp.dma_start(
                                crow[j:j + 1, s, :].rearrange("o (h t) -> o h t", t=T1),
                                c_parts[:, j, :].rearrange("h (b t) -> h b t", t=T1)[:, bass.ds(b, 1), :].rearrange("h o t -> h (o t)")
                            ).then_inc(sem(f"crow_in{s}"), 16)
                sp.wait_ge(sem("cparts_done"), layer + 1)
                c_rows(0)
                with sp.Fori(1, B // 2) as k:
                    c_rows(k)

            for layer in range(LAYERS):
                load_heads(layer, 0, 0)
                if layer == 0:
                    small_loads()
                load_heads(layer, 0, 1)
                if layer == 0:
                    sp.dma_start(x_sb[:], x_dram).then_inc(sem("x_in"), 16)
                wait(sp, "av_mm", NU * layer)
                sp.dma_start(VWb[H:H + 1, :], a["bo"][layer:layer + 1, :]).then_inc(sem("bo_in"), 16)
                with sp.Fori(1, NPAIR // 2) as j2:
                    for e in range(2):
                        load_heads(layer, j2, e)
                attention_loads(layer)

            sp.wait_ge(sem("vfold_mm"), 4 * NPAIR * LAYERS)
            sp.wait_ge(sem("usum_done"), 2 * NPAIR * LAYERS)

            def mlp_loads(n):
                w1, w2 = fc1_part(weights[n]), fc2_part(weights[n])
                sp.dma_start(w1, a[f"w1_{n}"].rearrange("(c p) f -> p c f", p=P)).then_inc(sem(f"mlpw_in{n}"), 16)
                sp.dma_start(w2, a[f"w2_{n}"].rearrange("(c p) d -> p c d", p=P)).then_inc(sem(f"mlpw_in{n}"), 16)

            mlp_loads(0)
            sp.wait_ge(sem("av_mm"), NU * LAYERS)
            sp.wait_ge(sem("logit_mm"), NU * LAYERS)
            sp.wait_ge(sem("resid_done"), NU * LAYERS)
            loads = [(mask_i[:], a["mask"]),
                     (qw[:], a["qw"].rearrange("(c p) n -> p c n", p=P)),
                     (kw[:], a["kw"].rearrange("(c p) n -> p c n", p=P)),
                     (vw[:], a["vw"].rearrange("(c p) n -> p c n", p=P)),
                     (qbc[:], a["qbc"]), (kbc[:], a["kbc"]),
                     (vbb[:], a["vb"][0:1, :].partition_broadcast(P)),
                     (obb[:], a["ob"][0:1, :].partition_broadcast(P)),
                     (ow[:], a["ow"].rearrange("(c p) n -> p c n", p=P))]
            for dst, src in loads:
                sp.dma_start(dst, src).then_inc(sem("l1w_in"), 16)
            sp.wait_ge(sem("mask_done"), 1)
            sp.dma_start(mrows, mask_row[:]).then_inc(sem("mrows_out"), 16)
            sp.wait_ge(sem("mrows_out"), 16)

            def parts_out(k, s):
                b = k * 2 + s
                made, stacked = known(b + 1), known(k * 16 * 13)
                sp.wait_ge(sem("qpart_done"), made)
                sp.wait_ge(sem("kpart_done"), made)
                wait(sp, f"stack_in{s}", stacked)
                for m in range(DC):
                    sp.dma_start(qparts[s, m * P:(m + 1) * P], part[:, 0, m, :, 0:Q]).then_inc(sem("parts_out"), 16)
                    sp.dma_start(kparts[s, m * P:(m + 1) * P], part[:, 1, m, :, :]).then_inc(sem("parts_out"), 16)

            def stack_in(k, s):
                b = k * 2 + s
                early = isinstance(b, int) and b < 2
                lats, ctxs = (0, 0) if early else (known((b - 1) * 8), known((b - 1) * 4))
                written = known((b + 1) * 64)
                b = known(b)
                sp.wait_ge(sem("parts_out"), written)
                wait(sp, "lat_mm", lats)
                wait(sp, "ctxp_mm", ctxs)
                settle()
                for j, (jq, jk) in enumerate(PRODUCTS):
                    rows = slice(j * DH, (j + 1) * DH)
                    sp.dma_start(Qst[rows, s, :, :], qparts[s].rearrange("(h d) j q -> d h j q", d=DH)[:, :, jq, :]
                                 ).then_inc(sem(f"stack_in{s}"), 16)
                    sp.dma_start(Kst[rows, s, :, :], kparts[s].rearrange("(h d) j q -> d h j q", d=DH)[:, :, jk, :]
                                 ).then_inc(sem(f"stack_in{s}"), 16)
                sp.dma_start(Kst[ROW_MASK:ROW_MASK + 1, s, :, :],
                             mrows[bass.ds(b, 1), :].unsqueeze(1).broadcast_to([1, H1, N1])).then_inc(sem(f"stack_in{s}"), 16)

            def max_in(k, s):
                made = known(k * 2 + s + 1)
                sp.wait_ge(sem("nmx_done"), made)
                sp.dma_start(Qst[ROWS_1:ROWS_2, s, :, :], nmx[:, s, :]).then_inc(sem(f"nmx_in{s}"), 16)

            def l1_loads(k, last=False):
                for s in range(2):
                    if not last:
                        parts_out(k + 1, s)
                    if not (last and s == 1):
                        max_in(k + s, 1 - s)
                    if not last:
                        stack_in(k + 1, s)

            sp.wait_ge(sem("ones_done"), 4)
            for s in range(2):
                parts_out(0, s)
                stack_in(0, s)
            max_in(0, 0)
            mlp_loads(1)
            l1_loads(0)
            with sp.Fori(1, B // 2 - 1) as k:
                l1_loads(k)
            l1_loads(B // 2 - 1, last=True)

            for n in range(4):
                sp.wait_ge(sem("fc2_done"), 16 + 4 * (n + 1))
                sp.dma_start(out_dram[:, 4 * n:4 * n + 4, :], x_sb[:, 4 * n:4 * n + 4, :]).then_inc(sem("out_done"), 16)
            sp.wait_ge(sem("out_done"), 64)

        @block.gpsimd
        def _(pool):
            nc.gpsimd.memset(ident[:], 0.0).then_inc(sem("ident_zero"), 1)
            nc.gpsimd.memset(mhalf[:], -0.5)
            nc.gpsimd.memset(ones3[:], 1.0)
            nc.gpsimd.memset(eps[:, 0:1], LN_EPS)
            nc.gpsimd.memset(eps[:, 1:2], RMS_EPS)
            nc.gpsimd.memset(pTb[:], 1.0).then_inc(sem("pool_const"), 1)
            pool.wait_ge(sem("ident_zero"), 1)
            nc.gpsimd.affine_select(out=ident[:], in_=ident[:], compare_op=ALU.not_equal, fill=1.0, base=0,
                                    pattern=[[-1, P]], channel_multiplier=1).then_inc(sem("ident_done"), 1)

            def root(n, s, e):
                pool.wait_ge(sem("var_done"), n)
                nc.gpsimd.tensor_tensor(vareps[:, s, :], meanvar[:, s, 1:2], eps[:, e:e + 1], ALU.add
                                        ).then_inc(sem("vareps_done"), 1)
                pool.wait_ge(sem("vareps_done"), n)
                nc.gpsimd.tensor_tensor(rstd[:, s, :], vareps[:, s, :], mhalf[:], ALU.pow).then_inc(sem("rstd_done"), 1)

            pool.wait_ge(sem("pool_const"), 1)
            with pool.Fori(0, (LAYERS + 1) * NU // 2) as k:
                for s in range(2):
                    root(k * 2 + s + 1, s, 0)
            pool.wait_ge(sem("av_mm"), NU * LAYERS)
            pool.wait_ge(sem("logit_mm"), NU * LAYERS)
            pool.wait_ge(sem("resid_done"), NU * LAYERS)
            nc.gpsimd.memset(mask_row[:], 0.0).then_inc(sem("row_zero"), 1)
            pool.wait_ge(sem("row_zero"), 1)
            def ctx_copy(b):
                wait(pool, "v_mm", b)
                for r in range(2):
                    last = nc.gpsimd.tensor_copy(ctxd[:, :, r, :], ctxT[:, :, bass.ds(b * T, T)])
                last.then_inc(sem("ctxd_done"), 1)
            ctx_copy(0)
            ones = (vlat[:], vctx[:], Qst[ROW_MASK:ROWS_2], Kst[ROW_MASK:ROWS_2])
            for n, t in enumerate(ones):
                if n == 2:
                    pool.wait_ge(sem("fc2_mm"), 16)
                nc.gpsimd.memset(t, 1.0).then_inc(sem("ones_done"), 1)
                pool.wait_ge(sem("ones_done"), n + 1)

            with pool.Fori(1, B) as b:
                ctx_copy(b)
            with pool.Fori((LAYERS + 1) * NU // 2, (LAYERS + 2) * NU // 2) as k:
                for s in range(2):
                    root(k * 2 + s + 1, s, 1)

        @block.tensor
        def _(pe):
            def mm(o, w, r, start=True, stop=True):
                return pe.matmul(o, w, r, start=start, stop=stop)

            pe.wait_ge(sem("ctx_in"), 16)
            pe.wait_ge(sem("ident_done"), 1)

            def kv_products(layer, j2, e, i):
                j = j2 * 2 + e
                g = 2 * (NPAIR * layer + j) + i
                slot = 2 * e + i
                pe.wait_ge(sem(f"w_in{slot}"), 32 * (NPAIR // 2 * layer + j2) + 32)
                wait(pe, "kT_done", g)
                for c in range(DC):
                    ins = mm(bank[0], wk_h(slot, c), ctxT[:, c, :], c == 0, c == DC - 1)
                ins.then_inc(sem("k_mm"), 1)
                wait(pe, "vT_done", g)
                for c in range(DC):
                    ins = mm(bank[1], wv_h(slot, c), ctxT[:, c, :], c == 0, c == DC - 1)
                ins.then_inc(sem("v0_mm"), 1)

            def kv_pair(layer, j2, e, first=False, last=False):
                j = j2 * 2 + e
                n = NPAIR * layer + j
                for i in range(2):
                    g = 2 * n + i
                    slot = 2 * e + i
                    if not (first and i == 0):
                        kv_products(layer, j2, e, i)
                    wait(pe, "misc_done", g)
                    for m in range(DC):
                        mm(bank[4][:, m:m + 1], wqT_h(slot, m), biaskc[:, layer, bass.ds(j * 2 + i, 1)])
                    for m in range(DC):
                        ins = mm(bank[4][:, 2 + m:3 + m], wo_h(slot, m * P, (m + 1) * P), biasvc[:, layer, bass.ds(j * 2 + i, 1)])
                    ins.then_inc(sem("misc_mm"), 1)
                    wait(pe, "kT_done", g + 1)
                    wait(pe, "wk_done", g)
                    for m in range(DC):
                        ins = mm(bank[2 + m], wqT_h(slot, m), kT[:, i, :])
                    ins.then_inc(sem("kfold_mm"), 1)
                if last:
                    c_row(layer)
                pe.wait_ge(sem("vT_done"), 2 * n + 2)
                for q in range(4):
                    wait(pe, "vw_done", 4 * n + (1 if q == 3 else 0))
                    for c in range(2):
                        b = 2 * q + c
                        for i in range(2):
                            ins = mm(bank[(5, 6, 7, 5)[q]][64 * i:64 * i + 64, c * D:(c + 1) * D],
                                     vT[:, i, b * T:(b + 1) * T], wo_h(2 * e + i))
                    ins.then_inc(sem("vfold_mm"), 1)

            def c_row(layer):
                n = 2 * NPAIR * (layer + 1)
                pe.wait_ge(sem("usum_done"), n)
                pe.wait_ge(sem("kT_done"), n)
                for c in range(DC):
                    ins = mm(bank[0][0:H, :], u_sb[:, c, :], ctxT[:, c, :], c == 0, c == DC - 1)
                ins.then_inc(sem("c_mm"), 1)
                pe.wait_ge(sem("misc_done"), n)
                for m in range(DC):
                    ins = pe.transpose(bank[4][0:H, m * P:(m + 1) * P], miscc[:, 2 + m, :], ident[:])
                ins.then_inc(sem("vwb_mm"), 1)

            def turn_h(layer, k, qt):
                n = unit(layer, k, qt)
                pe.wait_ge(sem("z_done"), n)
                wait(pe, "hT_done", n - 1)
                for m in range(DC):
                    ins = pe.transpose(bank[6][:, m * P:(m + 1) * P], z_sb[:, qt, m * P:(m + 1) * P], ident[:])
                ins.then_inc(sem("h_mm"), 1)

            def att_unit(layer, k2, s, qt, first=False, last=False):
                b = k2 * 2 + s
                n = unit(layer, b, qt)
                pe.wait_ge(sem("hT_done"), n)
                wait(pe, "sub_done", n - 1)
                for g in range(NG):
                    cols = slice(g * GC, (g + 1) * GC)
                    for m in range(DC):
                        mm(bank[g][:, 0:GC], hT[:, qt, m, :], WK[:, m, bass.ds(b, 1), cols].rearrange("p o n -> p (o n)"), m == 0, False)
                pqt = 1 - qt
                pb = b if qt == 1 else b - 1
                if not first:
                    turn_p(layer, pb, pqt)
                if qt == 0:
                    pe.wait_ge(sem(f"crow_in{s}"), 48 * (B // 2 * layer + k2 + 1))
                for g in range(NG):
                    cols = slice(g * GC, (g + 1) * GC)
                    ins = mm(bank[g][:, 0:GC], ones3[:], crow[:, s, cols], False, True)
                ins.then_inc(sem("logit_mm"), 1)
                if not last:
                    turn_h(layer, b + (qt == 1), 1 - qt)
                if not first:
                    pv(layer, pb, pqt)

            def turn_p(layer, b, qt):
                n = unit(layer, b, qt)
                pe.wait_ge(sem("pn_done"), n)
                wait(pe, "resid_done", n - 1)
                pe.transpose(bank[7][0:H, D:D + P], pn[:, NPAIR * P:], ident[:])
                for j in range(NPAIR):
                    ins = pe.transpose(bank[4 + j // 4][:, (j % 4) * P:(j % 4 + 1) * P], pn[:, j * P:(j + 1) * P], ident[:])
                    if j % 4 == 3:
                        ins.then_inc(sem("p_mm"), 1)

            def pv(layer, b, qt):
                n = unit(layer, b, qt)
                for j in range(NPAIR):
                    if j % 4 == 0:
                        pe.wait_ge(sem("pT_done"), 2 * (n - 1) + j // 4 + 1)
                    mm(bank[7][:, 0:D], pT[:, j, :], VW[:, bass.ds(b, 1), j, :].rearrange("p o d -> p (o d)"), j == 0, False)
                mm(bank[7][:, 0:D], pTb[0:H + 1, :], VWb[:], False, True).then_inc(sem("av_mm"), 1)

            for layer in range(LAYERS):
                if not layer:
                    kv_products(0, 0, 0, 0)
                    pe.wait_ge(sem("small_in"), 16 * 9)
                else:
                    pe.wait_ge(sem("pT_done"), 2 * NU * layer)
                    pe.wait_ge(sem("hT_done"), NU * layer)
                    pe.wait_ge(sem("resid_done"), NU * layer)
                    pe.wait_ge(sem("c_done"), layer)
                    pe.wait_ge(sem("vwb_done"), layer)
                for e in range(2):
                    kv_pair(layer, 0, e, first=(e == 0))
                with pe.Fori(1, NPAIR // 2 - 1) as j2:
                    for e in range(2):
                        kv_pair(layer, j2, e)
                for e in range(2):
                    kv_pair(layer, NPAIR // 2 - 1, e, last=(e == 1))
                pe.wait_ge(sem("vw_done"), 4 * NPAIR * (layer + 1) - 2)
                turn_h(layer, 0, 0)
                pe.wait_ge(sem("c_done"), layer + 1)
                pe.wait_ge(sem("vT_done"), H * (layer + 1))
                pe.wait_ge(sem("wk_done"), H * (layer + 1))
                pe.wait_ge(sem("vw_done"), 4 * NPAIR * (layer + 1))
                pe.wait_ge(sem("vwb_done"), layer + 1)
                pe.wait_ge(sem("wkb_done"), layer + 1)
                pe.wait_ge(sem("bo_in"), 16 * (layer + 1))
                for s in range(2):
                    for qt in range(QT):
                        att_unit(layer, 0, s, qt, first=(s == 0 and qt == 0))
                with pe.Fori(1, B // 2 - 1) as k2:
                    for s in range(2):
                        for qt in range(QT):
                            att_unit(layer, k2, s, qt)
                for s in range(2):
                    for qt in range(QT):
                        att_unit(layer, B // 2 - 1, s, qt, last=(s == 1 and qt == 1))
                if layer < LAYERS - 1:
                    pe.wait_ge(sem("sub_done"), NU * (layer + 1))
                    pe.wait_ge(sem("c_done"), layer + 1)
                    kv_products(layer + 1, 0, 0, 0)
                turn_p(layer, B - 1, 1)
                pv(layer, B - 1, 1)

            def nothing():
                pass

            def mlp(n, between=nothing):
                w_high, w_low = halves[n]
                u0 = NU * (LAYERS + n)

                def turn(t):
                    wait(pe, "hM_done", 2 * (4 * n + t))
                    for i in range(4):
                        pe.wait_ge(sem("z_done"), u0 + 4 * t + i + 1)
                        for m in range(DC):
                            ins = pe.transpose(bank[6 + m][:, i * P:(i + 1) * P], z_sb[:, i, m * P:(m + 1) * P], ident[:])
                        ins.then_inc(sem("h_mm"), 1)

                def fc1(t):
                    pe.wait_ge(sem("hL_done"), 2 * (4 * n + t + 1))
                    pe.wait_ge(sem("w_low_done"), 2 * n + 1)
                    passes = ((w_high, hMH), (w_high, hML), (w_low, hMH))
                    for f in range(FC):
                        g = FC * (4 * n + t) + f
                        wait(pe, "gelu_done", g - 3)
                        for m in range(DC):
                            for j, (w, h) in enumerate(passes):
                                ins = mm(bank[2 + f % 4], fc1_part(w)[:, m, f * P:(f + 1) * P], h[:, t % 2, m, :],
                                         m == 0 and j == 0, m == DC - 1 and j == 2)
                        ins.then_inc(sem("fc1_mm"), 1)
                        if t < 3 and f == TURN_AFTER:
                            turn(t + 1)

                def fc2(t):
                    if n == 1 and t == 0:
                        pe.wait_ge(sem("y_read"), B)
                    pe.wait_ge(sem("w_low_done"), 2 * n + 2)
                    passes = ((gH, w_high), (gL, w_high), (gH, w_low))
                    for i in range(4):
                        r = 4 * (4 * n + t) + i
                        wait(pe, "fc2_done", r - 1)
                        for f in range(FC):
                            if i == 0:
                                pe.wait_ge(sem("gL_done"), FC * (4 * n + t) + f + 1)
                            for j, (g, w) in enumerate(passes):
                                ins = mm(bank[i % 2][:, 0:D], g[:, t % 2, f, i * P:(i + 1) * P], fc2_part(w)[:, f, :],
                                         f == 0 and j == 0, f == FC - 1 and j == 2)
                        ins.then_inc(sem("fc2_mm"), 1)

                turn(0)
                between()
                fc1(0)
                for t in range(1, 4):
                    fc1(t)
                    fc2(t - 1)
                fc2(3)

            pe.wait_ge(sem("sub_done"), NU * LAYERS)
            pe.wait_ge(sem("pT_done"), 2 * NU * LAYERS)
            pe.wait_ge(sem("hT_done"), NU * LAYERS)
            pe.wait_ge(sem("resid_done"), NU * LAYERS)
            mlp(0)

            def known_int(b, limit):
                return isinstance(b, int) and b < limit

            def latents(k, s):
                b = k * 2 + s
                pe.wait_ge(sem("xlat_done"), b + 1)
                if not known_int(b, 3):
                    pe.wait_ge(sem("attn_done"), b - 2)
                elif b:
                    pe.wait_ge(sem("vc_done"), b)
                for u in range(2):
                    for m in range(DC):
                        ins = pe.transpose(bank[1][:, m * Q + u * P:m * Q + (u + 1) * P], z_sb[:, u, m * P:(m + 1) * P], ident[:])
                ins.then_inc(sem("lat_t_mm"), 1)

            def q_product(k, s, between=nothing):
                b = k * 2 + s
                pe.wait_ge(sem("latT_done"), b + 1)
                for m in range(DC):
                    for c in range(DC):
                        ins = mm(bank[1][:, m * Q:(m + 1) * Q], qw[:, c, m * P:(m + 1) * P], latT[:, c, :], c == 0, c == DC - 1)
                        if (m, c) == (DC - 1, DC - 1):
                            ins.then_inc(sem("q_mm"), 1)
                        between()

            def k_product(k, s, between=nothing):
                b = k * 2 + s
                if not known_int(b, 3):
                    pe.wait_ge(sem("aT_done"), b - 2)
                elif b:
                    pe.wait_ge(sem("vl_done"), b)
                for m in range(DC):
                    if m:
                        pe.wait_ge(sem("q_read"), b + 1)
                    for c in range(DC):
                        mm(bank[m][:, 0:Q], kw[:, c, m * P:(m + 1) * P], latT[:, c, :], c == 0, c == DC - 1)
                        between()
                    for c in range(DC):
                        ins = mm(bank[m][:, Q:N1], kw[:, c, m * P:(m + 1) * P], ctxT[:, c, bass.ds(b * T, T)], c == 0, c == DC - 1)
                    ins.then_inc(sem("kk_mm"), 1)

            def v_latents(k, s):
                b = k * 2 + s
                pe.wait_ge(sem("k_read"), 2 * b + 1)
                wait(pe, "nmx_done", b)
                for u in range(2):
                    for c in range(DC):
                        ins = mm(bank[0][:, u * D:(u + 1) * D], latT[:, c, u * P:(u + 1) * P], vw[:, c, :], c == 0, c == DC - 1)
                ins.then_inc(sem("vl_mm"), 1)

            def v_context(k, s):
                b = k * 2 + s
                pe.wait_ge(sem("k_read"), 2 * b + 2)
                pe.wait_ge(sem("ctxd_done"), b + 1)
                for c in range(DC):
                    ins = mm(bank[1][:, 0:D], ctxd[:, c, :, :].rearrange("p r t -> p (r t)"), vw[:, c, :], c == 0, c == DC - 1)
                ins.then_inc(sem("v_mm"), 1)

            def max_rounds(k, s, first, end):
                b = k * 2 + s
                for r in range(first, end):
                    qt, h = r // H1, r % H1
                    if r == 0:
                        pe.wait_ge(sem(f"stack_in{s}"), k * (16 * 13) + 16 * 13)
                    wait(pe, "mx_done", b * 32 + r - 1)
                    mm(bank[4 + r % 2][:, 0:N1], Qst[0:ROWS_1, s, h, qt * P:(qt + 1) * P], Kst[0:ROWS_1, s, h, :]
                       ).then_inc(sem("max_mm"), 1)

            def turn_max(k, s):
                b = k * 2 + s
                pe.wait_ge(sem("mx_done"), b * 32 + 32)
                if known_int(b, 2):
                    pe.wait_ge(sem("k_read"), 2 * b + 3)
                else:
                    pe.wait_ge(sem("y_read"), b - 1)
                for qt in range(QT):
                    ins = pe.transpose(bank[0][0:H1, qt * P:(qt + 1) * P], mx1[:, s, qt, :], ident[:])
                ins.then_inc(sem("mxt_mm"), 1)

            def second_context(k, s, g):
                b = k * 2 + s
                if g == 0:
                    pe.wait_ge(sem(f"nmx_in{s}"), k * 16 + 16)
                wait(pe, "pctx_done", b * 4 + g)
                for i in range(4):
                    h = 4 * g + i
                    ins = mm(bank[6][64 * (i % 2):64 * (i % 2) + 64, (i // 2) * Q:(i // 2 + 1) * Q],
                             Kst[0:ROWS_2, s, h, Q:N1], Qst[0:ROWS_2, s, h, :])
                ins.then_inc(sem("ctxp_mm"), 1)

            def second_latents(k, s, g, e):
                b = k * 2 + s
                wait(pe, "plat_done", b * 8 + 2 * g + e)
                for i in range(2):
                    h = 4 * g + 2 * e + i
                    for c in range(2):
                        ins = mm(bank[2 + i][:, c * Q:(c + 1) * Q], Kst[0:ROWS_2, s, h, c * P:(c + 1) * P], Qst[0:ROWS_2, s, h, :])
                ins.then_inc(sem("lat_mm"), 1)

            def values_product(k, s, g, between=nothing):
                b = k * 2 + s
                pe.wait_ge(sem("vc_done"), b + 1)
                pe.wait_ge(sem("plat_done"), b * 8 + 2 * g + 2)
                pe.wait_ge(sem("pctx_done"), b * 4 + g + 1)
                wait(pe, "raw_done", b * 4 + g)
                o = [bank[7][32 * i:32 * i + 32, 0:Q] for i in range(4)]
                for c in range(2):
                    for i in range(4):
                        h = 4 * g + i
                        mm(o[i], vlat[:, s, c, h, :, :].rearrange("p r d -> p (r d)"), plat[:, g % 2, i, c * Q:(c + 1) * Q], c == 0, False)
                    between()
                for i in range(4):
                    h = 4 * g + i
                    rows = slice(64 * (i % 2), 64 * (i % 2) + 64)
                    ins = mm(o[i], vctx[rows, s, h, :, :].rearrange("p r d -> p (r d)"), pctx[rows, g % 2, i // 2, :], False, True)
                ins.then_inc(sem("o_mm"), 1)
                between()

            def turn_pv(b):
                pe.wait_ge(sem("raw_done"), b * 4 + 4)
                near_end = isinstance(b, int)
                pe.wait_ge(sem("nmx_done"), min(b + 2, B) if near_end else b + 2)
                pe.wait_ge(sem("vl_done"), min(b + 3, B) if near_end else b + 3)
                pe.wait_ge(sem("vc_done"), min(b + 3, B) if near_end else b + 3)
                wait(pe, "y_read", b)
                for u in range(2):
                    for g in range(4):
                        ins = pe.transpose(bank[u][:, g * P:(g + 1) * P], pv_raw[:, g, u * P:(u + 1) * P], ident[:])
                ins.then_inc(sem("pv_turned"), 1)

            def turn_attn(b):
                pe.wait_ge(sem("attn_done"), b + 1)
                for c in range(DC):
                    for u in range(2):
                        ins = pe.transpose(bank[0][:, c * Q + u * P:c * Q + (u + 1) * P], attn[:, u, c * P:(c + 1) * P], ident[:])
                ins.then_inc(sem("attn_turned"), 1)

            def out_product(b, u, between=nothing):
                pe.wait_ge(sem("aT_done"), b + 1)
                if not (isinstance(b, int) and b + 3 >= B):
                    pe.wait_ge(sem("k_read"), 2 * b + 7)
                for c in range(DC):
                    ins = mm(bank[0][:, u * D:(u + 1) * D], aT[:, c, u * P:(u + 1) * P], ow[:, c, :], c == 0, c == DC - 1)
                    if (u, c) == (1, DC - 1):
                        ins.then_inc(sem("y_mm"), 1)
                    between()

            def l1_step(k, s, ahead=2, behind=True):
                one = (k + s, 1 - s)
                two = (k + 1, s)
                before = k * 2 + s - 1

                taken = [0]

                def maxima(rounds=1):
                    if ahead:
                        end = min(taken[0] + rounds, 32)
                        max_rounds(*one, taken[0], end)
                        taken[0] = end

                if ahead:
                    v_latents(*one)
                    v_context(*one)
                second_context(k, s, 0)
                second_latents(k, s, 0, 0)
                if behind:
                    turn_pv(before)
                second_latents(k, s, 0, 1)
                second_context(k, s, 1)
                if ahead > 1:
                    latents(*two)
                if behind:
                    turn_attn(before)
                if ahead > 1:
                    q_product(*two)
                maxima(2)
                second_latents(k, s, 1, 0)
                maxima()
                values_product(k, s, 0, maxima)
                second_latents(k, s, 1, 1)
                maxima()
                if ahead > 1:
                    k_product(*two, maxima)
                second_latents(k, s, 2, 0)
                maxima(2)
                second_context(k, s, 2)
                maxima()
                values_product(k, s, 1, maxima)
                second_latents(k, s, 2, 1)
                maxima(2)
                second_context(k, s, 3)
                maxima()
                if behind:
                    out_product(before, 0, maxima)
                second_latents(k, s, 3, 0)
                maxima(2)
                if behind:
                    out_product(before, 1, maxima)
                second_latents(k, s, 3, 1)
                maxima(2)
                values_product(k, s, 2, maxima)
                maxima(32)
                if ahead:
                    turn_max(*one)
                values_product(k, s, 3)

            pe.wait_ge(sem("gelu_done"), FC * 4)
            pe.wait_ge(sem("hM_done"), 8)
            pe.wait_ge(sem("fc2_done"), 16)
            pe.wait_ge(sem("l1w_in"), 16 * 9)
            for s in range(2):
                latents(0, s)
                q_product(0, s)
                k_product(0, s)
                if s == 0:
                    v_latents(0, 0)
                    v_context(0, 0)
            max_rounds(0, 0, 0, 32)
            turn_max(0, 0)
            for s in range(2):
                l1_step(0, s, behind=(s == 1))
            with pe.Fori(1, B // 2 - 1) as k:
                for s in range(2):
                    l1_step(k, s)
            for s in range(2):
                l1_step(B // 2 - 1, s, ahead=1 - s)
            def last_output():
                turn_attn(B - 1)
                for u in range(2):
                    out_product(B - 1, u)

            turn_pv(B - 1)
            pe.wait_ge(sem("mx_done"), 32 * B)
            pe.wait_ge(sem("plat_done"), 8 * B)
            pe.wait_ge(sem("pctx_done"), 4 * B)
            mlp(1, last_output)

        @block.scalar
        def _(act):
            def kv_biases(layer, j, i):
                n = NPAIR * layer + j
                g = 2 * n + i
                act.wait_ge(sem("k_mm"), g + 1)
                if not (isinstance(g, int) and g < 2):
                    act.wait_ge(sem("kfold_mm"), g - 1)
                nc.scalar.activation(kT[:, i, :], bank[0], ACT.Identity, bias=bkc[:, layer, bass.ds(j * 2 + i, 1)]
                                     ).then_inc(sem("kT_done"), 1)
                act.wait_ge(sem("v0_mm"), g + 1)
                wait(act, "vfold_mm", 4 * n)
                nc.scalar.activation(vT[:, i, :], bank[1], ACT.Identity, bias=bvc[:, layer, bass.ds(j * 2 + i, 1)]
                                     ).then_inc(sem("vT_done"), 1)

            def kv_pair(layer, j, first=False):
                n = NPAIR * layer + j
                for i in range(2):
                    if not (first and i == 0):
                        kv_biases(layer, j, i)
                for q in range(4):
                    act.wait_ge(sem("vfold_mm"), 4 * n + q + 1)
                    nc.scalar.activation(VW[:, 2 * q:2 * q + 2, bass.ds(j, 1), :].rearrange("p b o d -> p b (o d)"),
                                         bank[(5, 6, 7, 5)[q]].rearrange("p (b d) -> p b d", b=2), ACT.Copy
                                         ).then_inc(sem("vw_done"), 1)

            def turned_h(layer, k, qt):
                n = unit(layer, k, qt)
                act.wait_ge(sem("h_mm"), n)
                if not (isinstance(n, int) and n <= 2):
                    act.wait_ge(sem("logit_mm"), n - 2)
                for m in range(DC):
                    ins = nc.scalar.activation(hT[:, qt, m, :], bank[6][:, m * P:(m + 1) * P], ACT.Identity,
                                               bias=lnsc[:, layer, 1, m:m + 1], scale=lnsc[:, layer, 0, m:m + 1])
                ins.then_inc(sem("hT_done"), 1)

            def turned_p(layer, b, qt):
                n = unit(layer, b, qt)
                act.wait_ge(sem("p_mm"), 2 * n - 1)
                wait(act, "av_mm", n - 1)
                nc.scalar.activation(pTb[0:H, :], bank[7][0:H, D:D + P], ACT.Copy)
                nc.scalar.activation(pT[:, 0:4, :], bank[4].rearrange("p (j q) -> p j q", j=4), ACT.Copy
                                     ).then_inc(sem("pT_done"), 1)
                act.wait_ge(sem("p_mm"), 2 * n)
                nc.scalar.activation(pT[:, 4:8, :], bank[5].rearrange("p (j q) -> p j q", j=4), ACT.Copy
                                     ).then_inc(sem("pT_done"), 1)

            def high_weights(n, half):
                act.wait_ge(sem(f"mlpw_in{n}"), 32)
                nc.scalar.activation(halves[n][0][:, W_HALF[half]], weights[n][:, W_HALF[half]], ACT.Copy
                                     ).then_inc(sem("w_high_done"), 1)

            def att_unit(layer, b, qt, first=False, last=False):
                n = unit(layer, b, qt)
                if not first:
                    turned_p(layer, b if qt else b - 1, 1 - qt)
                if not last:
                    turned_h(layer, b + (qt == 1), 1 - qt)
                act.wait_ge(sem("sub_done"), n)
                nc.scalar.activation(p_sb[:], p_sb[:], ACT.Exp, scale=float(K) ** -0.5
                                     ).then_inc(sem("exp_done"), 1)

            act.wait_ge(sem("small_in"), 16 * 9)
            act.wait_ge(sem("pool_const"), 1)
            for layer in range(LAYERS):
                if layer == 0:
                    kv_biases(0, 0, 0)
                kv_pair(layer, 0, first=True)
                with act.Fori(1, NPAIR) as j:
                    kv_pair(layer, j)
                act.wait_ge(sem("vwb_mm"), layer + 1)
                nc.scalar.activation(VWb[0:H, :], bank[4][0:H, 0:D], ACT.Copy).then_inc(sem("vwb_done"), 1)
                turned_h(layer, 0, 0)
                for qt in range(QT):
                    att_unit(layer, 0, qt, first=(qt == 0))
                with act.Fori(1, B - 1) as b:
                    for qt in range(QT):
                        att_unit(layer, b, qt)
                for qt in range(QT):
                    att_unit(layer, B - 1, qt, last=(qt == 1))
                if layer < LAYERS - 1:
                    kv_biases(layer + 1, 0, 0)
                else:
                    act.wait_ge(sem("logit_mm"), NU * LAYERS)
                    high_weights(0, 0)
                turned_p(layer, B - 1, 1)

            def mlp(n, func, between=None):
                def turned(t):
                    u0 = NU * (LAYERS + n)
                    act.wait_ge(sem("h_mm"), u0 + 4 * t + 4)
                    if t >= 2:
                        act.wait_ge(sem("fc1_mm"), FC * (4 * n + t - 1))
                    for m in range(DC):
                        for dst in (hM, hMH):
                            ins = nc.scalar.activation(dst[:, t % 2, m, :], bank[6 + m], ACT.Identity,
                                                       bias=lnsc[:, LAYERS + n, 1, m:m + 1], scale=lnsc[:, LAYERS + n, 0, m:m + 1])
                        ins.then_inc(sem("hM_done"), 1)

                turned(0)
                if n == 0:
                    high_weights(0, 1)
                if between:
                    between()
                for t in range(4):
                    for f in range(FC):
                        act.wait_ge(sem("fc1_mm"), FC * (4 * n + t) + f + 1)
                        if f == 0 and t >= 2:
                            act.wait_ge(sem("fc2_mm"), 4 * (4 * n + t - 1))
                        for dst in (gT, gH):
                            ins = nc.scalar.activation(dst[:, t % 2, f, :], bank[2 + f % 4], func, bias=b1c[:, n, f:f + 1])
                        ins.then_inc(sem("gelu_done"), 1)
                        if t < 3 and f == TURN_AFTER:
                            turned(t + 1)

            act.wait_ge(sem("av_mm"), NU * LAYERS)
            act.wait_ge(sem("logit_mm"), NU * LAYERS)
            act.wait_ge(sem("resid_done"), NU * LAYERS)
            mlp(0, ACT.Gelu)

            def latents(b):
                wait(act, "lat_t_mm", b)
                nc.scalar.activation(z_sb[:, 0:QT, :], x_sb[:, bass.ds(b * QT, QT), :], ACT.Copy).then_inc(sem("xlat_done"), 1)

            def turned_latents(b):
                act.wait_ge(sem("lat_t_mm"), b + 1)
                wait(act, "vl_mm", b)
                nc.scalar.activation(latT[:], bank[1].rearrange("p (c q) -> p c q", c=DC), ACT.Copy
                                     ).then_inc(sem("latT_done"), 1)

            def biased(b, e):
                if e == 0:
                    act.wait_ge(sem("q_mm"), b + 1)
                    wait(act, "parts_out", b * 64)
                    wait(act, "qpart_done", b)
                else:
                    wait(act, "kpart_done", b)
                for m in range(DC):
                    if e == 0:
                        src, bias, width = bank[1][:, m * Q:(m + 1) * Q], qbc[:, m:m + 1], Q
                    else:
                        act.wait_ge(sem("kk_mm"), b * 2 + m + 1)
                        src, bias, width = bank[m][:, 0:N1], kbc[:, m:m + 1], N1
                    nc.scalar.activation(proj[:, e, m, 0:width], src, ACT.Identity, bias=bias)
                    ins = nc.scalar.activation(part[:, e, m, 0, 0:width], src, ACT.Identity, bias=bias)
                    if e == 1:
                        ins.then_inc(sem("k_read"), 1)
                if e == 0:
                    ins.then_inc(sem("q_read"), 1)

            def second_part(b, e):
                act.wait_ge(sem(("q_rest", "k_rest")[e]), b + 1)
                width = (Q, N1)[e]
                nc.scalar.activation(part[:, e, :, 1, 0:width], proj[:, e, :, 0:width], ACT.Copy
                                     ).then_inc(sem(("q_second", "k_second")[e]), 1)

            def turned_attn(b):
                act.wait_ge(sem("attn_turned"), b + 1)
                nc.scalar.activation(aT[:], bank[0].rearrange("p (c q) -> p c q", c=DC), ACT.Copy
                                     ).then_inc(sem("aT_done"), 1)

            def exp_context(b, g):
                act.wait_ge(sem("ctxp_mm"), b * 4 + g + 1)
                if not (isinstance(b, int) and b == 0 and g < 2):
                    act.wait_ge(sem("o_mm"), b * 4 + g - 1)
                nc.scalar.activation(pctx[:, g % 2, :, :], bank[6].rearrange("p (i q) -> p i q", i=2), ACT.Exp,
                                     scale=1.0 / DH).then_inc(sem("pctx_done"), 1)

            def exp_latents(b, g, e):
                act.wait_ge(sem("lat_mm"), b * 8 + 2 * g + e + 1)
                nc.scalar.activation(plat[:, g % 2, 2 * e:2 * e + 2, :], ps[:, 2:4, :], ACT.Exp,
                                     scale=1.0 / DH).then_inc(sem("plat_done"), 1)

            def raw(b, g):
                act.wait_ge(sem("o_mm"), b * 4 + g + 1)
                if g == 0:
                    wait(act, "pv_turned", b)
                nc.scalar.activation(pv_raw[:, g, :], bank[7][:, 0:Q], ACT.Copy).then_inc(sem("raw_done"), 1)

            def l1_step(b, ahead=2, behind=True, latents_left=True):
                exp_context(b, 0)
                exp_latents(b, 0, 0)
                exp_latents(b, 0, 1)
                if ahead > 1:
                    turned_latents(b + 2)
                if behind:
                    turned_attn(b - 1)
                exp_context(b, 1)
                if ahead > 1:
                    biased(b + 2, 0)
                exp_latents(b, 1, 0)
                raw(b, 0)
                if ahead > 1:
                    second_part(b + 2, 0)
                exp_latents(b, 1, 1)
                if ahead > 1:
                    biased(b + 2, 1)
                exp_latents(b, 2, 0)
                exp_context(b, 2)
                raw(b, 1)
                if ahead > 1:
                    second_part(b + 2, 1)
                exp_latents(b, 2, 1)
                if latents_left:
                    latents(b + 3)
                exp_context(b, 3)
                exp_latents(b, 3, 0)
                exp_latents(b, 3, 1)
                raw(b, 2)
                raw(b, 3)

            act.wait_ge(sem("fc2_done"), 16)
            act.wait_ge(sem("l1w_in"), 16 * 9)
            latents(0)
            for b in range(2):
                turned_latents(b)
                latents(b + 1)
                biased(b, 0)
                second_part(b, 0)
                biased(b, 1)
                second_part(b, 1)
            for b in range(2):
                l1_step(b, behind=(b == 1))
            for half in range(2):
                high_weights(1, half)
            with act.Fori(2, B - 3) as b:
                l1_step(b)
            for b in range(B - 3, B):
                l1_step(b, ahead=min(2, B - 1 - b), latents_left=False)
            mlp(1, ACT.Gelu_apprx_tanh, lambda: turned_attn(B - 1))

        @block.vector
        def _(dve):
            V = nc.vector

            def row_stats(n, s, row):
                if not (isinstance(n, int) and n <= 2):
                    dve.wait_ge(sem("z_done"), n - 2)
                V.bn_stats(stats[:, s, :], row).then_inc(sem("stats_done"), 1)
                dve.wait_ge(sem("stats_done"), n)
                V.memset(tick[:], 0.0)
                V.bn_aggr(meanvar[:, s, :], stats[:, s, :]).then_inc(sem("var_done"), 1)

            def row_norm(n, s, row):
                dve.wait_ge(sem("rstd_done"), n)
                if not (isinstance(n, int) and n <= 2):
                    dve.wait_ge(sem("h_mm"), n - 2)
                V.tensor_scalar(z_sb[:, s, :], row, meanvar[:, s, 0:1], rstd[:, s, :], ALU.subtract, ALU.mult
                                ).then_inc(sem("z_done"), 1)

            def x_row(b, qt):
                return x_sb[:, bass.ds(b * QT + qt, 1), :].rearrange("p o d -> p (o d)")

            def kv_pair(layer, j2, e):
                j = j2 * 2 + e
                n = NPAIR * layer + j
                for i in range(2):
                    g = 2 * n + i
                    slot = 2 * e + i
                    dve.wait_ge(sem(f"w_in{slot}"), 32 * (NPAIR // 2 * layer + j2) + 32)
                    wait(dve, "usum_done", g)
                    V.tensor_tensor(uprod, wstage[:, slot, 0:2 * K].rearrange("p (c k) -> p c k", c=DC),
                                    head_bq[:, slot, :].unsqueeze(1).broadcast_to([P, DC, K]), ALU.mult
                                    ).then_inc(sem("uprod_done"), 1)
                    dve.wait_ge(sem("uprod_done"), g + 1)
                    V.tensor_reduce(u_sb[:, :, bass.ds(j * 2 + i, 1)].rearrange("p c o -> p (c o)"), uprod, AX.X, ALU.add
                                    ).then_inc(sem("usum_done"), 1)
                    dve.wait_ge(sem("misc_mm"), g + 1)
                    V.tensor_copy(miscc[:, :, bass.ds(j * 2 + i, 1)].rearrange("p c o -> p (c o)"), bank[4][:, 0:4]
                                  ).then_inc(sem("misc_done"), 1)
                    dve.wait_ge(sem("kfold_mm"), g + 1)
                    for m in range(DC):
                        ins = V.tensor_copy(WK5[:, m, :, bass.ds(j * 2 + i, 1), 0:T].rearrange("p b o t -> p b (o t)"),
                                            bank[2 + m].rearrange("p (b t) -> p b t", b=B))
                    ins.then_inc(sem("wk_done"), 1)

            def bias_products(layer):
                for e in range(2):
                    wait(dve, "prod16_done", 2 * layer + e)
                    V.tensor_tensor(prod16[:], rows16[:, layer, 0, :], rows16[:, layer, 1 + e, :], ALU.mult
                                    ).then_inc(sem("prod_done"), 1)
                    dve.wait_ge(sem("prod_done"), 2 * layer + e + 1)
                    V.tensor_reduce(cconst[:, layer, e:e + 1], prod16[:], AX.X, ALU.add).then_inc(sem("prod16_done"), 1)

            def key_constants(layer):
                dve.wait_ge(sem("prod16_done"), 2 * layer + 2)
                dve.wait_ge(sem("c_mm"), layer + 1)
                c3 = c_sb.rearrange("h (b t) -> h b t", t=T1)
                V.tensor_scalar(c3[:, :, 0:T], bank[0][0:H, :].rearrange("h (b t) -> h b t", t=T),
                                cconst[:, layer, 0:1], None, ALU.add).then_inc(sem("c_done"), 1)
                V.tensor_copy(c3[:, :, T], cconst[:, layer, 1:2].broadcast_to([H, B])).then_inc(sem("csplit_step"), 1)
                dve.wait_ge(sem("misc_done"), H * (layer + 1))
                for m in range(DC):
                    ins = V.tensor_copy(WK5[:, m, :, :, T], miscc[:, m, :].unsqueeze(1).broadcast_to([P, B, H]))
                ins.then_inc(sem("wkb_done"), 1)
                dve.wait_ge(sem("c_done"), layer + 1)
                for j in range(3):
                    n = 6 * layer + 2 * j
                    dve.wait_ge(sem("csplit_step"), n + 1)
                    ins = V.tensor_copy(c_parts[:, j, :], c_sb)
                    if j < 2:
                        ins.then_inc(sem("csplit_step"), 1)
                        dve.wait_ge(sem("csplit_step"), n + 2)
                        V.tensor_tensor(c_sb, c_sb, c_parts[:, j, :], ALU.subtract).then_inc(sem("csplit_step"), 1)
                    else:
                        ins.then_inc(sem("cparts_done"), 1)
                V.tensor_copy(prod16[:, 0:1], cconst[:, layer, 0:1]).then_inc(sem("csplit_step"), 1)

            def residual(layer, b, qt):
                n = unit(layer, b, qt)
                dve.wait_ge(sem("av_mm"), n)
                V.tensor_tensor(x_row(b, qt), bank[7][:, 0:D], x_row(b, qt), ALU.add).then_inc(sem("resid_done"), 1)

            def att_unit(layer, b, qt, first=False, last=False):
                n = unit(layer, b, qt)
                if not last:
                    row_stats(n + 2, qt, x_row(b + 1, qt))
                dve.wait_ge(sem("logit_mm"), n)
                s4 = ps[:, 0:NG, 0:GC].rearrange("p g (h t) -> p g h t", t=T1)
                V.tensor_reduce(mx[:, qt, :].rearrange("p (g h) -> p g h", g=NG), s4, AX.X, ALU.max).then_inc(sem("max_done"), 1)
                dve.wait_ge(sem("max_done"), n)
                wait(dve, "pn_done", n - 1)
                V.tensor_tensor(p_sb[:].rearrange("p (g h t) -> p g h t", g=NG, t=T1), s4,
                                mx[:, qt, :].rearrange("p (g h) -> p g h", g=NG).unsqueeze(3).broadcast_to([P, NG, H // NG, T1]),
                                ALU.subtract).then_inc(sem("sub_done"), 1)
                if not last:
                    row_norm(n + 2, qt, x_row(b + 1, qt))
                dve.wait_ge(sem("exp_done"), n)
                p3 = p_sb[:].rearrange("p (h t) -> p h t", t=T1)
                V.tensor_reduce(sm[:], p3, AX.X, ALU.add).then_inc(sem("sum_done"), 1)
                dve.wait_ge(sem("sum_done"), n)
                V.reciprocal(rs[:], sm[:]).then_inc(sem("rs_done"), 1)
                dve.wait_ge(sem("rs_done"), n)
                wait(dve, "p_mm", 2 * n - 2)
                V.tensor_tensor(pn[:, NPAIR * P:], p3[:, :, T], rs[:], ALU.mult)
                V.tensor_tensor(pn[:, 0:NPAIR * P].rearrange("p (h t) -> p h t", t=T), p3[:, :, 0:T],
                                rs[:].unsqueeze(2).broadcast_to([P, H, T]), ALU.mult).then_inc(sem("pn_done"), 1)
                if not first:
                    residual(layer, b if qt else b - 1, 1 - qt)

            def low_weights(n, half):
                dve.wait_ge(sem("w_high_done"), 2 * n + half + 1)
                V.tensor_tensor(halves[n][1][:, W_HALF[half]], weights[n][:, W_HALF[half]],
                                halves[n][0][:, W_HALF[half]].bitcast(F32), ALU.subtract).then_inc(sem("w_low_done"), 1)

            def norm_rows(n, src, units, between=None):
                def stats_of(i):
                    u = NU * (LAYERS + n) + i + 1
                    if n == 0:
                        row_stats(u, i % 2, src[:, i, :])
                    else:
                        dve.wait_ge(sem("z_done"), u - 2)
                        V.tensor_tensor_reduce(squares[:, i % 2, :], src[:, i, :], src[:, i, :], 1.0 / D, 0.0, ALU.mult, ALU.add,
                                               meanvar[:, i % 2, 1:2]).then_inc(sem("var_done"), 1)

                def rows_of(i):
                    u = NU * (LAYERS + n) + i + 1
                    dve.wait_ge(sem("rstd_done"), u)
                    dve.wait_ge(sem("h_mm"), u - (2 if i < 2 else 4))
                    if n == 0:
                        ins = V.tensor_scalar(z_sb[:, i % 4, :], src[:, i, :], meanvar[:, i % 2, 0:1], rstd[:, i % 2, :],
                                              ALU.subtract, ALU.mult)
                    else:
                        ins = V.tensor_scalar(z_sb[:, i % 4, :], src[:, i, :], rstd[:, i % 2, :], None, ALU.mult)
                    ins.then_inc(sem("z_done"), 1)

                for i in units:
                    stats_of(i)
                    if i > units[0]:
                        rows_of(i - 1)
                        if between:
                            between(i - units[0] - 1)
                rows_of(units[-1])

            dve.wait_ge(sem("small_in"), 16 * 9)
            for layer in range(LAYERS):
                wait(dve, "logit_mm", NU * layer)
                wait(dve, "p_mm", 2 * NU * layer)
                for e in range(2):
                    kv_pair(layer, 0, e)
                bias_products(layer)
                if layer == 0:
                    dve.wait_ge(sem("x_in"), 16)
                wait(dve, "resid_done", NU * layer)
                for qt in range(QT):
                    row_stats(unit(layer, 0, qt), qt, x_row(0, qt))
                    row_norm(unit(layer, 0, qt), qt, x_row(0, qt))
                with dve.Fori(1, NPAIR // 2) as j2:
                    for e in range(2):
                        kv_pair(layer, j2, e)
                if layer:
                    dve.wait_ge(sem("crow_in0"), 48 * (B // 2) * layer)
                    dve.wait_ge(sem("crow_in1"), 48 * (B // 2) * layer)
                key_constants(layer)
                for qt in range(QT):
                    att_unit(layer, 0, qt, first=(qt == 0))
                with dve.Fori(1, B - 1) as b:
                    for qt in range(QT):
                        att_unit(layer, b, qt)
                for qt in range(QT):
                    att_unit(layer, B - 1, qt, last=True)
                if layer == LAYERS - 1:
                    norm_rows(0, x_sb, range(4))
                    low_weights(0, 0)
                residual(layer, B - 1, 1)

            def mlp(n, src, dst, between=None):
                def low_h(t):
                    for m in range(DC):
                        dve.wait_ge(sem("hM_done"), 2 * (4 * n + t) + m + 1)
                        V.tensor_tensor(hML[:, t % 2, m, :], hM[:, t % 2, m, :], hMH[:, t % 2, m, :].bitcast(F32), ALU.subtract
                                        ).then_inc(sem("hL_done"), 1)

                def low_g(t, chunks):
                    for f in chunks:
                        dve.wait_ge(sem("gelu_done"), FC * (4 * n + t) + f + 1)
                        V.tensor_tensor(gL[:, t % 2, f, :], gT[:, t % 2, f, :], gH[:, t % 2, f, :].bitcast(F32), ALU.subtract
                                        ).then_inc(sem("gL_done"), 1)

                def added(t):
                    for i in range(4):
                        u = 4 * t + i
                        r = 4 * (4 * n + t) + i
                        V.tensor_tensor(dst[:, u, :], dst[:, u, :], b2bc[:, n, :], ALU.add).then_inc(sem("bias_done"), 1)
                        dve.wait_ge(sem("bias_done"), r + 1)
                        dve.wait_ge(sem("fc2_mm"), r + 1)
                        ins = V.tensor_tensor(dst[:, u, :], bank[i % 2][:, 0:D], dst[:, u, :], ALU.add)
                        ins.then_inc(sem("fc2_done"), 1)
                low_h(0)
                if n == 0:
                    low_weights(0, 1)
                if between:
                    between()
                for t in range(4):
                    if t < 3:
                        norm_rows(n, src, range(4 * t + 4, 4 * t + 8), lambda i: low_g(t, [i]))
                        low_g(t, range(3, TURN_AFTER + 1))
                        low_h(t + 1)
                        low_g(t, range(TURN_AFTER + 1, FC))
                    else:
                        low_g(t, range(FC))
                    if t:
                        added(t - 1)
                added(3)

            mlp(0, x_sb, x_sb)

            dve.wait_ge(sem("fc2_done"), 16)
            dve.wait_ge(sem("l1w_in"), 16 * 9)
            dve.wait_ge(sem("row_zero"), 1)
            V.tensor_copy(mask_f[:], mask_i[:]).then_inc(sem("mask_step"), 1)
            dve.wait_ge(sem("mask_step"), 1)
            V.tensor_scalar(mask_g[:], mask_f[:], 0.0, MASKED, ALU.is_equal, ALU.mult).then_inc(sem("mask_step"), 1)
            dve.wait_ge(sem("mask_step"), 2)
            V.tensor_copy(mask_row[:, Q:N1], mask_g[:]).then_inc(sem("mask_done"), 1)
            dve.wait_ge(sem("ones_done"), 2)

            def split(k, s, e, step):
                b = k * 2 + s
                rest = proj[:, e, :, 0:(Q, N1)[e]]
                parts = part[:, e, :, :, 0:(Q, N1)[e]]
                if step == 0:
                    dve.wait_ge(sem(("q_read", "k_read")[e]), (b + 1, 2 * b + 2)[e])
                    V.tensor_tensor(rest, rest, parts[:, :, 0, :], ALU.subtract).then_inc(sem(("q_rest", "k_rest")[e]), 1)
                else:
                    dve.wait_ge(sem(("q_second", "k_second")[e]), b + 1)
                    V.tensor_tensor(parts[:, :, 2, :], rest, parts[:, :, 1, :], ALU.subtract
                                    ).then_inc(sem(("qpart_done", "kpart_done")[e]), 1)

            vb3 = vbb[:].rearrange("p (h d) -> p h d", d=DH)

            def v_latents(k, s):
                b = k * 2 + s
                if not (isinstance(b, int) and b < 2):
                    dve.wait_ge(sem("o_mm"), (b - 1) * 4)
                dve.wait_ge(sem("vl_mm"), b + 1)
                for u in range(2):
                    ins = V.tensor_tensor(vlat[:, s, u, :, 0, :], bank[0][:, u * D:(u + 1) * D].rearrange("p (h d) -> p h d", d=DH),
                                          vb3, ALU.add)
                ins.then_inc(sem("vl_done"), 1)

            def v_context(k, s):
                b = k * 2 + s
                if not (isinstance(b, int) and b < 2):
                    dve.wait_ge(sem("o_mm"), (b - 1) * 4)
                dve.wait_ge(sem("v_mm"), b + 1)
                V.tensor_tensor(vctx[:, s, :, 0, :], bank[1][:, 0:D].rearrange("p (h d) -> p h d", d=DH), vb3, ALU.add
                                ).then_inc(sem("vc_done"), 1)

            def max_rounds(k, s, first, end):
                b = k * 2 + s
                for r in range(first, end):
                    qt, h = r // H1, r % H1
                    dve.wait_ge(sem("max_mm"), b * 32 + r + 1)
                    V.tensor_reduce(mx1[:, s, qt, h:h + 1], bank[4 + r % 2][:, 0:N1], AX.X, ALU.max
                                    ).then_inc(sem("mx_done"), 1)

            def negated_maxima(k, s):
                b = k * 2 + s
                dve.wait_ge(sem("mxt_mm"), b + 1)
                V.tensor_scalar(nmx[:, s, :], bank[0][0:H1, 0:Q], -1.0, None, ALU.mult).then_inc(sem("nmx_done"), 1)

            def normalised(b):
                dve.wait_ge(sem("pv_turned"), b + 1)
                heads = ps[:, 0:QT, :].rearrange("p u (h r) -> p u h r", r=2 * DH)
                V.reciprocal(rsum[:], heads[:, :, :, DH]).then_inc(sem("rsum_done"), 1)
                dve.wait_ge(sem("rsum_done"), b + 1)
                V.tensor_tensor(attn[:].rearrange("p u (h d) -> p u h d", d=DH), heads[:, :, :, 0:DH],
                                rsum[:].unsqueeze(3).broadcast_to([P, QT, H1, DH]), ALU.mult).then_inc(sem("attn_done"), 1)

            def y_row(b, u):
                return y_sb[:, bass.ds(b * QT + u, 1), :].rearrange("p o d -> p (o d)")

            def output_bias(b):
                for u in range(2):
                    ins = V.tensor_tensor(y_row(b, u), x_row(b, u), obb[:], ALU.add)
                ins.then_inc(sem("ybias_done"), 1)

            def output(b):
                dve.wait_ge(sem("ybias_done"), b + 1)
                dve.wait_ge(sem("y_mm"), b + 1)
                for u in range(2):
                    ins = V.tensor_tensor(y_row(b, u), bank[0][:, u * D:(u + 1) * D], y_row(b, u), ALU.add)
                ins.then_inc(sem("y_read"), 1)

            def l1_step(k, s, ahead=2, behind=True):
                one = (k + s, 1 - s)
                two = (k + 1, s)
                before = k * 2 + s - 1

                def maxima(first, end):
                    if ahead:
                        max_rounds(*one, first, end)

                if ahead:
                    v_latents(*one)
                    v_context(*one)
                if behind:
                    normalised(before)
                maxima(0, 2)
                if ahead > 1:
                    split(*two, 0, 0)
                maxima(2, 7)
                if ahead > 1:
                    split(*two, 0, 1)
                maxima(7, 14)
                if ahead > 1:
                    split(*two, 1, 0)
                maxima(14, 19)
                if ahead > 1:
                    split(*two, 1, 1)
                maxima(19, 22)
                if behind:
                    output_bias(before)
                maxima(22, 28)
                if behind:
                    output(before)
                maxima(28, 32)
                if ahead:
                    negated_maxima(*one)

            for s in range(2):
                for e in range(2):
                    for step in range(2):
                        split(0, s, e, step)
                if s == 0:
                    v_latents(0, 0)
                    v_context(0, 0)
            max_rounds(0, 0, 0, 32)
            negated_maxima(0, 0)
            for s in range(2):
                l1_step(0, s, behind=(s == 1))
            with dve.Fori(1, B // 2 - 1) as k:
                for s in range(2):
                    l1_step(k, s)
            for s in range(2):
                l1_step(B // 2 - 1, s, ahead=1 - s)
            for half in range(2):
                low_weights(1, half)
            norm_rows(1, y_sb, range(4))
            output_bias(B - 1)
            normalised(B - 1)
            mlp(1, y_sb, x_sb, lambda: output(B - 1))


def kernel(**inputs):
    import numpy as np
    import concourse.bacc as bacc
    from concourse.bass_utils import run_bass_kernel_spmd

    v = {k: np.asarray(x) for k, x in inputs.items()}

    def cols(n, width=P):
        return v[n].reshape(-1, width).T

    arrays = {"x": v["x"], "ctxT": v["ctx_2048"].reshape(BT, D).T, "mask": v["mask_BxS2_ik0"]}
    l0 = "L0_xattn_"
    for n in range(LAYERS):
        wq, wk, wv, wo = (v[f"{l0}w{c}{n + 1}"] for c in "qkvo")
        by_head = lambda w: w.reshape(DC, P, H, K).transpose(2, 1, 0, 3).reshape(H, P, DC * K)
        arrays[f"whead{n}"] = np.concatenate(
            [by_head(wk), wq.reshape(D, H, K).transpose(1, 2, 0), by_head(wv), wo.reshape(H, K, D)], axis=2)
        arrays[f"bq{n}"] = v[f"{l0}bq{n + 1}"].reshape(H, K)
    arrays["bkc"] = np.stack([cols(f"{l0}bk{n + 1}") for n in range(LAYERS)], 1)
    arrays["bvc"] = np.stack([cols(f"{l0}bv{n + 1}") for n in range(LAYERS)], 1)
    arrays["biaskc"] = np.stack([cols(f"{l0}bias_k{n + 1}") for n in range(LAYERS)], 1)
    arrays["biasvc"] = np.stack([cols(f"{l0}bias_v{n + 1}") for n in range(LAYERS)], 1)
    arrays["rows16"] = np.stack([np.stack([v[f"{l0}{c}{n + 1}"].reshape(H, K) for c in ("bq", "bk", "bias_k")], 1)
                                 for n in range(LAYERS)], 1)
    arrays["bo"] = np.stack([v[f"{l0}bo{n + 1}"] for n in range(LAYERS)])
    norms = [(v[f"{l0}ln{n}_scale"], v[f"{l0}ln{n}_offset"]) for n in ("1", "2", "_mlp")]
    norms.append((v["L1_xattn_postnorm_w"], np.zeros(D, np.float32)))
    arrays["lnsc"] = np.stack([np.stack([s.reshape(DC, P).T for s in pair], 1) for pair in norms], 1)
    l1 = "L1_xattn_"
    arrays["b1c"] = np.stack([cols(l0 + "b_fc1"), cols(l1 + "mlp_b1")], 1)
    arrays["b2"] = np.stack([v[l0 + "b_fc2"], v[l1 + "mlp_b2"]])
    arrays["w1_0"], arrays["w2_0"] = v[l0 + "w_fc1"], v[l0 + "w_fc2"]
    arrays["w1_1"], arrays["w2_1"] = v[l1 + "mlp_w1"], v[l1 + "mlp_w2"]
    arrays["qw"], arrays["ow"] = v[l1 + "q_w"], v[l1 + "out_w"]
    arrays["kw"], arrays["vw"] = v[l1 + "kv_w"][:, 0::2], v[l1 + "kv_w"][:, 1::2]
    arrays["qbc"] = cols(l1 + "q_b")
    arrays["kbc"] = v[l1 + "kv_b"][0::2].reshape(DC, P).T
    arrays["vb"] = v[l1 + "kv_b"][1::2].reshape(1, D)
    arrays["ob"] = v[l1 + "out_b"].reshape(1, D)
    arrays = {k: np.ascontiguousarray(x) for k, x in arrays.items()}

    nc = bacc.Bacc("TRN2", target_bir_lowering=False, num_devices=1)
    aps = {k: nc.dram_tensor(f"in_{k}", x.shape, mybir.dt.from_np(x.dtype), kind="ExternalInput").ap()
           for k, x in arrays.items()}
    out = nc.dram_tensor("out_0", (B, Q, D), F32, kind="ExternalOutput").ap()
    build_program(nc, aps, out)
    r = run_bass_kernel_spmd(nc, [{f"in_{k}": x for k, x in arrays.items()}], core_ids=[0])
    return r.results[0]["out_0"]
```
